# Optimizing a Trainium2 kernel written in Bass

```python
import numpy as np
import jax
import jax.numpy as jnp

def _softmax(x, axis=-1):
    return jax.nn.softmax(x, axis=axis)

def _gelu(x):
    return jax.nn.gelu(x, approximate=True)

def _silu(x):
    return jax.nn.silu(x)

def _sigmoid(x):
    return jax.nn.sigmoid(x)

def _layernorm(x, axis=-1, eps=1e-05):
    m = jnp.mean(x, axis=axis, keepdims=True)
    v = jnp.var(x, axis=axis, keepdims=True)
    return (x - m) / jnp.sqrt(v + eps)

def _scatter_add(tgt, idx, src, axis=0):
    return tgt.at[idx].add(src)

def _segment_sum(src, seg, n):
    return jax.ops.segment_sum(src, seg, n)
kernel_name = 'mk_gnn_preln_d2_gnn_r64_fb542f'

def setup_inputs(seed: int=0):
    np.random.seed(seed)
    _w = jnp.asarray

    def _rec_inputs():
        import jax
        import jax.numpy as jnp
        _gk = jax.random.key(seed)
        x = -0.0003713 + 1 * jax.random.normal(jax.random.fold_in(_gk, 1), (100000, 128), jnp.float32)
        src = jax.random.randint(jax.random.fold_in(_gk, 2), (50000,), 0, 100000, jnp.int32)
        dst = jnp.minimum((100000 * jax.random.uniform(jax.random.fold_in(_gk, 3), (50000,)) ** 2.0).astype(jnp.int32), 99999)
        _o = jnp.argsort(dst, stable=True)
        src = src[_o]
        dst = dst[_o]
        edge_type_8 = jax.random.randint(jax.random.fold_in(_gk, 13), (50000,), 0, 8, jnp.int32)
        edge_weight = jax.random.uniform(jax.random.fold_in(_gk, 14), (50000,), jnp.float32, 0.0, 1)
        return (x, src, dst, edge_type_8, edge_weight)
    x, src, dst, edge_type_8, edge_weight = _rec_inputs()

    def _L0_gnn_setup():
        import jax, jax.numpy as jnp
        import numpy as np
        N = 100000
        E = 25000
        IN_DIM = 128
        OUT_DIM = 128
        H = 8
        D = OUT_DIM // H
        L = 2
        NEG_SLOPE = 0.1

        def gat_layer(x, src, dst, w, W, al, ar):
            ft = (x @ W).reshape(N, H, D)
            el = jnp.einsum('nhd,hd->nh', ft, al)
            er = jnp.einsum('nhd,hd->nh', ft, ar)
            e = jax.nn.leaky_relu(el[src] + er[dst], negative_slope=NEG_SLOPE)
            e = w[:, None] * e
            m = jax.ops.segment_max(e, dst, num_segments=N)
            m = jnp.where(jnp.isfinite(m), m, 0.0)
            ex = jnp.exp(e - m[dst])
            s = jax.ops.segment_sum(ex, dst, num_segments=N)
            a = ex / s[dst]
            msg = ft[src] * a[:, :, None]
            out = jax.ops.segment_sum(msg, dst, num_segments=N)
            out = jax.nn.relu(out)
            return out.reshape(N, H * D)
        key = jax.random.key(seed)
        ks = jax.random.split(key, 12)
        features = jax.random.normal(ks[0], (N, IN_DIM), dtype=jnp.float32)
        src = jax.random.randint(ks[1], (E,), 0, N, dtype=jnp.int32)
        dst = jax.random.randint(ks[2], (E,), 0, N, dtype=jnp.int32)
        w = jax.random.uniform(ks[3], (E,), dtype=jnp.float32)
        s = 1.0 / np.sqrt(IN_DIM)
        W1 = jax.random.uniform(ks[4], (IN_DIM, H * D), minval=-s, maxval=s, dtype=jnp.float32)
        al1 = jax.random.normal(ks[5], (H, D), dtype=jnp.float32) * 0.1
        ar1 = jax.random.normal(ks[6], (H, D), dtype=jnp.float32) * 0.1
        W2 = jax.random.uniform(ks[7], (OUT_DIM, H * D), minval=-s, maxval=s, dtype=jnp.float32)
        al2 = jax.random.normal(ks[8], (H, D), dtype=jnp.float32) * 0.1
        ar2 = jax.random.normal(ks[9], (H, D), dtype=jnp.float32) * 0.1
        so = 1.0 / np.sqrt(L * OUT_DIM)
        Wm = jax.random.uniform(ks[10], (L * OUT_DIM, OUT_DIM), minval=-so, maxval=so, dtype=jnp.float32)
        bm = jax.random.uniform(ks[11], (OUT_DIM,), minval=-so, maxval=so, dtype=jnp.float32)
        return {'features': features, 'src': src, 'dst': dst, 'w': w, 'W1': W1, 'al1': al1, 'ar1': ar1, 'W2': W2, 'al2': al2, 'ar2': ar2, 'Wm': Wm, 'bm': bm}
    _L0_gnn_all = _L0_gnn_setup()
    _L0_gnn_in = {k: v for k, v in _L0_gnn_all.items() if k in ('W1', 'al1', 'ar1', 'W2', 'al2', 'ar2', 'Wm', 'bm')}
    del _L0_gnn_all

    def _L1_gnn_setup():
        import jax, jax.numpy as jnp
        import numpy as np
        N_NODES = 50000
        N_EDGES = 12500
        IN_CH = 128
        OUT_CH = 128
        N_REL = 8
        N_BASES = 8
        key = jax.random.key(seed)
        ks = jax.random.split(key, 8)
        x = jax.random.normal(ks[0], (N_NODES, IN_CH), dtype=jnp.float32)
        edge_index = jax.random.randint(ks[1], (2, N_EDGES), 0, N_NODES, dtype=jnp.int64)
        edge_type = jax.random.randint(ks[2], (N_EDGES,), 0, N_REL, dtype=jnp.int64)
        scale = 1.0 / np.sqrt(IN_CH)
        basis = jax.random.normal(ks[3], (N_BASES, IN_CH, OUT_CH), dtype=jnp.float32) * scale
        comp = jax.random.normal(ks[4], (N_REL, N_BASES), dtype=jnp.float32) * (1.0 / np.sqrt(N_BASES))
        root = jax.random.normal(ks[5], (IN_CH, OUT_CH), dtype=jnp.float32) * scale
        bias = jnp.zeros((OUT_CH,), dtype=jnp.float32)
        alpha = jnp.full((OUT_CH,), 0.25, dtype=jnp.float32)
        return {'x': x, 'edge_index': edge_index, 'edge_type': edge_type, 'basis': basis, 'comp': comp, 'root': root, 'bias': bias, 'alpha': alpha}
    _L1_gnn_all = _L1_gnn_setup()
    _L1_gnn_in = {k: v for k, v in _L1_gnn_all.items() if k in ('basis', 'comp', 'root', 'bias', 'alpha')}
    del _L1_gnn_all
    return {'x': x, 'src': src, 'dst': dst, 'edge_type_8': edge_type_8, 'edge_weight': edge_weight, 'L0_gnn_W1': _L0_gnn_in['W1'], 'L0_gnn_al1': _L0_gnn_in['al1'], 'L0_gnn_ar1': _L0_gnn_in['ar1'], 'L0_gnn_W2': _L0_gnn_in['W2'], 'L0_gnn_al2': _L0_gnn_in['al2'], 'L0_gnn_ar2': _L0_gnn_in['ar2'], 'L0_gnn_Wm': _L0_gnn_in['Wm'], 'L0_gnn_bm': _L0_gnn_in['bm'], 'L1_gnn_basis': _L1_gnn_in['basis'], 'L1_gnn_comp': _L1_gnn_in['comp'], 'L1_gnn_root': _L1_gnn_in['root'], 'L1_gnn_bias': _L1_gnn_in['bias'], 'L1_gnn_alpha': _L1_gnn_in['alpha']}

def reference(x, src, dst, edge_type_8, edge_weight, L0_gnn_W1, L0_gnn_al1, L0_gnn_ar1, L0_gnn_W2, L0_gnn_al2, L0_gnn_ar2, L0_gnn_Wm, L0_gnn_bm, L1_gnn_basis, L1_gnn_comp, L1_gnn_root, L1_gnn_bias, L1_gnn_alpha):
    import jax
    import jax.numpy as jnp

    def _L0_gnn_ref(features, src, dst, w, W1, al1, ar1, W2, al2, ar2, Wm, bm):
        import jax, jax.numpy as jnp
        import numpy as np
        N = 100000
        E = 25000
        IN_DIM = 128
        OUT_DIM = 128
        H = 8
        D = OUT_DIM // H
        L = 2
        NEG_SLOPE = 0.1

        def gat_layer(x, src, dst, w, W, al, ar):
            ft = (x @ W).reshape(N, H, D)
            el = jnp.einsum('nhd,hd->nh', ft, al)
            er = jnp.einsum('nhd,hd->nh', ft, ar)
            e = jax.nn.leaky_relu(el[src] + er[dst], negative_slope=NEG_SLOPE)
            e = w[:, None] * e
            m = jax.ops.segment_max(e, dst, num_segments=N)
            m = jnp.where(jnp.isfinite(m), m, 0.0)
            ex = jnp.exp(e - m[dst])
            s = jax.ops.segment_sum(ex, dst, num_segments=N)
            a = ex / s[dst]
            msg = ft[src] * a[:, :, None]
            out = jax.ops.segment_sum(msg, dst, num_segments=N)
            out = jax.nn.relu(out)
            return out.reshape(N, H * D)
        x1 = gat_layer(features, src, dst, w, W1, al1, ar1)
        x2 = gat_layer(x1, src, dst, w, W2, al2, ar2)
        h = jnp.concatenate([x1, x2], axis=-1)
        return h @ Wm + bm

    def _L1_gnn_ref(x, edge_index, edge_type, basis, comp, root, bias, alpha):
        import jax, jax.numpy as jnp
        import numpy as np
        N_NODES = 50000
        N_EDGES = 12500
        IN_CH = 128
        OUT_CH = 128
        N_REL = 8
        N_BASES = 8
        N = x.shape[0]
        R = comp.shape[0]
        W = jnp.einsum('rb,bio->rio', comp, basis)
        xw = jnp.einsum('ni,rio->rno', x, W)
        src = edge_index[0]
        dst = edge_index[1]
        msg = xw[edge_type, src]
        seg = edge_type * N + dst
        cnt = jax.ops.segment_sum(jnp.ones(msg.shape[0], dtype=x.dtype), seg, num_segments=R * N)
        norm = 1.0 / jnp.maximum(cnt, 1.0)
        agg = jax.ops.segment_sum(msg * norm[seg][:, None], dst, num_segments=N)
        out = agg + x @ root + bias
        return jnp.where(out >= 0, out, alpha * out)
    edge_index = jnp.stack([src, dst])
    h = jnp.maximum(_layernorm(x, axis=-1), 0.0)
    x = x + _L0_gnn_ref(h, src, dst, edge_weight, L0_gnn_W1, L0_gnn_al1, L0_gnn_ar1, L0_gnn_W2, L0_gnn_al2, L0_gnn_ar2, L0_gnn_Wm, L0_gnn_bm)
    h = jnp.maximum(_layernorm(x, axis=-1), 0.0)
    x = x + _L1_gnn_ref(h, edge_index, edge_type_8, L1_gnn_basis, L1_gnn_comp, L1_gnn_root, L1_gnn_bias, L1_gnn_alpha)
    return x

_drawn_inputs = setup_inputs


def setup_inputs(seed=0):
    import zlib

    import numpy as np

    out = dict(_drawn_inputs(seed))
    spreads = {'L1_gnn_bias': (0.0, 0.1), 'L1_gnn_alpha': (0.25, 0.6)}
    factors = {'edge_weight': 22.002,
     'L0_gnn_al1': 21.81,
     'L0_gnn_ar1': 34.174,
     'L0_gnn_W2': 4.006,
     'L0_gnn_al2': 27.258,
     'L0_gnn_ar2': 37.978}
    for name, (base, spread) in spreads.items():
        noise = np.random.default_rng([zlib.crc32(name.encode()), seed]).standard_normal(out[name].shape)
        drawn = base * np.exp(spread * noise) if base else spread * noise
        out[name] = jnp.asarray(drawn.astype(out[name].dtype))
    for name, factor in factors.items():
        out[name] = (out[name] * factor).astype(out[name].dtype)
    return out
```

```python
import numpy as np

N = 100000
E = 50000
F = 128
H = 8
D = F // H
R = 8
BE = 512
J = BE // 128
NB = 2 * -(-E // (2 * BE))
EP = NB * BE
TILES = EP // 128
C = 8
CL = EP // C
CT = CL // 128
NP = 125
NQ = N // (NP * J)
ZERO_ROW = EP
FAR = 1 << 20
CUT = -1e30
EPS = 1e-5
SLOPE = 0.1
DMA_SEMS = {"x_loaded", "stored", "gathered", "placed", "spilled", "f_stored", "ids_loaded", "rows_loaded",
            "x1f_loaded", "found", "found_stored", "at_loaded", "ends_loaded", "scattered"}
TABLE = "natural_log_exp_and_others"


def steps(eng, count, step):
    step(0, 0, True, False)
    with eng.Fori(0, (count - 2) // 2) as i:
        step(i * 2 + 1, 1, True, True)
        step(i * 2 + 2, 0, True, True)
    step(count - 1, 1, True, True)
    step(count, 0, False, True)


def blocks(eng, count, body):
    with eng.Fori(0, count // 2) as i:
        body(i * 2, 0)
        body(i * 2 + 1, 1)


def nth(k, b, slot):
    return (b - slot) * (k // 2) + k


class Link:

    def __init__(self, eng, sem, per_block):
        self.eng, self.sem, self.per_block = eng, sem, per_block

    def begin(self, b):
        self.base, self.n = b * self.per_block, 0

    def __call__(self, ins):
        self.n += 1
        ins.then_inc(self.sem, 1)
        self.eng.wait_ge(self.sem, self.base + self.n)

    def end(self):
        assert self.n == self.per_block, self.n


class Memory:

    def __init__(self, nc, ctx, name):
        from concourse import mybir

        self.nc, self.ctx, self.name, self.fp32 = nc, ctx, name, mybir.dt.float32

    def sb(self, name, shape, dt=None):
        return self.ctx.enter_context(self.nc.sbuf_tensor(f"{self.name}_{name}", shape, dt or self.fp32))

    def ps(self, name, shape):
        return self.ctx.enter_context(self.nc.psum_tensor(f"{self.name}_{name}", shape, self.fp32))

    def slots(self, name):
        return [self.sem(f"{name}{u}") for u in range(2)]

    def sem(self, name):
        return self.ctx.enter_context(self.nc.semaphore(f"{self.name}_{name}"))


def weights_phase(nc, keep, inp):
    from contextlib import ExitStack
    from concourse.alu_op_type import AluOpType as ALU

    with ExitStack() as ctx:
        m = Memory(nc, ctx, "wt")
        wT = m.sb("wT", [128, 2, 128])
        att = m.sb("att", [128, 4])
        attx = m.sb("attx", [128, 4, 128])
        blockmask = m.sb("blockmask", [128, 128])
        headsel = m.sb("headsel", [128, H])
        att8 = m.sb("att8", [128, H])
        basis = m.sb("basis", [128, R, 128])
        comp = m.sb("comp", [128, R * R])
        p_wT = m.ps("p_wT", [128, 2, 128])
        p_x = m.ps("p_x", [128, 3, 128])
        p_8 = m.ps("p_8", [128, H])
        loaded, expanded, turned, turned_sb, folded, step, done = (m.sem(n) for n in (
            "loaded", "expanded", "turned", "turned_sb", "folded", "step", "done"))
        block = ctx.enter_context(nc.Block())
        LOADS = 18 + 2 * J

        @block.sync
        def _(eng):
            def load(dst, src):
                eng.dma_start(dst, src).then_inc(loaded, 16)

            load(keep["ident"][:, :], inp["ident"])
            load(blockmask[:, :], inp["blockmask"])
            load(headsel[:, :], inp["headsel"])
            load(keep["expand"][:, :], inp["expand"])
            load(keep["pick"][:, :], inp["pick"])
            load(keep["w1"][:, :], inp["W1"])
            load(keep["w2"][:, :], inp["W2"])
            with nc.allow_non_contiguous_dma(reason="four columns of 128 numbers"):
                for n, name in enumerate(("al1", "ar1", "al2", "ar2")):
                    load(att[:, n:n + 1], inp[name].rearrange("h (d a) -> (h d) a", a=1))
            load(keep["wm"][:, :, :], inp["Wm"].rearrange("(l k) n -> k l n", l=2))
            load(keep["bmrow"][:, :], inp["bm"].rearrange("(a n) -> a n", a=1))
            load(keep["root"][:, :], inp["root"])
            load(keep["biasrow"][:, :], inp["bias"].rearrange("(a n) -> a n", a=1))
            load(basis[:, :, :], inp["basis"].rearrange("b k n -> k b n"))
            load(comp[:, :], inp["comp"].rearrange("r b -> (r b)").partition_broadcast(128))
            load(keep["ones"][:, :], inp["ones"])
            for j in range(J):
                load(keep["bm4"][:, j, :], inp["bm"].partition_broadcast(128))
                load(keep["alpha4"][:, j, :], inp["alpha"].partition_broadcast(128))

        @block.tensor
        def _(eng):
            eng.wait_ge(loaded, 16 * LOADS)
            eng.transpose(p_wT[:, 0, :], keep["w1"][:, :], keep["ident"][:, :])
            eng.transpose(p_wT[:, 1, :], keep["w2"][:, :], keep["ident"][:, :]).then_inc(turned, 1)
            eng.wait_ge(turned_sb, 1)
            eng.wait_ge(expanded, 1)
            for n, layer in ((0, 0), (1, 0), (2, 1)):
                eng.matmul(p_x[:, n, :], wT[:, layer, :], attx[:, n, :], start=True, stop=True)
            eng.matmul(p_8[:, :], wT[:, 1, :], att8[:, :], start=True, stop=True).then_inc(folded, 1)

        @block.vector
        def _(eng):
            link = Link(eng, step, R * R)
            link.begin(0)
            eng.wait_ge(loaded, 16 * LOADS)
            for n in range(3):
                eng.tensor_scalar(attx[:, n, :], blockmask[:, :], att[:, n:n + 1], None, ALU.mult)
            eng.tensor_scalar(att8[:, :], headsel[:, :], att[:, 3:4], None, ALU.mult).then_inc(expanded, 1)
            eng.wait_ge(turned, 1)
            eng.tensor_copy(wT[:, :, :], p_wT[:, :, :]).then_inc(turned_sb, 1)
            for b in range(R):
                for r in range(R):
                    w, c = keep["wrel"][:, r, :], comp[:, r * R + b:r * R + b + 1]
                    if b == 0:
                        link(eng.tensor_scalar(w, basis[:, b, :], c, None, ALU.mult))
                    else:
                        link(eng.scalar_tensor_tensor(w, basis[:, b, :], c, w, ALU.mult, ALU.add))
            link.end()
            eng.wait_ge(folded, 1)
            eng.tensor_copy(keep["wel1"][:, :], p_x[:, 0, :])
            eng.tensor_copy(keep["wer1"][:, :], p_x[:, 1, :])
            eng.tensor_copy(keep["wel2"][:, :], p_x[:, 2, :])
            eng.tensor_copy(keep["wer2"][:, :], p_8[:, :]).then_inc(done, 1)


def edge_rows_phase(nc, keep, inp, tab):
    from contextlib import ExitStack
    from concourse import mybir
    from concourse.alu_op_type import AluOpType as ALU

    i32 = mybir.dt.int32
    FILL = N // NP
    with ExitStack() as ctx:
        m = Memory(nc, ctx, "er")
        cur, prev = m.sb("cur", [NB, BE], i32), m.sb("prev", [NB, BE], i32)
        same, cut = m.sb("same", [NB, BE]), m.sb("cut", [NB, BE])
        here, nxt = m.sb("here", [128, TILES], i32), m.sb("nxt", [128, TILES], i32)
        goes_on, end = m.sb("goes_on", [128, TILES]), m.sb("end", [128, TILES], i32)
        zero, no_edge = m.sb("zero", [1, F]), m.sb("no_edge", [128, FILL], i32)
        loaded, step, ready, stored = (m.sem(n) for n in ("loaded", "step", "ready", "stored"))
        block = ctx.enter_context(nc.Block())

        @block.sync
        def _(eng):
            row = lambda k: inp["dseg"][k:k + EP].rearrange("(b e) -> b e", e=BE)
            eng.dma_start(cur[:, :], row(1)).then_inc(loaded, 16)
            eng.dma_start(prev[:, :], row(0)).then_inc(loaded, 16)
            eng.dma_start(here[:, :], inp["here"]).then_inc(loaded, 16)
            eng.dma_start(nxt[:, :], inp["next"]).then_inc(loaded, 16)
            eng.wait_ge(ready, 3)
            rows = lambda t: t.rearrange("(b e) -> b e", e=BE)
            eng.dma_start(rows(tab["cut"]), cut[:, :]).then_inc(stored, 16)
            eng.dma_start(rows(tab["same"]), same[:, :]).then_inc(stored, 16)
            eng.dma_start(tab["end"][0:NB].rearrange("b p j -> p b j"),
                          end[:, :].rearrange("p (b j) -> p b j", j=J)).then_inc(stored, 16)
            eng.dma_start(tab["x1"][ZERO_ROW:ZERO_ROW + 1, :], zero[:, :]).then_inc(stored, 16)
            eng.dma_start(tab["delta"][ZERO_ROW:ZERO_ROW + 1, :], keep["bmrow"][:, :]).then_inc(stored, 16)
            eng.dma_start(tab["pos"].rearrange("(p n) a -> p (n a)", p=NP), no_edge[0:NP, :]).then_inc(stored, 16)
            eng.dma_start(tab["end"][NB, :, :], no_edge[:, 0:J]).then_inc(stored, 16)
            eng.dma_start(tab["at"][NB, :, :], no_edge[:, 0:J]).then_inc(stored, 16)
            eng.wait_ge(stored, 8 * 16)

        @block.vector
        def _(eng):
            link = Link(eng, step, 2)
            link.begin(0)
            eng.memset(zero[:, :], 0.0)
            eng.memset(no_edge[:, :], ZERO_ROW).then_inc(ready, 1)
            eng.wait_ge(loaded, 64)
            link(eng.tensor_tensor(same[:, :], cur[:, :], prev[:, :], ALU.is_equal))
            eng.tensor_scalar(cut[:, :], same[:, :], -CUT, CUT, ALU.mult, ALU.add).then_inc(ready, 1)
            link(eng.tensor_tensor(goes_on[:, :], here[:, :], nxt[:, :], ALU.is_equal))
            eng.scalar_tensor_tensor(end[:, :], goes_on[:, :], float(FAR), here[:, :],
                                     ALU.mult, ALU.add).then_inc(ready, 1)
            link.end()


def chunk_scan_phase(nc, keep, name, on, add, out, backward):
    from contextlib import ExitStack
    from concourse import mybir
    from concourse.alu_op_type import AluOpType as ALU

    P = H * C
    way = slice(None, None, -1) if backward else slice(None)
    last = 0 if backward else CL - 1
    with ExitStack() as ctx:
        m = Memory(nc, ctx, name)
        whole, col = m.sb("whole", [P, 1]), m.sb("col", [P, 1])
        whole_row, sum_row, carry_row = m.sb("whole_row", [1, P]), m.sb("sum_row", [1, P]), m.sb("carry_row", [1, P])
        p_rows, p_col = m.ps("p_rows", [1, 2, P]), m.ps("p_col", [P, 1])
        summed, rowed, carried, columned, step = (m.sem(n) for n in ("summed", "rowed", "carried", "columned", "step"))
        block = ctx.enter_context(nc.Block())

        @block.vector
        def _(eng):
            link = Link(eng, step, 5)
            link.begin(0)
            eng.tensor_tensor_scan(out[:, way], on[:, way], add[:, way], 0.0, ALU.mult, ALU.add)
            eng.tensor_reduce(whole[:, :], on, mybir.AxisListType.X, ALU.min).then_inc(summed, 1)
            eng.wait_ge(rowed, 1)
            link(eng.tensor_copy(whole_row[:, :], p_rows[:, 1, :]))
            link(eng.tensor_tensor_scan(sum_row[:, way], whole_row[:, way], p_rows[:, 0, way], 0.0,
                                        ALU.mult, ALU.add))
            link(eng.memset(carry_row[:, :], 0.0))
            rows = lambda t: t[:, :].rearrange("a (h c) -> a h c", c=C)
            if backward:
                to, frm = rows(carry_row)[:, :, 0:C - 1], rows(sum_row)[:, :, 1:C]
            else:
                to, frm = rows(carry_row)[:, :, 1:C], rows(sum_row)[:, :, 0:C - 1]
            eng.tensor_copy(to, frm).then_inc(carried, 1)
            eng.wait_ge(columned, 1)
            link(eng.tensor_copy(col[:, :], p_col[:, :]))
            link(eng.tensor_tensor_scan(out[:, way], on[:, way], add[:, way], col[:, 0:1], ALU.mult, ALU.add))
            link.end()

        @block.tensor
        def _(eng):
            eng.wait_ge(summed, 1)
            eng.matmul(p_rows[:, 0, :], out[:, last:last + 1], keep["ident"][0:P, 0:P], start=True, stop=True)
            eng.matmul(p_rows[:, 1, :], whole[:, :], keep["ident"][0:P, 0:P], start=True, stop=True).then_inc(rowed, 1)
            eng.wait_ge(carried, 1)
            eng.matmul(p_col[:, :], carry_row[:, :], keep["ones"][0:1, 0:1], start=True, stop=True).then_inc(columned, 1)


def chunked(t):
    return t.rearrange("(c e) -> c e", e=CL)


def counts_phases(nc, keep, inp, tab):
    from contextlib import ExitStack
    from concourse import mybir
    from concourse.alu_op_type import AluOpType as ALU

    i32, bf16 = mybir.dt.int32, mybir.dt.bfloat16
    P = R * C
    with ExitStack() as ctx:
        m = Memory(nc, ctx, "ct")
        kind, cur = m.sb("kind", [P, CL], i32), m.sb("cur", [P, CL], i32)
        before, after = m.sb("before", [P, CL]), m.sb("after", [P, CL])
        hot, hot16 = m.sb("hot", [P, CL]), m.sb("hot16", [P, CL], bf16)
        relcol, chunksel = m.sb("relcol", [P, 1]), m.sb("chunksel", [P, C])
        fwd, bwd = kind[:, :].bitcast(m.fp32), cur[:, :].bitcast(m.fp32)
        loaded, ready, made, stored = (m.sem(n) for n in ("loaded", "ready", "made", "stored"))
        with nc.Block() as block:
            @block.sync
            def _(eng):
                eng.dma_start(relcol[:, :], inp["relcol"]).then_inc(loaded, 16)
                eng.dma_start(chunksel[:, :], inp["chunksel"]).then_inc(loaded, 16)
                for r in range(R):
                    at = slice(r * C, r * C + C)
                    eng.dma_start(kind[at, :], chunked(inp["kind"])).then_inc(loaded, 16)
                    eng.dma_start(cur[at, :], chunked(inp["dseg"][1:EP + 1])).then_inc(loaded, 16)
                    eng.dma_start(before[at, :].bitcast(i32), chunked(inp["dseg"][0:EP])).then_inc(loaded, 16)
                    eng.dma_start(after[at, :].bitcast(i32), chunked(inp["dseg"][2:EP + 2])).then_inc(loaded, 16)
                eng.wait_ge(ready, 1)
                eng.dma_start(tab["hot"].rearrange("r (c e) -> (r c) e", e=CL), hot16[:, :]).then_inc(stored, 16)
                eng.wait_ge(stored, 16)

            @block.vector
            def _(eng):
                eng.wait_ge(loaded, 16 * (2 + 4 * R))
                eng.tensor_scalar(hot[:, :], kind[:, :], relcol[:, 0:1], None, ALU.is_equal).then_inc(made, 1)
                eng.wait_ge(made, 1)
                eng.tensor_copy(hot16[:, :], hot[:, :]).then_inc(ready, 1)
                eng.tensor_tensor(before[:, :], cur[:, :], before[:, :].bitcast(i32), ALU.is_equal)
                eng.tensor_tensor(after[:, :], cur[:, :], after[:, :].bitcast(i32), ALU.is_equal).then_inc(made, 1)
                eng.wait_ge(made, 2)
        chunk_scan_phase(nc, keep, "cf", before[:, :], hot[:, :], fwd, False)
        chunk_scan_phase(nc, keep, "cb", after[:, :], hot[:, :], bwd, True)
        p_cnt = m.ps("p_cnt", [128, CT, C])
        cnt = m.sb("cnt", [128, CT, C])
        link_sem, own, counted, done = (m.sem(n) for n in ("step", "own", "counted", "done"))
        with nc.Block() as block:
            @block.vector
            def _(eng):
                link = Link(eng, link_sem, 3)
                link.begin(0)
                link(eng.tensor_tensor(fwd, fwd, bwd, ALU.add))
                link(eng.tensor_tensor(fwd, fwd, hot[:, :], ALU.subtract))
                eng.tensor_tensor(fwd, fwd, hot[:, :], ALU.mult).then_inc(own, 1)
                eng.wait_ge(counted, 1)
                link(eng.tensor_scalar(cnt[:, :, :], p_cnt[:, :, :], 1.0, None, ALU.max))
                eng.reciprocal(keep["norm"][:, :].rearrange("p (c t) -> p t c", t=CT), cnt[:, :, :]).then_inc(done, 1)
                link.end()

            @block.tensor
            def _(eng):
                eng.wait_ge(own, 1)
                for t in range(CT):
                    last = eng.matmul(p_cnt[:, t, :], fwd[:, t * 128:(t + 1) * 128], chunksel[:, :],
                                      start=True, stop=True)
                last.then_inc(counted, 1)


def spread_phases(nc, keep, inp, tab):
    from contextlib import ExitStack
    from concourse import mybir
    from concourse.alu_op_type import AluOpType as ALU

    i32 = mybir.dt.int32
    P = H * C
    with ExitStack() as ctx:
        m = Memory(nc, ctx, "sp")
        cur, after = m.sb("cur", [P, CL], i32), m.sb("after", [P, CL])
        term, spread = m.sb("term", [P, CL]), m.sb("spread", [P, CL])
        loaded, step, stored = (m.sem(n) for n in ("loaded", "step", "stored"))
        rows = tab["er2"].rearrange("h (c e) -> (h c) e", e=CL)
        with nc.Block() as block:
            @block.sync
            def _(eng):
                eng.dma_start(term[:, :], rows).then_inc(loaded, 16)
                for h in range(H):
                    at = slice(h * C, h * C + C)
                    eng.dma_start(cur[at, :], chunked(inp["dseg"][1:EP + 1])).then_inc(loaded, 16)
                    eng.dma_start(after[at, :].bitcast(i32), chunked(inp["dseg"][2:EP + 2])).then_inc(loaded, 16)

            @block.vector
            def _(eng):
                link = Link(eng, step, 3)
                link.begin(0)
                eng.wait_ge(loaded, 16 * (1 + 2 * H))
                link(eng.tensor_tensor(after[:, :], cur[:, :], after[:, :].bitcast(i32), ALU.is_equal))
                link(eng.tensor_tensor(spread[:, :], term[:, :], after[:, :], ALU.mult))
                link(eng.tensor_tensor(term[:, :], term[:, :], spread[:, :], ALU.subtract))
                link.end()
        chunk_scan_phase(nc, keep, "sb", after[:, :], term[:, :], spread[:, :], True)
        with nc.Block() as block:
            @block.sync
            def _(eng):
                eng.dma_start(rows, spread[:, :]).then_inc(stored, 16)
                eng.wait_ge(stored, 16)


class Norm:

    def __init__(self, m, parts, groups):
        def two(name):
            return [m.sb(f"{name}{u}", [parts, groups]) for u in range(2)]

        self.raw = [m.sb(f"raw{u}", [parts, groups, 6]) for u in range(2)]
        self.total, self.apart, self.spread, self.var = two("total"), two("apart"), two("spread"), two("var")
        self.log, self.guess, self.square, self.part = two("log"), two("guess"), two("square"), two("part")
        self.scale, self.shift = two("scale"), two("shift")


def moments(eng, link, n, u):
    from concourse.alu_op_type import AluOpType as ALU

    raw = n.raw[u]
    eng.tensor_tensor(n.total[u][:, :], raw[:, :, 1], raw[:, :, 4], ALU.add)
    eng.tensor_tensor(n.spread[u][:, :], raw[:, :, 2], raw[:, :, 5], ALU.add)
    link(eng.tensor_tensor(n.apart[u][:, :], raw[:, :, 1], raw[:, :, 4], ALU.subtract))
    link(eng.tensor_tensor(n.square[u][:, :], n.apart[u][:, :], n.apart[u][:, :], ALU.mult))
    link(eng.scalar_tensor_tensor(n.apart[u][:, :], n.square[u][:, :], F / 4.0, n.spread[u][:, :],
                                  ALU.mult, ALU.add))
    return eng.tensor_scalar(n.var[u][:, :], n.apart[u][:, :], 1.0 / F, EPS, ALU.mult, ALU.add)


def scales(eng, link, n, u, factor=None):
    from concourse.alu_op_type import AluOpType as ALU

    g, s, v, t = n.guess[u][:, :], n.square[u][:, :], n.var[u][:, :], n.part[u][:, :]
    link(eng.tensor_tensor(s, g, g, ALU.mult))
    link(eng.scalar_tensor_tensor(t, v, -0.5, s, ALU.mult, ALU.mult))
    link(eng.scalar_tensor_tensor(n.scale[u][:, :], t, 1.5, g, ALU.add, ALU.mult))
    if factor is not None:
        half = n.scale[u][:, 0:J]
        link(eng.tensor_tensor(half, half, factor, ALU.mult))
    return eng.scalar_tensor_tensor(n.shift[u][:, :], n.total[u][:, :], -0.5, n.scale[u][:, :], ALU.mult, ALU.mult)


def nodes_phase(nc, keep, inp, out):
    from contextlib import ExitStack
    from concourse import mybir
    from concourse.alu_op_type import AluOpType as ALU

    ACT = mybir.ActivationFunctionType
    x_b = inp["x"].rearrange("(p b j) f -> p b j f", p=NP, j=J)
    out_b = out.rearrange("(p b j) f -> p b j f", p=NP, j=J)
    with ExitStack() as ctx:
        m = Memory(nc, ctx, "nd")
        two = lambda n, s: [m.sb(f"{n}{u}", s) for u in range(2)]
        x, y, hn, res = (two(n, [NP, J, F]) for n in ("x", "y", "hn", "res"))
        low, high = two("low", [NP, J, F]), two("high", [NP, J, F])
        hT = two("hT", [128, J, NP])
        norm = Norm(m, NP, J)
        p_hT = [m.ps(f"p_hT{u}", [128, J, NP]) for u in range(2)]
        p_o = [m.ps(f"p_o{u}", [NP, J, F]) for u in range(2)]
        names = ("x_loaded", "x_free", "var_ready", "log_ready", "guess_ready", "scale_ready", "hn_ready",
                 "hT_ready", "hT_copied", "o_ready", "low_ready", "high_ready", "res_ready", "stored", "step_a", "step_b", "step_c")
        (x_loaded, x_free, var_ready, log_ready, guess_ready, scale_ready, hn_ready, hT_ready, hT_copied,
         o_ready, low_ready, high_ready, res_ready, stored, step_a, step_b, step_c) = (m.slots(n) if n in DMA_SEMS else m.sem(n) for n in names)
        block = ctx.enter_context(nc.Block())

        @block.sync
        def _(eng):
            for u in range(2):
                eng.sem_inc(stored[u], 16)

            def step(b, u, early, late):
                if early:
                    eng.wait_ge(x_free, b + 1)
                    eng.dma_start(x[u][:, :, :], x_b[:, b, :, :]).then_inc(x_loaded[u], 16)
                if late:
                    eng.wait_ge(res_ready, b)
                    eng.dma_start(out_b[:, b - 1, :, :], res[1 - u][:, :, :]).then_inc(stored[1 - u], 16)

            steps(eng, NQ, step)
            for u in range(2):
                eng.wait_ge(stored[u], 8 * NQ + 16)

        @block.vector
        def _(eng):
            eng.sem_inc(x_free, 2)
            la, lb, lc = Link(eng, step_a, 4), Link(eng, step_b, 3), Link(eng, step_c, 1)

            def step(b, u, early, late):
                if early:
                    la.begin(b)
                    eng.wait_ge(x_loaded[u], nth(16, b, u))
                    eng.tensor_tensor(y[u][:, :, :], x[u][:, :, :], keep["bm4"][0:NP, :, :], ALU.add).then_inc(x_free, 1)
                    eng.wait_ge(x_free, b + 3)
                    for j in range(J):
                        last = eng.bn_stats(norm.raw[u][:, j, :], y[u][:, j, :])
                    la(last)
                    moments(eng, la, norm, u).then_inc(var_ready, 1)
                    la.end()
                if late:
                    v = 1 - u
                    eng.wait_ge(o_ready, b)
                    lc.begin(b - 1)
                    lc(eng.scalar_tensor_tensor(low[v][:, :, :], p_o[v][:, :, :], 0.0, keep["alpha4"][0:NP, :, :],
                                                ALU.min, ALU.mult))
                    eng.wait_ge(stored[v], nth(16, b - 1, v))
                    eng.scalar_tensor_tensor(low[v][:, :, :], p_o[v][:, :, :], 0.0, low[v][:, :, :],
                                             ALU.max, ALU.add).then_inc(low_ready, 1)
                    eng.wait_ge(low_ready, b)
                    eng.tensor_tensor(res[v][:, :, :], low[v][:, :, :], y[v][:, :, :], ALU.add).then_inc(res_ready, 1)
                    lc.end()
                if early:
                    lb.begin(b)
                    eng.wait_ge(guess_ready, b + 1)
                    scales(eng, lb, norm, u).then_inc(scale_ready, 1)
                    lb.end()

            steps(eng, NQ, step)

        @block.scalar
        def _(eng):
            eng.preload_act_table_set(TABLE)

            def step(b, u, early, late):
                if early:
                    eng.wait_ge(var_ready, b + 1)
                    eng.activation(norm.log[u][:, :], norm.var[u][:, :], ACT.Ln).then_inc(log_ready, 1)
                    eng.wait_ge(log_ready, b + 1)
                    eng.activation(norm.guess[u][:, :], norm.log[u][:, :], ACT.Exp, scale=-0.5).then_inc(guess_ready, 1)
                    eng.wait_ge(scale_ready, b + 1)
                    for j in range(J):
                        last = eng.activation(hn[u][:, j, :], y[u][:, j, :], ACT.Relu,
                                              bias=norm.shift[u][:, j:j + 1], scale=norm.scale[u][:, j:j + 1])
                    last.then_inc(hn_ready, 1)
                    eng.wait_ge(hT_ready, b + 1)
                    eng.activation(hT[u][:, :, :], p_hT[u][:, :, :], ACT.Copy).then_inc(hT_copied, 1)

            steps(eng, NQ, step)

        @block.tensor
        def _(eng):
            def body(b, u):
                eng.wait_ge(hn_ready, b + 1)
                for j in range(J):
                    last = eng.transpose(p_hT[u][:, j, :], hn[u][:, j, :], keep["ident"][0:NP, 0:NP])
                last.then_inc(hT_ready, 1)
                eng.wait_ge(hT_copied, b + 1)
                for j in range(J):
                    eng.matmul(p_o[u][:, j, :], hT[u][:, j, :], keep["root"][:, :], start=True, stop=False)
                    last = eng.matmul(p_o[u][:, j, :], keep["ones"][0:1, 0:NP], keep["biasrow"][:, :],
                                      start=False, stop=True)
                last.then_inc(o_ready, 1)

            blocks(eng, NQ, body)


def first_attention(eng, link, z, slope, w, cut, t, u):
    from concourse.alu_op_type import AluOpType as ALU

    top, logit, below, fall = t["top"][u], t["logit"], t["below"], t["fall"]
    link(eng.tensor_tensor(logit[:, :], z[:, :], slope[:, :], ALU.max))
    link(eng.tensor_tensor(logit[:, :], w[:, :], logit[:, :], ALU.mult))
    link(eng.tensor_copy(top[:, 0:1], t["top"][1 - u][:, BE:BE + 1]))
    link(eng.tensor_tensor_scan(top[:, 1:BE + 1], cut[:, :], logit[:, :], top[:, 0:1], ALU.add, ALU.max))
    eng.tensor_tensor(below[:, :], logit[:, :], top[:, 1:BE + 1], ALU.subtract)
    link(eng.tensor_tensor(fall[:, :], cut[:, :], top[:, 0:BE], ALU.add))
    return eng.tensor_tensor(fall[:, :], fall[:, :], top[:, 1:BE + 1], ALU.subtract)


FIRST_LINKS, LAST_LINKS = 5, 3


def last_attention(eng, link, t, u, result):
    from concourse.alu_op_type import AluOpType as ALU

    num, den = t["num"], t["den"]
    link(eng.tensor_tensor_scan(num[u][:, :], t["fade"][:, :], t["message"][:, :], num[1 - u][:, BE - 1:BE],
                                ALU.mult, ALU.add))
    link(eng.tensor_tensor_scan(den[u][:, :], t["fade"][:, :], t["weight"][:, :], den[1 - u][:, BE - 1:BE],
                                ALU.mult, ALU.add))
    link(eng.reciprocal(t["inverse"][:, :], den[u][:, :]))
    return eng.scalar_tensor_tensor(result, num[u][:, :], 0.0, t["inverse"][:, :], ALU.max, ALU.mult)


def attention_tiles(m):
    one = lambda n: m.sb(n, [128, BE])
    return {"top": [m.sb(f"top{u}", [128, BE + 1]) for u in range(2)],
            "num": [one("num0"), one("num1")], "den": [one("den0"), one("den1")],
            "logit": one("logit"), "below": one("below"), "fall": one("fall"), "weight": one("weight"),
            "fade": one("fade"), "message": one("message"), "inverse": one("inverse")}


def start_attention(eng, t, sem):
    eng.memset(t["top"][1][:, BE:BE + 1], CUT)
    eng.memset(t["num"][1][:, BE - 1:BE], 0.0)
    eng.memset(t["den"][1][:, BE - 1:BE], 0.0).then_inc(sem, 1)
    eng.wait_ge(sem, 1)


def edge_rows_of(table, b):
    import concourse.bass as bass

    return table[bass.ds(b * BE, BE), :].rearrange("(j p) f -> p j f", p=128)


def gat1_phase(nc, keep, inp, tab):
    from contextlib import ExitStack
    import concourse.bass as bass
    from concourse import mybir
    from concourse.alu_op_type import AluOpType as ALU

    ACT, i32 = mybir.ActivationFunctionType, mybir.dt.int32
    with ExitStack() as ctx:
        m = Memory(nc, ctx, "g1")
        two = lambda n, s, dt=None: [m.sb(f"{n}{u}", s, dt) for u in range(2)]
        ids, ends = two("ids", [128, 3 * J], i32), two("ends", [128, J], i32)
        x = two("x", [128, 2 * J, F])
        rows = two("rows", [1, 2, BE])
        h, hT = m.sb("h", [128, 2 * J, F]), m.sb("hT", [128, 2, BE])
        slope = m.sb("slope", [128, BE])
        x1f, x1e, er2 = two("x1f", [128, BE]), two("x1e", [128, J, F]), two("er2", [H, BE])
        t, norm = attention_tiles(m), Norm(m, 128, 2 * J)
        p_hT = [m.ps("p_hs", [128, BE]), m.ps("p_hd", [128, BE])]
        p_ft, p_z, p_w, p_cut = (m.ps(n, [128, BE]) for n in ("p_ft", "p_z", "p_w", "p_cut"))
        p_x1, p_er2 = m.ps("p_x1", [128, BE]), m.ps("p_er2", [H, BE])
        names = ("ids_loaded", "rows_loaded", "gathered", "placed", "spilled", "stored", "f_stored", "var_ready", "log_ready",
                 "guess_ready", "scale_ready", "h_ready", "hT_ready", "hT_copied", "z_ready", "ft_ready",
                 "slope_ready", "gaps_ready", "exp_ready", "message_ready", "x1_ready", "x1_turned",
                 "x1_copied", "start", "pool_go", "step_n", "step_s", "step_f", "step_l")
        (ids_loaded, rows_loaded, gathered, placed, spilled, stored, f_stored, var_ready, log_ready, guess_ready,
         scale_ready, h_ready, hT_ready, hT_copied, z_ready, ft_ready, slope_ready, gaps_ready, exp_ready,
         message_ready, x1_ready, x1_turned, x1_copied, start, pool_go, step_n, step_s, step_f, step_l) = (
            m.slots(n) if n in DMA_SEMS else m.sem(n) for n in names)
        block = ctx.enter_context(nc.Block())

        @block.sync
        def _(eng):
            for u in range(2):
                eng.sem_inc(spilled[u], 32)
                eng.sem_inc(stored[u], 32)
                eng.sem_inc(f_stored[u], 16)

            def load_ids(b, u):
                eng.dma_start(ids[u][:, :], inp["ids"][b, :, :]).then_inc(ids_loaded[u], 16)
                eng.dma_start(ends[u][:, :], tab["end"][b, :, :]).then_inc(ids_loaded[u], 16)

            def load_rows(b, u):
                at = bass.ds(b * BE, BE)
                eng.dma_start(rows[u][:, 0, :], inp["w"][at].rearrange("(a e) -> a e", a=1)).then_inc(rows_loaded[u], 16)
                eng.dma_start(rows[u][:, 1, :], tab["cut"][at].rearrange("(a e) -> a e", a=1)).then_inc(rows_loaded[u], 16)

            def step(b, u, early, late):
                if early:
                    eng.wait_ge(gathered[u], nth(128, b, u))
                    eng.dma_start(tab["xs"][b, :, :], x[u][:, 0:J, :].rearrange("p j f -> p (j f)")).then_inc(spilled[u], 16)
                    eng.dma_start(tab["xd"][b, :, :], x[u][:, J:, :].rearrange("p j f -> p (j f)")).then_inc(spilled[u], 16)
                    if not (isinstance(b, int) and b == NB - 1):
                        eng.wait_ge(z_ready, b + 1)
                        load_rows(b + 1, 1 - u)
                        eng.wait_ge(placed[u], nth(64, b, u))
                        load_ids(b + 2, u)
                if late:
                    v = 1 - u
                    eng.wait_ge(x1_ready, b)
                    eng.dma_start(tab["x1f"][b - 1, :, :], x1f[v][:, :]).then_inc(f_stored[v], 16)
                    eng.wait_ge(x1_copied, b + 1)
                    eng.dma_start(edge_rows_of(tab["x1"], b - 1), x1e[v][:, :, :]).then_inc(stored[v], 16)
                    eng.dma_start(tab["er2"][:, bass.ds((b - 1) * BE, BE)], er2[v][:, :]).then_inc(stored[v], 16)

            load_ids(0, 0)
            load_ids(1, 1)
            load_rows(0, 0)
            steps(eng, NB, step)
            for u in range(2):
                eng.wait_ge(spilled[u], 16 * NB + 32)
                eng.wait_ge(stored[u], 16 * NB + 32)
                eng.wait_ge(f_stored[u], 8 * NB + 16)
            eng.wait_ge(ids_loaded[0], 16 * NB + 32)

        @block.gpsimd
        def _(eng):
            def body(b, u):
                eng.wait_ge(ids_loaded[u], nth(32, b, u))
                eng.wait_ge(h_ready, b + 1)
                eng.wait_ge(spilled[u], nth(32, b, u))
                eng.sem_inc(pool_go, 1)
                for j in range(J):
                    for k in (0, 1):
                        eng.indirect_dma_start(
                            x[u][:, k * J + j, :], None, inp["x"][:, :],
                            bass.IndirectOffsetOnAxis(ap=ids[u][:, k * J + j:k * J + j + 1], axis=0)).then_inc(gathered[u], 16)
                for j in range(J):
                    eng.indirect_dma_start(
                        tab["pos"][:, :], bass.IndirectOffsetOnAxis(ap=ends[u][:, j:j + 1], axis=0),
                        ids[u][:, 2 * J + j:2 * J + j + 1], None,
                        bounds_check=N - 1, oob_is_err=False).then_inc(placed[u], 16)

            blocks(eng, NB, body)
            for u in range(2):
                eng.wait_ge(placed[u], 32 * NB)

        @block.vector
        def _(eng):
            ln, ls = Link(eng, step_n, 4), Link(eng, step_s, 3)
            lf, ll = Link(eng, step_f, FIRST_LINKS), Link(eng, step_l, LAST_LINKS)
            eng.sem_inc(gaps_ready, 1)
            eng.sem_inc(message_ready, 1)
            start_attention(eng, t, start)

            def step(b, u, early, late):
                v = 1 - u
                if early:
                    ln.begin(b)
                    eng.wait_ge(gathered[u], nth(128, b, u))
                    for g in range(2 * J):
                        last = eng.bn_stats(norm.raw[u][:, g, :], x[u][:, g, :])
                    ln(last)
                    moments(eng, ln, norm, u).then_inc(var_ready, 1)
                    ln.end()
                if late:
                    lf.begin(b - 1)
                    eng.wait_ge(slope_ready, b)
                    first_attention(eng, lf, p_z, slope, p_w, p_cut, t, v).then_inc(gaps_ready, 1)
                    lf.end()
                if early:
                    ls.begin(b)
                    eng.wait_ge(guess_ready, b + 1)
                    scales(eng, ls, norm, u).then_inc(scale_ready, 1)
                    ls.end()
                if late:
                    ll.begin(b - 1)
                    eng.wait_ge(exp_ready, b)
                    eng.wait_ge(ft_ready, b)
                    eng.tensor_tensor(t["message"][:, :], p_ft[:, :], t["weight"][:, :], ALU.mult).then_inc(message_ready, 1)
                    eng.wait_ge(message_ready, b + 1)
                    eng.wait_ge(f_stored[v], nth(16, b - 1, v))
                    last_attention(eng, ll, t, v, x1f[v][:, :]).then_inc(x1_ready, 1)
                    ll.end()

            steps(eng, NB, step)

        @block.scalar
        def _(eng):
            eng.preload_act_table_set(TABLE)
            eng.sem_inc(h_ready, 2)
            eng.sem_inc(x1_copied, 1)

            def step(b, u, early, late):
                v = 1 - u
                if early:
                    eng.wait_ge(var_ready, b + 1)
                    eng.activation(norm.log[u][:, :], norm.var[u][:, :], ACT.Ln).then_inc(log_ready, 1)
                    eng.wait_ge(log_ready, b + 1)
                    eng.activation(norm.guess[u][:, :], norm.log[u][:, :], ACT.Exp, scale=-0.5).then_inc(guess_ready, 1)
                if late:
                    eng.wait_ge(gaps_ready, b + 1)
                    eng.activation(t["weight"][:, :], t["below"][:, :], ACT.Exp)
                    eng.activation(t["fade"][:, :], t["fall"][:, :], ACT.Exp).then_inc(exp_ready, 1)
                if early:
                    eng.wait_ge(scale_ready, b + 1)
                    for g in range(2 * J):
                        last = eng.activation(h[:, g, :], x[u][:, g, :], ACT.Relu,
                                              bias=norm.shift[u][:, g:g + 1], scale=norm.scale[u][:, g:g + 1])
                    last.then_inc(h_ready, 1)
                    eng.wait_ge(hT_ready, b + 1)
                    eng.activation(hT[:, 0, :], p_hT[0][:, :], ACT.Copy)
                    eng.activation(hT[:, 1, :], p_hT[1][:, :], ACT.Copy).then_inc(hT_copied, 1)
                    eng.wait_ge(z_ready, b + 2)
                    eng.activation(slope[:, :], p_z[:, :], ACT.Copy, scale=SLOPE).then_inc(slope_ready, 1)
                if late:
                    eng.wait_ge(x1_turned, b)
                    eng.wait_ge(stored[v], nth(32, b - 1, v))
                    eng.activation(x1e[v][:, :, :].rearrange("p j f -> p (j f)"), p_x1[:, :], ACT.Copy)
                    eng.activation(er2[v][:, :], p_er2[:, :], ACT.Copy).then_inc(x1_copied, 1)

            steps(eng, NB, step)

        @block.tensor
        def _(eng):
            eng.sem_inc(z_ready, 1)

            def step(b, u, early, late):
                v = 1 - u
                if early:
                    eng.wait_ge(h_ready, b + 3)
                    for g in range(2 * J):
                        at = slice(g % J * 128, g % J * 128 + 128)
                        last = eng.transpose(p_hT[g // J][:, at], h[:, g, :], keep["ident"][:, :])
                    last.then_inc(hT_ready, 1)
                    eng.wait_ge(gaps_ready, b + 1)
                    eng.wait_ge(rows_loaded[u], nth(32, b, u))
                    eng.matmul(p_w[:, :], keep["ones"][0:1, :], rows[u][:, 0, :], start=True, stop=True)
                    eng.matmul(p_cut[:, :], keep["ones"][0:1, :], rows[u][:, 1, :], start=True, stop=True)
                    eng.wait_ge(hT_copied, b + 1)
                    eng.matmul(p_z[:, :], keep["wel1"][:, :], hT[:, 0, :], start=True, stop=False)
                    eng.matmul(p_z[:, :], keep["wer1"][:, :], hT[:, 1, :], start=False, stop=True).then_inc(z_ready, 1)
                    eng.wait_ge(message_ready, b + 1)
                    eng.matmul(p_ft[:, :], keep["w1"][:, :], hT[:, 0, :], start=True, stop=True).then_inc(ft_ready, 1)
                if late:
                    eng.wait_ge(x1_ready, b)
                    eng.wait_ge(x1_copied, b)
                    for j in range(J):
                        at = slice(j * 128, j * 128 + 128)
                        eng.transpose(p_x1[:, at], x1f[v][:, at], keep["ident"][:, :])
                    eng.matmul(p_er2[:, :], keep["wer2"][:, :], x1f[v][:, :], start=True, stop=True).then_inc(x1_turned, 1)

            steps(eng, NB, step)


def gat2_phase(nc, keep, inp, tab):
    from contextlib import ExitStack
    import concourse.bass as bass
    from concourse import mybir
    from concourse.alu_op_type import AluOpType as ALU

    ACT, i32 = mybir.ActivationFunctionType, mybir.dt.int32
    with ExitStack() as ctx:
        m = Memory(nc, ctx, "g2")
        two = lambda n, s, dt=None: [m.sb(f"{n}{u}", s, dt) for u in range(2)]
        ids, at_edge = two("ids", [128, 3 * J], i32), two("at_edge", [128, J], i32)
        x, x1f, x2f = two("x", [128, J, F]), two("x1f", [128, BE]), two("x2f", [128, BE])
        rows, er2 = two("rows", [1, 2, BE]), two("er2", [H, BE])
        hT, slope = m.sb("hT", [128, BE]), m.sb("slope", [128, BE])
        delta = two("delta", [128, J, F])
        t = attention_tiles(m)
        p_hT, p_ft, p_z, p_w, p_cut, p_delta = (m.ps(n, [128, BE]) for n in ("p_hT", "p_ft", "p_z", "p_w", "p_cut", "p_delta"))
        names = ("ids_loaded", "rows_loaded", "x1f_loaded", "found", "found_stored", "gathered", "stored", "hT_ready",
                 "hT_copied", "z_ready", "ft_ready", "slope_ready", "gaps_ready", "exp_ready", "message_ready",
                 "x2_ready", "delta_ready", "delta_copied", "start", "pool_go", "step_f", "step_l")
        (ids_loaded, rows_loaded, x1f_loaded, found, found_stored, gathered, stored, hT_ready, hT_copied, z_ready,
         ft_ready, slope_ready, gaps_ready, exp_ready, message_ready, x2_ready, delta_ready, delta_copied, start,
         pool_go, step_f, step_l) = (m.slots(n) if n in DMA_SEMS else m.sem(n) for n in names)
        block = ctx.enter_context(nc.Block())

        @block.sync
        def _(eng):
            for u in range(2):
                eng.sem_inc(found_stored[u], 16)
                eng.sem_inc(stored[u], 16)

            def load_ids(b, u):
                eng.dma_start(ids[u][:, :], inp["ids"][b, :, :]).then_inc(ids_loaded[u], 16)

            def load_rows(b, u):
                at = bass.ds(b * BE, BE)
                eng.dma_start(rows[u][:, 0, :], inp["w"][at].rearrange("(a e) -> a e", a=1)).then_inc(rows_loaded[u], 16)
                eng.dma_start(rows[u][:, 1, :], tab["cut"][at].rearrange("(a e) -> a e", a=1)).then_inc(rows_loaded[u], 16)
                eng.dma_start(er2[u][:, :], tab["er2"][:, at]).then_inc(rows_loaded[u], 16)

            def step(b, u, early, late):
                if early:
                    eng.wait_ge(found[u], nth(64, b, u))
                    eng.dma_start(tab["at"][b, :, :], at_edge[u][:, :]).then_inc(found_stored[u], 16)
                    if not (isinstance(b, int) and b == NB - 1):
                        load_ids(b + 2, u)
                        eng.wait_ge(z_ready, b + 1)
                        load_rows(b + 1, 1 - u)
                    eng.wait_ge(delta_ready, b + 1)
                    eng.dma_start(x1f[u][:, :], tab["x1f"][b, :, :]).then_inc(x1f_loaded[u], 16)
                if late:
                    eng.wait_ge(delta_copied, b + 1)
                    eng.dma_start(edge_rows_of(tab["delta"], b - 1), delta[1 - u][:, :, :]).then_inc(stored[1 - u], 16)

            load_ids(0, 0)
            load_ids(1, 1)
            load_rows(0, 0)
            steps(eng, NB, step)
            for u in range(2):
                eng.wait_ge(found_stored[u], 8 * NB + 16)
                eng.wait_ge(stored[u], 8 * NB + 16)
            eng.wait_ge(ids_loaded[0], 8 * NB + 16)

        @block.gpsimd
        def _(eng):

            def step(b, u, early, late):
                v = 1 - u
                if early:
                    eng.wait_ge(ids_loaded[u], nth(16, b, u))
                    eng.wait_ge(hT_ready, b + 1)
                    eng.wait_ge(found_stored[u], nth(16, b, u))
                    eng.sem_inc(pool_go, 1)
                    for j in range(J):
                        eng.indirect_dma_start(
                            at_edge[u][:, j:j + 1], None, tab["pos"][:, :],
                            bass.IndirectOffsetOnAxis(ap=ids[u][:, j:j + 1], axis=0)).then_inc(found[u], 16)
                if late:
                    eng.wait_ge(found[v], nth(64, b - 1, v))
                    eng.wait_ge(hT_ready, b)
                    eng.sem_inc(pool_go, 1)
                    for j in range(J):
                        eng.indirect_dma_start(
                            x[v][:, j, :], None, tab["x1"][:, :],
                            bass.IndirectOffsetOnAxis(ap=at_edge[v][:, j:j + 1], axis=0)).then_inc(gathered[v], 16)

            steps(eng, NB, step)

        @block.vector
        def _(eng):
            lf, ll = Link(eng, step_f, FIRST_LINKS), Link(eng, step_l, LAST_LINKS)
            eng.sem_inc(gaps_ready, 1)
            eng.sem_inc(message_ready, 1)
            start_attention(eng, t, start)

            def step(b, u, early, late):
                v = 1 - u
                if early:
                    lf.begin(b)
                    eng.wait_ge(slope_ready, b + 1)
                    eng.wait_ge(exp_ready, b) if late else None
                    first_attention(eng, lf, p_z, slope, p_w, p_cut, t, u).then_inc(gaps_ready, 1)
                    lf.end()
                if late:
                    ll.begin(b - 1)
                    eng.wait_ge(exp_ready, b)
                    eng.wait_ge(ft_ready, b)
                    eng.tensor_tensor(t["message"][:, :], p_ft[:, :], t["weight"][:, :], ALU.mult).then_inc(message_ready, 1)
                    eng.wait_ge(message_ready, b + 1)
                    last_attention(eng, ll, t, v, x2f[v][:, :]).then_inc(x2_ready, 1)
                    ll.end()

            steps(eng, NB, step)

        @block.scalar
        def _(eng):
            eng.preload_act_table_set(TABLE)
            eng.sem_inc(delta_copied, 1)

            def step(b, u, early, late):
                v = 1 - u
                if early:
                    eng.wait_ge(hT_ready, b + 3)
                    eng.activation(hT[:, :], p_hT[:, :], ACT.Copy).then_inc(hT_copied, 1)
                    eng.wait_ge(z_ready, b + 2)
                    eng.activation(slope[:, :], p_z[:, :], ACT.Copy, scale=SLOPE).then_inc(slope_ready, 1)
                if late:
                    eng.wait_ge(delta_ready, b + 2)
                    eng.wait_ge(stored[v], nth(16, b - 1, v))
                    eng.activation(delta[v][:, :, :].rearrange("p j f -> p (j f)"), p_delta[:, :], ACT.Copy).then_inc(delta_copied, 1)
                if early:
                    eng.wait_ge(gaps_ready, b + 2)
                    if late:
                        eng.wait_ge(x2_ready, b)
                    eng.activation(t["weight"][:, :], t["below"][:, :], ACT.Exp)
                    eng.activation(t["fade"][:, :], t["fall"][:, :], ACT.Exp).then_inc(exp_ready, 1)

            steps(eng, NB, step)

        @block.tensor
        def _(eng):
            eng.sem_inc(z_ready, 1)
            eng.sem_inc(hT_ready, 2)
            eng.sem_inc(delta_ready, 2)

            def step(b, u, early, late):
                v = 1 - u
                if early:
                    eng.wait_ge(gathered[u], nth(64, b, u))
                    for j in range(J):
                        last = eng.transpose(p_hT[:, j * 128:(j + 1) * 128], x[u][:, j, :], keep["ident"][:, :])
                    last.then_inc(hT_ready, 1)
                    eng.wait_ge(gaps_ready, b + 1)
                    eng.wait_ge(rows_loaded[u], nth(48, b, u))
                    eng.matmul(p_w[:, :], keep["ones"][0:1, :], rows[u][:, 0, :], start=True, stop=True)
                    eng.matmul(p_cut[:, :], keep["ones"][0:1, :], rows[u][:, 1, :], start=True, stop=True)
                    eng.matmul(p_z[:, :], keep["expand"][:, :], er2[u][:, :], start=True, stop=False)
                    eng.wait_ge(hT_copied, b + 1)
                    eng.matmul(p_z[:, :], keep["wel2"][:, :], hT[:, :], start=False, stop=True).then_inc(z_ready, 1)
                    eng.wait_ge(message_ready, b + 1)
                    eng.matmul(p_ft[:, :], keep["w2"][:, :], hT[:, :], start=True, stop=True).then_inc(ft_ready, 1)
                if late:
                    eng.wait_ge(x1f_loaded[v], nth(16, b - 1, v))
                    eng.wait_ge(x2_ready, b)
                    eng.wait_ge(delta_copied, b)
                    for j in range(J):
                        at = slice(j * 128, j * 128 + 128)
                        eng.matmul(p_delta[:, at], keep["ones"][0:1, :], keep["bmrow"][:, :], start=True, stop=False)
                        eng.matmul(p_delta[:, at], x1f[v][:, at], keep["wm"][:, 0, :], start=False, stop=False)
                        last = eng.matmul(p_delta[:, at], x2f[v][:, at], keep["wm"][:, 1, :], start=False, stop=True)
                    last.then_inc(delta_ready, 1)

            steps(eng, NB, step)


def rgcn_phase(nc, keep, inp, tab, out):
    from contextlib import ExitStack
    import concourse.bass as bass
    from concourse import mybir
    from concourse.alu_op_type import AluOpType as ALU

    ACT, i32, bf16 = mybir.ActivationFunctionType, mybir.dt.int32, mybir.dt.bfloat16
    with ExitStack() as ctx:
        m = Memory(nc, ctx, "rg")
        two = lambda n, s, dt=None: [m.sb(f"{n}{u}", s, dt) for u in range(2)]
        at_edge, ends = two("at_edge", [128, J], i32), two("ends", [128, J], i32)
        x, own, far = two("x", [128, 2 * J, F]), two("own", [128, J, F]), two("far", [128, J, F])
        y = two("y", [128, 2 * J, F])
        hot, same = two("hot", [R, BE], bf16), two("same", [1, BE])
        h, hT = m.sb("h", [128, 2 * J, F]), m.sb("hT", [128, 2, BE])
        of_rel = m.sb("of_rel", [128, R, BE])
        message, agg = m.sb("message", [128, BE]), two("agg", [128, BE])
        low, res = m.sb("low", [128, J, F]), two("res", [128, J, F])
        norm = Norm(m, 128, 2 * J)
        p_hT = [m.ps("p_hs", [128, BE]), m.ps("p_hd", [128, BE])]
        p_mask = [m.ps("p_mask0", [128, BE]), m.ps("p_mask1", [128, BE])]
        p_msg, p_same, p_o = m.ps("p_msg", [128, BE]), m.ps("p_same", [128, BE]), m.ps("p_o", [128, J, F])
        names = ("at_loaded", "ends_loaded", "x_loaded", "rows_loaded", "gathered", "scattered", "y_ready",
                 "var_ready", "log_ready", "guess_ready", "scale_ready", "h_ready", "hT_ready", "hT_copied",
                 "mask_ready", "of_rel_ready", "msg_ready", "same_ready", "msg_copied", "agg_ready", "o_ready", "res_ready",
                 "rows_left", "pool_go", "start", "step_n", "step_s", "step_o")
        (at_loaded, ends_loaded, x_loaded, rows_loaded, gathered, scattered, y_ready, var_ready, log_ready,
         guess_ready, scale_ready, h_ready, hT_ready, hT_copied, mask_ready, of_rel_ready, msg_ready, same_ready,
         msg_copied, agg_ready, o_ready, res_ready, rows_left, pool_go, start, step_n, step_s, step_o) = (m.slots(n) if n in DMA_SEMS else m.sem(n) for n in names)
        block = ctx.enter_context(nc.Block())

        @block.sync
        def _(eng):
            def load_at(b, u):
                eng.dma_start(at_edge[u][:, :], tab["at"][b, :, :]).then_inc(at_loaded[u], 16)

            def load_x(b, u):
                eng.dma_start(x[u][:, 0:J, :].rearrange("p j f -> p (j f)"), tab["xs"][b, :, :]).then_inc(x_loaded[u], 16)
                eng.dma_start(x[u][:, J:, :].rearrange("p j f -> p (j f)"), tab["xd"][b, :, :]).then_inc(x_loaded[u], 16)
                eng.dma_start(own[u][:, :, :], edge_rows_of(tab["delta"], b)).then_inc(x_loaded[u], 16)

            def step(b, u, early, late):
                if early:
                    eng.wait_ge(msg_ready, b + 1)
                    if not (isinstance(b, int) and b == NB - 1):
                        eng.wait_ge(y_ready, b + 1)
                        load_x(b + 1, 1 - u)
                    at = bass.ds(b * BE, BE)
                    eng.dma_start(hot[u][:, :], tab["hot"][:, at]).then_inc(rows_loaded[u], 16)
                    eng.dma_start(same[u][:, :], tab["same"][at].rearrange("(a e) -> a e", a=1)).then_inc(rows_loaded[u], 16)
                    eng.wait_ge(rows_left, b + 1)
                    eng.dma_start(ends[u][:, :], tab["end"][b, :, :]).then_inc(ends_loaded[u], 16)
                    if not (isinstance(b, int) and b == NB - 1):
                        eng.wait_ge(gathered[u], nth(64, b, u))
                        load_at(b + 2, u)

            load_at(0, 0)
            load_at(1, 1)
            load_x(0, 0)
            steps(eng, NB, step)
            eng.wait_ge(at_loaded[0], 8 * NB + 16)

        @block.gpsimd
        def _(eng):
            eng.sem_inc(rows_left, 2)

            def gather(b, u):
                eng.wait_ge(at_loaded[u], nth(16, b, u))
                if not (isinstance(b, int) and b == 0):
                    eng.wait_ge(y_ready, b)
                eng.sem_inc(pool_go, 1)
                for j in range(J):
                    eng.indirect_dma_start(
                        far[u][:, j, :], None, tab["delta"][:, :],
                        bass.IndirectOffsetOnAxis(ap=at_edge[u][:, j:j + 1], axis=0)).then_inc(gathered[u], 16)

            def step(b, u, early, late):
                v = 1 - u
                if early and not (isinstance(b, int) and b == NB - 1):
                    gather(b + 1, v)
                if late:
                    eng.wait_ge(ends_loaded[v], nth(16, b - 1, v))
                    eng.wait_ge(res_ready, b + 1)
                    eng.sem_inc(pool_go, 1)
                    for j in range(J):
                        eng.indirect_dma_start(
                            out[:, :], bass.IndirectOffsetOnAxis(ap=ends[v][:, j:j + 1], axis=0),
                            res[v][:, j, :], None, bounds_check=N - 1, oob_is_err=False).then_inc(scattered[v], 16)
                    eng.wait_ge(scattered[v], nth(64, b - 1, v))
                    eng.sem_inc(rows_left, 1)

            eng.wait_ge(start, 1)
            gather(0, 0)
            steps(eng, NB, step)

        @block.vector
        def _(eng):
            ln, ls, lo = Link(eng, step_n, 4), Link(eng, step_s, 4), Link(eng, step_o, 2)
            eng.sem_inc(y_ready, 1)
            eng.sem_inc(res_ready, 1)
            eng.memset(agg[1][:, BE - 1:BE], 0.0).then_inc(start, 1)
            eng.wait_ge(start, 1)

            def step(b, u, early, late):
                v = 1 - u
                if early:
                    ln.begin(b)
                    eng.wait_ge(x_loaded[u], nth(48, b, u))
                    eng.wait_ge(gathered[u], nth(64, b, u))
                    if late:
                        eng.wait_ge(res_ready, b)
                    eng.tensor_tensor(y[u][:, J:, :], x[u][:, J:, :], own[u][:, :, :], ALU.add)
                    eng.tensor_tensor(y[u][:, 0:J, :], x[u][:, 0:J, :], far[u][:, :, :], ALU.add).then_inc(y_ready, 1)
                    eng.wait_ge(y_ready, b + 2)
                    for g in range(2 * J):
                        last = eng.bn_stats(norm.raw[u][:, g, :], y[u][:, g, :])
                    ln(last)
                    moments(eng, ln, norm, u).then_inc(var_ready, 1)
                    ln.end()
                if late:
                    eng.wait_ge(hT_copied, b)
                    for r in range(R):
                        eng.wait_ge(mask_ready, (b - 1) * R + r + 1)
                        eng.tensor_tensor(of_rel[:, r, :], p_mask[r % 2][:, :], hT[:, 0, :], ALU.mult).then_inc(of_rel_ready, 1)
                if early:
                    ls.begin(b)
                    eng.wait_ge(guess_ready, b + 1)
                    scales(eng, ls, norm, u, keep["norm"][:, bass.ds(b * J, J)]).then_inc(scale_ready, 1)
                    ls.end()
                if late:
                    eng.wait_ge(msg_copied, b)
                    eng.wait_ge(same_ready, b)
                    eng.tensor_tensor_scan(agg[v][:, :], p_same[:, :], message[:, :], agg[u][:, BE - 1:BE],
                                           ALU.mult, ALU.add).then_inc(agg_ready, 1)
                    lo.begin(b - 1)
                    eng.wait_ge(o_ready, b)
                    lo(eng.scalar_tensor_tensor(low[:, :, :], p_o[:, :, :], 0.0, keep["alpha4"][:, :, :],
                                                ALU.min, ALU.mult))
                    lo(eng.scalar_tensor_tensor(low[:, :, :], p_o[:, :, :], 0.0, low[:, :, :], ALU.max, ALU.add))
                    eng.wait_ge(rows_left, b)
                    eng.tensor_tensor(res[v][:, :, :], low[:, :, :], y[v][:, J:, :], ALU.add).then_inc(res_ready, 1)
                    lo.end()

            steps(eng, NB, step)

        @block.scalar
        def _(eng):
            eng.preload_act_table_set(TABLE)

            def step(b, u, early, late):
                if early:
                    eng.wait_ge(var_ready, b + 1)
                    eng.activation(norm.log[u][:, :], norm.var[u][:, :], ACT.Ln).then_inc(log_ready, 1)
                    eng.wait_ge(log_ready, b + 1)
                    eng.activation(norm.guess[u][:, :], norm.log[u][:, :], ACT.Exp, scale=-0.5).then_inc(guess_ready, 1)
                if late:
                    eng.wait_ge(msg_ready, b + 2)
                    eng.activation(message[:, :], p_msg[:, :], ACT.Copy).then_inc(msg_copied, 1)
                if early:
                    eng.wait_ge(scale_ready, b + 1)
                    for g in range(2 * J):
                        last = eng.activation(h[:, g, :], y[u][:, g, :], ACT.Relu,
                                              bias=norm.shift[u][:, g:g + 1], scale=norm.scale[u][:, g:g + 1])
                    last.then_inc(h_ready, 1)
                    eng.wait_ge(hT_ready, b + 1)
                    eng.activation(hT[:, 0, :], p_hT[0][:, :], ACT.Copy)
                    eng.activation(hT[:, 1, :], p_hT[1][:, :], ACT.Copy).then_inc(hT_copied, 1)

            steps(eng, NB, step)

        @block.tensor
        def _(eng):
            eng.sem_inc(msg_ready, 2)

            def step(b, u, early, late):
                v = 1 - u
                if late:
                    def mask(r):
                        eng.matmul(p_mask[r % 2][:, :], keep["pick"][:, r, :], hot[v][:, :],
                                   start=True, stop=True).then_inc(mask_ready, 1)

                    eng.wait_ge(rows_loaded[v], nth(32, b - 1, v))
                    mask(0)
                    mask(1)
                    eng.matmul(p_same[:, :], keep["ones"][0:1, :], same[v][:, :], start=True, stop=True).then_inc(same_ready, 1)
                    for r in range(R):
                        eng.wait_ge(of_rel_ready, (b - 1) * R + r + 1)
                        last = eng.matmul(p_msg[:, :], keep["wrel"][:, r, :], of_rel[:, r, :],
                                          start=(r == 0), stop=(r == R - 1))
                        if r < R - 2:
                            mask(r + 2)
                    last.then_inc(msg_ready, 1)
                    eng.wait_ge(agg_ready, b)
                    for j in range(J):
                        at = slice(j * 128, j * 128 + 128)
                        eng.matmul(p_o[:, j, :], hT[:, 1, at], keep["root"][:, :], start=True, stop=False)
                        eng.matmul(p_o[:, j, :], keep["ones"][0:1, :], keep["biasrow"][:, :], start=False, stop=False)
                        last = eng.matmul(p_o[:, j, :], agg[v][:, at], keep["ident"][:, :], start=False, stop=True)
                    last.then_inc(o_ready, 1)
                if early:
                    eng.wait_ge(h_ready, b + 1)
                    for g in range(2 * J):
                        at = slice(g % J * 128, g % J * 128 + 128)
                        last = eng.transpose(p_hT[g // J][:, at], h[:, g, :], keep["ident"][:, :])
                    last.then_inc(hT_ready, 1)

            steps(eng, NB, step)


def program(nc, inp, out):
    from contextlib import ExitStack
    from concourse import mybir

    fp32, i32, bf16 = mybir.dt.float32, mybir.dt.int32, mybir.dt.bfloat16
    shapes = {"xs": ((NB, 128, BE), fp32), "xd": ((NB, 128, BE), fp32), "x1f": ((NB, 128, BE), fp32),
              "x1": ((EP + 1, F), fp32), "delta": ((EP + 1, F), fp32), "er2": ((H, EP), fp32),
              "cut": ((EP,), fp32), "same": ((EP,), fp32), "hot": ((R, EP), bf16), "pos": ((N, 1), i32),
              "end": ((NB + 1, 128, J), i32), "at": ((NB + 1, 128, J), i32)}
    tab = {k: nc.dram_tensor(f"tab_{k}", s, dt).ap() for k, (s, dt) in shapes.items()}
    with ExitStack() as ctx:
        m = Memory(nc, ctx, "keep")
        keep = {"ident": m.sb("ident", [128, 128]), "expand": m.sb("expand", [H, 128]),
                "pick": m.sb("pick", [R, R, 128], bf16), "ones": m.sb("ones", [1, 128]),
                "w1": m.sb("w1", [128, 128]), "w2": m.sb("w2", [128, 128]), "wm": m.sb("wm", [128, 2, 128]),
                "root": m.sb("root", [128, 128]), "wrel": m.sb("wrel", [128, R, 128]),
                "wel1": m.sb("wel1", [128, 128]), "wer1": m.sb("wer1", [128, 128]),
                "wel2": m.sb("wel2", [128, 128]), "wer2": m.sb("wer2", [128, H]),
                "bmrow": m.sb("bmrow", [1, F]), "biasrow": m.sb("biasrow", [1, F]),
                "bm4": m.sb("bm4", [128, J, F]), "alpha4": m.sb("alpha4", [128, J, F]),
                "norm": m.sb("norm", [128, TILES])}
        weights_phase(nc, keep, inp)
        edge_rows_phase(nc, keep, inp, tab)
        counts_phases(nc, keep, inp, tab)
        nodes_phase(nc, keep, inp, out)
        gat1_phase(nc, keep, inp, tab)
        spread_phases(nc, keep, inp, tab)
        gat2_phase(nc, keep, inp, tab)
        rgcn_phase(nc, keep, inp, tab, out)


def kernel(**inputs):
    import concourse.bacc as _bacc
    from concourse import mybir as _mybir
    from concourse.bass_utils import run_bass_kernel_spmd as _run
    import ml_dtypes

    src, dst, kind, w = (np.asarray(inputs[k]) for k in ("src", "dst", "edge_type_8", "edge_weight"))

    def padded(a, value, extra=0):
        return np.concatenate([a, np.full(EP + extra - E, value, a.dtype)])

    def edge_rows(a):
        return np.ascontiguousarray(a.reshape(-1, 128).T)

    def by_block(a):
        return a.reshape(NB + 1, J, 128).transpose(0, 2, 1)

    numbers = padded(np.arange(E, dtype=np.int32), 0, BE)
    ids = np.concatenate([by_block(padded(src, 0, BE)), by_block(padded(dst, 0, BE)), by_block(numbers)], axis=2)
    segments = padded(dst, N)
    row = np.arange(128)
    heads = (row[:, None] // D == np.arange(H)[None, :])
    arrays = {
        "x": np.asarray(inputs["x"]), "ids": np.ascontiguousarray(ids), "w": padded(w, 0), "kind": padded(kind, 0),
        "dseg": np.concatenate([np.full(1, -1, dst.dtype), segments, np.full(1, -1, dst.dtype)]),
        "here": edge_rows(segments), "next": edge_rows(np.concatenate([segments[1:], np.full(1, -1, dst.dtype)])),
        "ident": np.eye(128, dtype=np.float32), "ones": np.ones((1, 128), np.float32),
        "blockmask": (row[:, None] // D == row[None, :] // D).astype(np.float32),
        "headsel": heads.astype(np.float32), "expand": np.ascontiguousarray(heads.T.astype(np.float32)),
        "pick": np.ascontiguousarray(np.broadcast_to(np.eye(R)[:, :, None], (R, R, 128)).astype(ml_dtypes.bfloat16)),
        "relcol": (np.arange(R * C) // C).astype(np.float32)[:, None],
        "chunksel": (np.arange(R * C)[:, None] % C == np.arange(C)[None, :]).astype(np.float32),
        "W1": np.asarray(inputs["L0_gnn_W1"]), "W2": np.asarray(inputs["L0_gnn_W2"]),
        "al1": np.asarray(inputs["L0_gnn_al1"]), "ar1": np.asarray(inputs["L0_gnn_ar1"]),
        "al2": np.asarray(inputs["L0_gnn_al2"]), "ar2": np.asarray(inputs["L0_gnn_ar2"]),
        "Wm": np.asarray(inputs["L0_gnn_Wm"]), "bm": np.asarray(inputs["L0_gnn_bm"]),
        "basis": np.asarray(inputs["L1_gnn_basis"]), "comp": np.asarray(inputs["L1_gnn_comp"]),
        "root": np.asarray(inputs["L1_gnn_root"]), "bias": np.asarray(inputs["L1_gnn_bias"]),
        "alpha": np.asarray(inputs["L1_gnn_alpha"]),
    }
    nc = _bacc.Bacc("TRN2", target_bir_lowering=False, num_devices=1)
    inp = {k: nc.dram_tensor(f"in_{k}", a.shape, _mybir.dt.from_np(a.dtype), kind="ExternalInput").ap()
           for k, a in arrays.items()}
    out = nc.dram_tensor("out_0", (N, F), _mybir.dt.float32, kind="ExternalOutput").ap()
    program(nc, inp, out)
    r = _run(nc, [{f"in_{k}": a for k, a in arrays.items()}], core_ids=[0])
    return r.results[0]["out_0"]
```

```python
import numpy as np

N = 100000
E = 50000
F = 128
H = 8
D = F // H
R = 8
BE = 512
J = BE // 128
NB = 2 * -(-E // (2 * BE))
EP = NB * BE
TILES = EP // 128
C = 8
CL = EP // C
CT = CL // 128
NP = 125
JN = 8
NQ = N // (NP * JN)
ZERO_ROW = EP
FAR = 1 << 20
CUT = -1e30
EPS = 1e-5
SLOPE = 0.1
DMA_SEMS = {"x_loaded", "stored", "gathered", "placed", "spilled", "f_stored", "ids_loaded", "rows_loaded",
            "x1f_loaded", "found", "found_stored", "y_kept", "at_loaded", "ends_loaded", "scattered"}
TABLE = "natural_log_exp_and_others"


def steps(eng, count, depth, step, ahead=0, ways=2):
    def peeled(b):
        step(b, b % ways, lambda k: 0 <= b - k < count)

    head = -(-depth // ways) * ways
    turns = (count - head - ahead) // ways
    for b in range(head):
        peeled(b)
    with eng.Fori(0, turns) as i:
        for k in range(ways):
            step(i * ways + (head + k), k, lambda k: True)
    for b in range(head + turns * ways, count + depth):
        peeled(b)


def blocks(eng, count, body):
    with eng.Fori(0, count // 2) as i:
        body(i * 2, 0)
        body(i * 2 + 1, 1)


def nth(k, b, slot, ways=2):
    return (b - slot) * (k // ways) + k


class Link:

    def __init__(self, eng, sem, per_block):
        self.eng, self.sem, self.per_block = eng, sem, per_block

    def begin(self, b):
        self.block, self.base, self.n = b, b * self.per_block, 0

    def __call__(self, ins):
        self.n += 1
        ins.then_inc(self.sem, 1)
        self.eng.wait_ge(self.sem, self.base + self.n)

    def end(self):
        assert self.n == self.per_block, self.n


class Memory:

    used = []

    def __init__(self, nc, ctx, name):
        from concourse import mybir

        self.nc, self.ctx, self.name, self.fp32 = nc, ctx, name, mybir.dt.float32

    def sb(self, name, shape, dt=None):
        return self.ctx.enter_context(self.nc.sbuf_tensor(f"{self.name}_{name}", shape, dt or self.fp32))

    def ps(self, name, shape):
        return self.ctx.enter_context(self.nc.psum_tensor(f"{self.name}_{name}", shape, self.fp32))

    def slots(self, name):
        return [self.sem(f"{name}{u}") for u in range(2)]

    def sem(self, name):
        sem = self.ctx.enter_context(self.nc.semaphore(f"{self.name}_{name}"))
        Memory.used.append(sem)
        return sem


def clear_semaphores(nc):
    with nc.Block() as block:
        @block.gpsimd
        def _(eng):
            for sem in Memory.used:
                eng.sem_clear(sem)
            Memory.used.clear()


def weights_phase(nc, keep, inp, tab):
    from contextlib import ExitStack
    from concourse import mybir
    from concourse.alu_op_type import AluOpType as ALU

    bf16 = mybir.dt.bfloat16
    with ExitStack() as ctx:
        m = Memory(nc, ctx, "wt")
        wT = m.sb("wT", [128, 2, 128])
        att = m.sb("att", [128, 4])
        attx = m.sb("attx", [128, 4, 128])
        blockmask = m.sb("blockmask", [128, 128])
        headsel = m.sb("headsel", [128, H])
        att8 = m.sb("att8", [128, H])
        basis = m.sb("basis", [128, R, 128])
        comp = m.sb("comp", [128, R * R])
        p_wT = m.ps("p_wT", [128, 2, 128])
        p_x = m.ps("p_x", [128, 3, 128])
        p_8 = m.ps("p_8", [128, H])
        rest = [m.sb(f"rest{k}", [1, F]) for k in range(3)]
        part = [[m.sb(f"part{n}{k}", [1, F], bf16) for k in range(3)] for n in range(2)]
        loaded, expanded, turned, turned_sb, folded, step, done, split, stored, spread = (m.sem(n) for n in (
            "loaded", "expanded", "turned", "turned_sb", "folded", "step", "done", "split", "stored", "spread"))
        block = ctx.enter_context(nc.Block())
        LOADS = 20 + J

        @block.sync
        def _(eng):
            def load(dst, src):
                eng.dma_start(dst, src).then_inc(loaded, 16)

            load(keep["ident"][:, :], inp["ident"])
            load(blockmask[:, :], inp["blockmask"])
            load(headsel[:, :], inp["headsel"])
            load(keep["expand"][:, :], inp["expand"])
            load(keep["pick"][:, :, :], inp["pick"])
            load(keep["ones3"][:, :], inp["ones3"])
            load(keep["rowpick"][:, :, :], inp["rowpick"])
            load(keep["w1"][:, :], inp["W1"])
            load(keep["w2"][:, :], inp["W2"])
            with nc.allow_non_contiguous_dma(reason="four columns of 128 numbers"):
                for n, name in enumerate(("al1", "ar1", "al2", "ar2")):
                    load(att[:, n:n + 1], inp[name].rearrange("h (d a) -> (h d) a", a=1))
            load(keep["wm"][:, :, :], inp["Wm"].rearrange("(l k) n -> k l n", l=2))
            load(keep["bmrow"][:, :], inp["bm"].rearrange("(a n) -> a n", a=1))
            load(keep["root"][:, :], inp["root"])
            load(keep["biasrow"][:, :], inp["bias"].rearrange("(a n) -> a n", a=1))
            load(basis[:, :, :], inp["basis"].rearrange("b k n -> k b n"))
            load(comp[:, :], inp["comp"].rearrange("r b -> (r b)").partition_broadcast(128))
            load(keep["ones"][:, :], inp["ones"])
            for j in range(J):
                load(keep["alpha4"][:, j, :], inp["alpha"].partition_broadcast(128))
            eng.wait_ge(split, 1)
            for n in range(2):
                for k in range(3):
                    eng.dma_start(tab["parts"][n, k:k + 1, :], part[n][k][:, :]).then_inc(stored, 16)
            eng.wait_ge(stored, 6 * 16)
            for n, name in enumerate(("bm3", "bias3")):
                for j in range(J):
                    eng.dma_start(keep[name][:, j, :], tab["parts"][n]).then_inc(spread, 16)
            eng.wait_ge(spread, 2 * J * 16)

        @block.tensor
        def _(eng):
            eng.wait_ge(loaded, 16 * LOADS)
            eng.transpose(p_wT[:, 0, :], keep["w1"][:, :], keep["ident"][:, :])
            eng.transpose(p_wT[:, 1, :], keep["w2"][:, :], keep["ident"][:, :]).then_inc(turned, 1)
            eng.wait_ge(turned_sb, 1)
            eng.wait_ge(expanded, 1)
            for n, layer in ((0, 0), (1, 0), (2, 1)):
                eng.matmul(p_x[:, n, :], wT[:, layer, :], attx[:, n, :], start=True, stop=True)
            eng.matmul(p_8[:, :], wT[:, 1, :], att8[:, :], start=True, stop=True).then_inc(folded, 1)

        @block.vector
        def _(eng):
            link = Link(eng, step, R * R + 11)
            link.begin(0)
            eng.wait_ge(loaded, 16 * LOADS)
            for n, row in enumerate((keep["bmrow"], keep["biasrow"])):
                link(eng.tensor_copy(rest[0][:, :], row[:, :]))
                for k in range(3):
                    if n == 1 and k == 2:
                        eng.tensor_copy(part[n][k][:, :], rest[k][:, :]).then_inc(split, 1)
                    else:
                        link(eng.tensor_copy(part[n][k][:, :], rest[k][:, :]))
                    if k < 2:
                        link(eng.tensor_tensor(rest[k + 1][:, :], rest[k][:, :], part[n][k][:, :], ALU.subtract))
            for n in range(3):
                eng.tensor_scalar(attx[:, n, :], blockmask[:, :], att[:, n:n + 1], None, ALU.mult)
            eng.tensor_scalar(att8[:, :], headsel[:, :], att[:, 3:4], None, ALU.mult).then_inc(expanded, 1)
            eng.wait_ge(turned, 1)
            eng.tensor_copy(wT[:, :, :], p_wT[:, :, :]).then_inc(turned_sb, 1)
            for b in range(R):
                for r in range(R):
                    w, c = keep["wrel"][:, r, :], comp[:, r * R + b:r * R + b + 1]
                    if b == 0:
                        link(eng.tensor_scalar(w, basis[:, b, :], c, None, ALU.mult))
                    else:
                        link(eng.scalar_tensor_tensor(w, basis[:, b, :], c, w, ALU.mult, ALU.add))
            link.end()
            eng.wait_ge(folded, 1)
            eng.tensor_copy(keep["wel1"][:, :], p_x[:, 0, :])
            eng.tensor_copy(keep["wer1"][:, :], p_x[:, 1, :])
            eng.tensor_copy(keep["wel2"][:, :], p_x[:, 2, :])
            eng.tensor_copy(keep["wer2"][:, :], p_8[:, :]).then_inc(done, 1)


def edge_rows_phase(nc, keep, inp, tab):
    from contextlib import ExitStack
    from concourse import mybir
    from concourse.alu_op_type import AluOpType as ALU

    i32, bf16 = mybir.dt.int32, mybir.dt.bfloat16
    FILL = N // NP
    with ExitStack() as ctx:
        m = Memory(nc, ctx, "er")
        cur, prev = m.sb("cur", [NB, BE], i32), m.sb("prev", [NB, BE], i32)
        same, cut = m.sb("same", [NB, BE]), m.sb("cut", [NB, BE], bf16)
        same16 = m.sb("same16", [NB, BE], bf16)
        w, part = [m.sb(f"w{k}", [NB, BE]) for k in range(3)], [m.sb(f"part{k}", [NB, BE], bf16) for k in range(3)]
        here, nxt = m.sb("here", [128, TILES], i32), m.sb("nxt", [128, TILES], i32)
        goes_on, end = m.sb("goes_on", [128, TILES]), m.sb("end", [128, TILES], i32)
        zero, no_edge = m.sb("zero", [1, F]), m.sb("no_edge", [128, FILL], i32)
        loaded, step, ready, stored = (m.sem(n) for n in ("loaded", "step", "ready", "stored"))
        block = ctx.enter_context(nc.Block())

        @block.sync
        def _(eng):
            row = lambda k: inp["dseg"][k:k + EP].rearrange("(b e) -> b e", e=BE)
            eng.dma_start(cur[:, :], row(1)).then_inc(loaded, 16)
            eng.dma_start(prev[:, :], row(0)).then_inc(loaded, 16)
            eng.dma_start(here[:, :], inp["here"]).then_inc(loaded, 16)
            eng.dma_start(nxt[:, :], inp["next"]).then_inc(loaded, 16)
            eng.dma_start(w[0][:, :], inp["w"].rearrange("(b e) -> b e", e=BE)).then_inc(loaded, 16)
            eng.wait_ge(ready, 4)
            rows = lambda t: t.rearrange("(b e) -> b e", e=BE)
            for k, t in enumerate((*part, cut)):
                eng.dma_start(rows(tab["rows"][k, :]), t[:, :]).then_inc(stored, 16)
            eng.dma_start(rows(tab["hot"][R, :]), same16[:, :]).then_inc(stored, 16)
            eng.dma_start(tab["end"][0:NB].rearrange("b p j -> p b j"),
                          end[:, :].rearrange("p (b j) -> p b j", j=J)).then_inc(stored, 16)
            eng.dma_start(tab["x1"][ZERO_ROW:ZERO_ROW + 1, :], zero[:, :]).then_inc(stored, 16)
            eng.dma_start(tab["delta"][ZERO_ROW:ZERO_ROW + 1, :], keep["bmrow"][:, :]).then_inc(stored, 16)
            eng.dma_start(tab["pos"].rearrange("(p n) a -> p (n a)", p=NP), no_edge[0:NP, :]).then_inc(stored, 16)
            eng.dma_start(tab["end"][NB, :, :], no_edge[:, 0:J]).then_inc(stored, 16)
            eng.dma_start(tab["at"][NB, :, :], no_edge[:, 0:J]).then_inc(stored, 16)
            eng.wait_ge(stored, 11 * 16)

        @block.vector
        def _(eng):
            link = Link(eng, step, 6)
            link.begin(0)
            eng.memset(zero[:, :], 0.0)
            eng.memset(no_edge[:, :], ZERO_ROW).then_inc(ready, 1)
            eng.wait_ge(loaded, 80)
            for k in range(3):
                if k == 2:
                    eng.tensor_copy(part[k][:, :], w[k][:, :]).then_inc(ready, 1)
                else:
                    link(eng.tensor_copy(part[k][:, :], w[k][:, :]))
                    link(eng.tensor_tensor(w[k + 1][:, :], w[k][:, :], part[k][:, :], ALU.subtract))
            link(eng.tensor_tensor(same[:, :], cur[:, :], prev[:, :], ALU.is_equal))
            eng.tensor_copy(same16[:, :], same[:, :])
            eng.tensor_scalar(cut[:, :], same[:, :], -CUT, CUT, ALU.mult, ALU.add).then_inc(ready, 1)
            link(eng.tensor_tensor(goes_on[:, :], here[:, :], nxt[:, :], ALU.is_equal))
            eng.scalar_tensor_tensor(end[:, :], goes_on[:, :], float(FAR), here[:, :],
                                     ALU.mult, ALU.add).then_inc(ready, 1)
            link.end()


def chunk_scan_phase(nc, keep, name, on, add, out, backward):
    from contextlib import ExitStack
    from concourse import mybir
    from concourse.alu_op_type import AluOpType as ALU

    P = H * C
    way = slice(None, None, -1) if backward else slice(None)
    last = 0 if backward else CL - 1
    with ExitStack() as ctx:
        m = Memory(nc, ctx, name)
        whole, col = m.sb("whole", [P, 1]), m.sb("col", [P, 1])
        whole_row, sum_row, carry_row = m.sb("whole_row", [1, P]), m.sb("sum_row", [1, P]), m.sb("carry_row", [1, P])
        p_rows, p_col = m.ps("p_rows", [1, 2, P]), m.ps("p_col", [P, 1])
        summed, rowed, carried, columned, step = (m.sem(n) for n in ("summed", "rowed", "carried", "columned", "step"))
        block = ctx.enter_context(nc.Block())

        @block.vector
        def _(eng):
            link = Link(eng, step, 5)
            link.begin(0)
            eng.tensor_tensor_scan(out[:, way], on[:, way], add[:, way], 0.0, ALU.mult, ALU.add)
            eng.tensor_reduce(whole[:, :], on, mybir.AxisListType.X, ALU.min).then_inc(summed, 1)
            eng.wait_ge(rowed, 1)
            link(eng.tensor_copy(whole_row[:, :], p_rows[:, 1, :]))
            link(eng.tensor_tensor_scan(sum_row[:, way], whole_row[:, way], p_rows[:, 0, way], 0.0,
                                        ALU.mult, ALU.add))
            link(eng.memset(carry_row[:, :], 0.0))
            rows = lambda t: t[:, :].rearrange("a (h c) -> a h c", c=C)
            if backward:
                to, frm = rows(carry_row)[:, :, 0:C - 1], rows(sum_row)[:, :, 1:C]
            else:
                to, frm = rows(carry_row)[:, :, 1:C], rows(sum_row)[:, :, 0:C - 1]
            eng.tensor_copy(to, frm).then_inc(carried, 1)
            eng.wait_ge(columned, 1)
            link(eng.tensor_copy(col[:, :], p_col[:, :]))
            link(eng.tensor_tensor_scan(out[:, way], on[:, way], add[:, way], col[:, 0:1], ALU.mult, ALU.add))
            link.end()

        @block.tensor
        def _(eng):
            eng.wait_ge(summed, 1)
            eng.matmul(p_rows[:, 0, :], out[:, last:last + 1], keep["ident"][0:P, 0:P], start=True, stop=True)
            eng.matmul(p_rows[:, 1, :], whole[:, :], keep["ident"][0:P, 0:P], start=True, stop=True).then_inc(rowed, 1)
            eng.wait_ge(carried, 1)
            eng.matmul(p_col[:, :], carry_row[:, :], keep["ones"][0:1, 0:1], start=True, stop=True).then_inc(columned, 1)


def chunked(t):
    return t.rearrange("(c e) -> c e", e=CL)


def counts_phases(nc, keep, inp, tab):
    from contextlib import ExitStack
    from concourse import mybir
    from concourse.alu_op_type import AluOpType as ALU

    i32, bf16 = mybir.dt.int32, mybir.dt.bfloat16
    P = R * C
    with ExitStack() as ctx:
        m = Memory(nc, ctx, "ct")
        kind, cur = m.sb("kind", [P, CL], i32), m.sb("cur", [P, CL], i32)
        before, after = m.sb("before", [P, CL]), m.sb("after", [P, CL])
        hot, hot16 = m.sb("hot", [P, CL]), m.sb("hot16", [P, CL], bf16)
        relcol, chunksel = m.sb("relcol", [P, 1]), m.sb("chunksel", [P, C])
        fwd, bwd = kind[:, :].bitcast(m.fp32), cur[:, :].bitcast(m.fp32)
        loaded, ready, made, stored = (m.sem(n) for n in ("loaded", "ready", "made", "stored"))
        with nc.Block() as block:
            @block.sync
            def _(eng):
                eng.dma_start(relcol[:, :], inp["relcol"]).then_inc(loaded, 16)
                eng.dma_start(chunksel[:, :], inp["chunksel"]).then_inc(loaded, 16)
                for r in range(R):
                    at = slice(r * C, r * C + C)
                    eng.dma_start(kind[at, :], chunked(inp["kind"])).then_inc(loaded, 16)
                    eng.dma_start(cur[at, :], chunked(inp["dseg"][1:EP + 1])).then_inc(loaded, 16)
                    eng.dma_start(before[at, :].bitcast(i32), chunked(inp["dseg"][0:EP])).then_inc(loaded, 16)
                    eng.dma_start(after[at, :].bitcast(i32), chunked(inp["dseg"][2:EP + 2])).then_inc(loaded, 16)
                eng.wait_ge(ready, 1)
                eng.dma_start(tab["hot"][0:R, :].rearrange("r (c e) -> (r c) e", e=CL), hot16[:, :]).then_inc(stored, 16)
                eng.wait_ge(stored, 16)

            @block.vector
            def _(eng):
                eng.wait_ge(loaded, 16 * (2 + 4 * R))
                eng.tensor_scalar(hot[:, :], kind[:, :], relcol[:, 0:1], None, ALU.is_equal).then_inc(made, 1)
                eng.wait_ge(made, 1)
                eng.tensor_copy(hot16[:, :], hot[:, :]).then_inc(ready, 1)
                eng.tensor_tensor(before[:, :], cur[:, :], before[:, :].bitcast(i32), ALU.is_equal)
                eng.tensor_tensor(after[:, :], cur[:, :], after[:, :].bitcast(i32), ALU.is_equal).then_inc(made, 1)
                eng.wait_ge(made, 2)
        chunk_scan_phase(nc, keep, "cf", before[:, :], hot[:, :], fwd, False)
        chunk_scan_phase(nc, keep, "cb", after[:, :], hot[:, :], bwd, True)
        p_cnt = m.ps("p_cnt", [128, CT, C])
        cnt = m.sb("cnt", [128, CT, C])
        link_sem, own, counted, done = (m.sem(n) for n in ("step", "own", "counted", "done"))
        with nc.Block() as block:
            @block.vector
            def _(eng):
                link = Link(eng, link_sem, 3)
                link.begin(0)
                link(eng.tensor_tensor(fwd, fwd, bwd, ALU.add))
                link(eng.tensor_tensor(fwd, fwd, hot[:, :], ALU.subtract))
                eng.tensor_tensor(fwd, fwd, hot[:, :], ALU.mult).then_inc(own, 1)
                eng.wait_ge(counted, 1)
                link(eng.tensor_scalar(cnt[:, :, :], p_cnt[:, :, :], 1.0, None, ALU.max))
                eng.reciprocal(keep["norm"][:, :].rearrange("p (c t) -> p t c", t=CT), cnt[:, :, :]).then_inc(done, 1)
                link.end()

            @block.tensor
            def _(eng):
                eng.wait_ge(own, 1)
                for t in range(CT):
                    last = eng.matmul(p_cnt[:, t, :], fwd[:, t * 128:(t + 1) * 128], chunksel[:, :],
                                      start=True, stop=True)
                last.then_inc(counted, 1)


def spread_phases(nc, keep, inp, tab):
    from contextlib import ExitStack
    from concourse import mybir
    from concourse.alu_op_type import AluOpType as ALU

    i32 = mybir.dt.int32
    P = H * C
    with ExitStack() as ctx:
        m = Memory(nc, ctx, "sp")
        cur, after = m.sb("cur", [P, CL], i32), m.sb("after", [P, CL])
        term, spread = m.sb("term", [P, CL]), m.sb("spread", [P, CL])
        loaded, step, stored = (m.sem(n) for n in ("loaded", "step", "stored"))
        rows = tab["er2"].rearrange("h (c e) -> (h c) e", e=CL)
        with nc.Block() as block:
            @block.sync
            def _(eng):
                eng.dma_start(term[:, :], rows).then_inc(loaded, 16)
                for h in range(H):
                    at = slice(h * C, h * C + C)
                    eng.dma_start(cur[at, :], chunked(inp["dseg"][1:EP + 1])).then_inc(loaded, 16)
                    eng.dma_start(after[at, :].bitcast(i32), chunked(inp["dseg"][2:EP + 2])).then_inc(loaded, 16)

            @block.vector
            def _(eng):
                link = Link(eng, step, 3)
                link.begin(0)
                eng.wait_ge(loaded, 16 * (1 + 2 * H))
                link(eng.tensor_tensor(after[:, :], cur[:, :], after[:, :].bitcast(i32), ALU.is_equal))
                link(eng.tensor_tensor(spread[:, :], term[:, :], after[:, :], ALU.mult))
                link(eng.tensor_tensor(term[:, :], term[:, :], spread[:, :], ALU.subtract))
                link.end()
        chunk_scan_phase(nc, keep, "sb", after[:, :], term[:, :], spread[:, :], True)
        with nc.Block() as block:
            @block.sync
            def _(eng):
                eng.dma_start(rows, spread[:, :]).then_inc(stored, 16)
                eng.wait_ge(stored, 16)


class Norm:

    def __init__(self, m, parts, groups):
        def two(name):
            return [m.sb(f"{name}{u}", [parts, groups]) for u in range(2)]

        self.raw = [m.sb(f"raw{u}", [parts, groups, 6]) for u in range(2)]
        self.total, self.apart, self.spread, self.var = two("total"), two("apart"), two("spread"), two("var")
        self.log, self.guess, self.square, self.part = two("log"), two("guess"), two("square"), two("part")
        self.scale, self.shift = two("scale"), two("shift")


def moments(eng, link, n, u):
    from concourse.alu_op_type import AluOpType as ALU

    raw = n.raw[u]
    eng.tensor_tensor(n.total[u][:, :], raw[:, :, 1], raw[:, :, 4], ALU.add)
    eng.tensor_tensor(n.spread[u][:, :], raw[:, :, 2], raw[:, :, 5], ALU.add)
    link(eng.tensor_tensor(n.apart[u][:, :], raw[:, :, 1], raw[:, :, 4], ALU.subtract))
    link(eng.tensor_tensor(n.square[u][:, :], n.apart[u][:, :], n.apart[u][:, :], ALU.mult))
    link(eng.scalar_tensor_tensor(n.apart[u][:, :], n.square[u][:, :], F / 4.0, n.spread[u][:, :],
                                  ALU.mult, ALU.add))
    return eng.tensor_scalar(n.var[u][:, :], n.apart[u][:, :], 1.0 / F, EPS, ALU.mult, ALU.add)


def scales(eng, link, n, u, factor=None):
    from concourse.alu_op_type import AluOpType as ALU

    g, s, v, t = n.guess[u][:, :], n.square[u][:, :], n.var[u][:, :], n.part[u][:, :]
    link(eng.tensor_tensor(s, g, g, ALU.mult))
    link(eng.scalar_tensor_tensor(t, v, -0.5, s, ALU.mult, ALU.mult))
    link(eng.scalar_tensor_tensor(n.scale[u][:, :], t, 1.5, g, ALU.add, ALU.mult))
    if factor is not None:
        half = n.scale[u][:, 0:J]
        link(eng.tensor_tensor(half, half, factor, ALU.mult))
    return eng.scalar_tensor_tensor(n.shift[u][:, :], n.total[u][:, :], -0.5, n.scale[u][:, :], ALU.mult, ALU.mult)


def nodes_phase(nc, keep, inp, out):
    from contextlib import ExitStack
    from concourse import mybir
    from concourse.alu_op_type import AluOpType as ALU

    ACT = mybir.ActivationFunctionType
    x_b = inp["x"].rearrange("(p b j) f -> p b j f", p=NP, j=JN)
    out_b = out.rearrange("(p b j) f -> p b j f", p=NP, j=JN)
    AHEAD = 2
    WAYS = 4
    with ExitStack() as ctx:
        m = Memory(nc, ctx, "nd")
        x, y = ([m.sb(f"{n}{s}", [NP, JN, F]) for s in range(WAYS)] for n in ("x", "y"))
        low, res = ([m.sb(f"{n}{u}", [NP, JN, F]) for u in range(2)] for n in ("low", "res"))
        hn, hT = m.sb("hn", [NP, JN, F]), m.sb("hT", [128, JN, NP])
        bm8, alpha8 = m.sb("bm8", [NP, JN, F]), m.sb("alpha8", [NP, JN, F])
        norm = Norm(m, NP, JN)
        p_hT = m.ps("p_hT", [128, JN, 128])
        p_o = [m.ps(f"p_o{u}", [NP, JN, F]) for u in range(2)]
        x_loaded, stored = [m.sem(f"x_loaded{s}") for s in range(WAYS)], m.slots("stored")
        (rows_loaded, y_ready, var_ready, log_ready, guess_ready, scale_ready, hn_ready, hT_ready, hT_copied,
         o_ready, low_ready, res_ready, pool_go, step_n, step_c, step_o) = (m.sem(n) for n in (
            "rows_loaded", "y_ready", "var_ready", "log_ready", "guess_ready", "scale_ready", "hn_ready", "hT_ready",
            "hT_copied", "o_ready", "low_ready", "res_ready", "pool_go", "step_n", "step_c", "step_o"))
        block = ctx.enter_context(nc.Block())

        @block.sync
        def _(eng):
            for u in range(2):
                eng.sem_inc(stored[u], 16)

            def load_x(b, s):
                eng.dma_start(x[s][:, :, :], x_b[:, b, :, :]).then_inc(x_loaded[s], 16)

            def step(b, s, on):
                if on(2):
                    eng.wait_ge(res_ready, b + 1)
                    eng.dma_start(out_b[:, b - 2, :, :], res[s % 2][:, :, :]).then_inc(stored[s % 2], 16)
                if on(-AHEAD - WAYS):
                    eng.wait_ge(y_ready, b + AHEAD + 1)
                    load_x(b + AHEAD + WAYS, (s + AHEAD) % WAYS)

            load_x(0, 0)
            load_x(1, 1)
            for j in range(JN):
                eng.dma_start(bm8[:, j, :], inp["bm"].partition_broadcast(NP)).then_inc(rows_loaded, 16)
                eng.dma_start(alpha8[:, j, :], inp["alpha"].partition_broadcast(NP)).then_inc(rows_loaded, 16)
            load_x(2, 2)
            load_x(3, 3)
            for b in range(AHEAD):
                eng.wait_ge(y_ready, b + 1)
                load_x(b + WAYS, b)
            steps(eng, NQ, 2, step, ahead=AHEAD + WAYS, ways=WAYS)
            for u in range(2):
                eng.wait_ge(stored[u], 8 * NQ + 16)

        @block.gpsimd
        def _(eng):
            eng.sem_inc(res_ready, 2)

            def add_bm(b, s):
                eng.wait_ge(x_loaded[s], nth(16, b, s, WAYS))
                eng.sem_inc(pool_go, 1)
                eng.tensor_tensor(y[s][:, :, :], x[s][:, :, :], bm8[:, :, :], ALU.add).then_inc(y_ready, 1)

            def step(b, s, on):
                if on(2):
                    eng.wait_ge(low_ready, b + 1)
                    eng.wait_ge(stored[s % 2], nth(16, b - 2, s % 2))
                    eng.sem_inc(pool_go, 1)
                    eng.tensor_tensor(res[s % 2][:, :, :], low[s % 2][:, :, :], y[(s + 2) % WAYS][:, :, :],
                                      ALU.add).then_inc(res_ready, 1)
                if on(-AHEAD):
                    eng.wait_ge(res_ready, b + 1 if on(2) else 2)
                    add_bm(b + AHEAD, (s + AHEAD) % WAYS)

            eng.wait_ge(rows_loaded, 2 * JN * 16)
            for b in range(AHEAD):
                add_bm(b, b)
            steps(eng, NQ, 2, step, ahead=AHEAD, ways=WAYS)

        @block.vector
        def _(eng):
            eng.sem_inc(low_ready, 2)
            ln, lc, lo = Link(eng, step_n, 4), Link(eng, step_c, 3), Link(eng, step_o, 1)

            def step(b, s, on):
                u = s % 2
                if on(0):
                    ln.begin(b)
                    eng.wait_ge(y_ready, b + 1)
                    for j in range(JN):
                        last = eng.bn_stats(norm.raw[u][:, j, :], y[s][:, j, :])
                    ln(last)
                    moments(eng, ln, norm, u).then_inc(var_ready, 1)
                    ln.end()
                if on(2):
                    lo.begin(b - 2)
                    eng.wait_ge(o_ready, b)
                    eng.wait_ge(res_ready, b - 1)
                    lo(eng.scalar_tensor_tensor(low[u][:, :, :], p_o[u][:, :, :], 0.0, alpha8[:, :, :],
                                                ALU.min, ALU.mult))
                    eng.scalar_tensor_tensor(low[u][:, :, :], p_o[u][:, :, :], 0.0, low[u][:, :, :],
                                             ALU.max, ALU.add).then_inc(low_ready, 1)
                    lo.end()
                if on(0):
                    lc.begin(b)
                    eng.wait_ge(guess_ready, b + 1)
                    scales(eng, lc, norm, u).then_inc(scale_ready, 1)
                    lc.end()

            eng.wait_ge(rows_loaded, 2 * JN * 16)
            steps(eng, NQ, 2, step, ways=WAYS)

        @block.scalar
        def _(eng):
            eng.preload_act_table_set(TABLE)

            def step(b, s, on):
                u = s % 2
                if on(0):
                    eng.wait_ge(var_ready, b + 1)
                    eng.activation(norm.log[u][:, :], norm.var[u][:, :], ACT.Ln).then_inc(log_ready, 1)
                    eng.wait_ge(log_ready, b + 1)
                    eng.activation(norm.guess[u][:, :], norm.log[u][:, :], ACT.Exp, scale=-0.5).then_inc(guess_ready, 1)
                if on(1):
                    eng.wait_ge(hT_ready, b)
                    eng.wait_ge(o_ready, b)
                    eng.activation(hT[:, :, :], p_hT[:, :, 0:NP], ACT.Copy).then_inc(hT_copied, 1)
                if on(0):
                    eng.wait_ge(scale_ready, b + 1)
                    for j in range(JN):
                        last = eng.activation(hn[:, j, :], y[s][:, j, :], ACT.Relu,
                                              bias=norm.shift[u][:, j:j + 1], scale=norm.scale[u][:, j:j + 1])
                    last.then_inc(hn_ready, 1)

            steps(eng, NQ, 1, step, ways=WAYS)

        @block.tensor
        def _(eng):
            eng.sem_inc(o_ready, 1)

            def step(b, u, on):
                v = 1 - u
                if on(1):
                    eng.wait_ge(hT_copied, b)
                    eng.wait_ge(low_ready, b)
                    for j in range(JN):
                        if j % 4 == 0:
                            eng.matmul(p_o[v][:, j:j + 4, :], keep["ones3"][:, 0:NP], keep["bias3"][:, :, :],
                                       start=True, stop=False)
                        last = eng.matmul(p_o[v][:, j, :], hT[:, j, :], keep["root"][:, :], start=False, stop=j % 4 == 3)
                    last.then_inc(o_ready, 1)
                if on(0):
                    eng.wait_ge(hn_ready, b + 1)
                    for j in range(JN):
                        last = eng.transpose(p_hT[:, j, 0:NP], hn[:, j, :], keep["ident"][0:NP, 0:NP])
                    last.then_inc(hT_ready, 1)

            steps(eng, NQ, 1, step)


def attention_logits(eng, link, z, slope, w, cut, t, u):
    from concourse.alu_op_type import AluOpType as ALU

    logit, before = t["logit"], t["before"]
    eng.tensor_copy(logit[u][:, 0:1], logit[1 - u][:, BE:BE + 1])
    link(eng.tensor_tensor(slope[:, :], z[:, :], slope[:, :], ALU.max))
    link(eng.tensor_tensor(logit[u][:, 1:BE + 1], w[:, :], slope[:, :], ALU.mult))
    link(eng.tensor_tensor_scan(before[u][:, :], logit[u][:, 0:BE], cut[:, :], before[1 - u][:, BE - 1:BE],
                                ALU.max, ALU.add))
    return eng.tensor_tensor(t["lead"][u][:, :], logit[u][:, 1:BE + 1], before[u][:, :], ALU.subtract)


def attention_exps(eng, t, u, sem, count):
    from concourse import mybir

    ACT = mybir.ActivationFunctionType
    eng.activation(t["under"][:, :], t["lead"][u][:, :], ACT.Relu, scale=-1.0)
    eng.activation(t["over"][:, :], t["lead"][u][:, :], ACT.Relu).then_inc(sem, 1)
    eng.wait_ge(sem, count)
    eng.activation(t["weight"][u][:, :], t["under"][:, :], ACT.Exp, scale=-1.0)
    return eng.activation(t["fade"][u][:, :], t["over"][:, :], ACT.Exp, scale=-1.0)


def attention_sums(eng, link, t, ft, u):
    from concourse.alu_op_type import AluOpType as ALU

    num, den = t["num"], t["den"]
    eng.tensor_tensor_scan(den[u][:, :], t["fade"][u][:, :], t["weight"][u][:, :], den[1 - u][:, BE - 1:BE],
                           ALU.mult, ALU.add)
    link(eng.tensor_tensor(t["message"][:, :], ft[:, :], t["weight"][u][:, :], ALU.mult))
    return eng.tensor_tensor_scan(num[u][:, :], t["fade"][u][:, :], t["message"][:, :], num[1 - u][:, BE - 1:BE],
                                  ALU.mult, ALU.add)


def attention_inverse(eng, t, u, sem, count):
    from concourse import mybir

    ACT = mybir.ActivationFunctionType
    eng.activation(t["log"][:, :], t["den"][u][:, :], ACT.Ln).then_inc(sem, 1)
    eng.wait_ge(sem, count)
    return eng.activation(t["near"][:, :], t["log"][:, :], ACT.Exp, scale=-1.0)


def attention_mean(eng, link, t, u, result):
    from concourse.alu_op_type import AluOpType as ALU

    link(eng.tensor_tensor(t["inverse"][:, :], t["den"][u][:, :], t["near"][:, :], ALU.mult))
    link(eng.scalar_tensor_tensor(t["inverse"][:, :], t["inverse"][:, :], 2.0, t["near"][:, :],
                                  ALU.subtract, ALU.mult, reverse0=True))
    return eng.scalar_tensor_tensor(result, t["num"][u][:, :], 0.0, t["inverse"][:, :], ALU.max, ALU.mult)


LOGIT_LINKS, SUM_LINKS, MEAN_LINKS = 3, 1, 2


def attention_tiles(m):
    def two(name, width=BE):
        return [m.sb(f"{name}{u}", [128, width]) for u in range(2)]

    t = {"logit": two("logit", BE + 1)}
    t.update({name: two(name) for name in ("before", "lead", "weight", "fade", "num", "den")})
    t.update({name: m.sb(name, [128, BE]) for name in ("under", "over", "message", "inverse", "log", "near")})
    return t


def start_attention(eng, t, sem):
    eng.memset(t["logit"][1][:, BE:BE + 1], CUT)
    eng.memset(t["before"][1][:, BE - 1:BE], CUT)
    eng.memset(t["num"][1][:, BE - 1:BE], 0.0)
    eng.memset(t["den"][1][:, BE - 1:BE], 0.0).then_inc(sem, 1)
    eng.wait_ge(sem, 1)


def edge_rows_of(table, b):
    import concourse.bass as bass

    return table[bass.ds(b * BE, BE), :].rearrange("(j p) f -> p j f", p=128)


def gat1_phase(nc, keep, inp, tab):
    from contextlib import ExitStack
    import concourse.bass as bass
    from concourse import mybir
    from concourse.alu_op_type import AluOpType as ALU

    ACT, i32, bf16 = mybir.ActivationFunctionType, mybir.dt.int32, mybir.dt.bfloat16
    with ExitStack() as ctx:
        m = Memory(nc, ctx, "g1")
        two = lambda n, s, dt=None: [m.sb(f"{n}{u}", s, dt) for u in range(2)]
        ids, ends = two("ids", [128, 3 * J], i32), two("ends", [128, J], i32)
        x = two("x", [128, 2 * J, F])
        rows = two("rows", [4, BE], bf16)
        h, hT = m.sb("h", [128, 2 * J, F]), m.sb("hT", [128, 2, BE])
        slope = two("slope", [128, BE])
        x1f, x1e, er2 = two("x1f", [128, BE]), two("x1e", [128, J, F]), two("er2", [H, BE])
        t, norm = attention_tiles(m), Norm(m, 128, 2 * J)
        p_t = [m.ps("p_t0", [128, BE]), m.ps("p_t1", [128, BE])]
        p_w, p_cut = m.ps("p_w", [128, BE]), m.ps("p_cut", [128, BE])
        p_z, p_ft = ([m.ps(f"{n}{u}", [128, BE]) for u in range(2)] for n in ("p_z", "p_ft"))
        names = ("ids_loaded", "rows_loaded", "gathered", "placed", "spilled", "stored", "f_stored", "var_ready", "log_ready",
                 "guess_ready", "scale_ready", "h_ready", "hT_ready", "hT_copied", "z_ready", "ft_ready", "cut_ready",
                 "slope_ready", "lead_ready", "relu_ready", "exp_ready", "sums_ready", "ln_ready", "near_ready", "x1_ready",
                 "x1_turned", "x1_copied", "start", "pool_go", "sync_go", "step_n", "step_c", "step_f", "step_s", "step_m")
        (ids_loaded, rows_loaded, gathered, placed, spilled, stored, f_stored, var_ready, log_ready, guess_ready,
         scale_ready, h_ready, hT_ready, hT_copied, z_ready, ft_ready, cut_ready, slope_ready, lead_ready, relu_ready,
         exp_ready, sums_ready, ln_ready, near_ready, x1_ready, x1_turned, x1_copied, start, pool_go, sync_go, step_n, step_c,
         step_f, step_s, step_m) = (m.slots(n) if n in DMA_SEMS else m.sem(n) for n in names)
        block = ctx.enter_context(nc.Block())

        @block.sync
        def _(eng):
            for u in range(2):
                eng.sem_inc(spilled[u], 32)
                eng.sem_inc(stored[u], 32)
                eng.sem_inc(f_stored[u], 16)

            def load_ids(b, u):
                eng.dma_start(ids[u][:, :], inp["ids"][b, :, :]).then_inc(ids_loaded[u], 16)
                eng.dma_start(ends[u][:, :], tab["end"][b, :, :]).then_inc(ids_loaded[u], 16)

            def load_rows(b, u):
                at = bass.ds(b * BE, BE)
                eng.dma_start(rows[u][:, :], tab["rows"][:, at]).then_inc(rows_loaded[u], 16)

            def step(b, u, on):
                v = 1 - u
                if on(0):
                    eng.wait_ge(gathered[u], nth(128, b, u))
                    eng.dma_start(tab["xs"][b, :, :], x[u][:, 0:J, :].rearrange("p j f -> p (j f)")).then_inc(spilled[u], 16)
                    eng.dma_start(tab["xd"][b, :, :], x[u][:, J:, :].rearrange("p j f -> p (j f)")).then_inc(spilled[u], 16)
                    if on(-1):
                        eng.wait_ge(cut_ready, b + 1)
                        eng.sem_inc(sync_go, 1)
                        load_rows(b + 1, v)
                        eng.wait_ge(placed[u], nth(64, b, u))
                        load_ids(b + 2, u)
                if on(3):
                    eng.wait_ge(x1_ready, b - 1)
                    eng.dma_start(tab["x1f"][b - 3, :, :], x1f[v][:, :]).then_inc(f_stored[v], 16)
                    eng.wait_ge(x1_copied, b - 2)
                    eng.dma_start(edge_rows_of(tab["x1"], b - 3), x1e[v][:, :, :]).then_inc(stored[v], 16)
                    eng.dma_start(tab["er2"][:, bass.ds((b - 3) * BE, BE)], er2[v][:, :]).then_inc(stored[v], 16)

            load_ids(0, 0)
            load_ids(1, 1)
            load_rows(0, 0)
            steps(eng, NB, 3, step, ahead=2)
            for u in range(2):
                eng.wait_ge(spilled[u], 16 * NB + 32)
                eng.wait_ge(stored[u], 16 * NB + 32)
                eng.wait_ge(f_stored[u], 8 * NB + 16)
            eng.wait_ge(ids_loaded[0], 16 * NB + 32)

        @block.gpsimd
        def _(eng):
            def body(b, u):
                eng.wait_ge(ids_loaded[u], nth(32, b, u))
                eng.wait_ge(h_ready, b + 1)
                eng.wait_ge(spilled[u], nth(32, b, u))
                eng.sem_inc(pool_go, 1)
                for j in range(J):
                    for k in (0, 1):
                        eng.indirect_dma_start(
                            x[u][:, k * J + j, :], None, inp["x"][:, :],
                            bass.IndirectOffsetOnAxis(ap=ids[u][:, k * J + j:k * J + j + 1], axis=0)).then_inc(gathered[u], 16)
                for j in range(J):
                    eng.indirect_dma_start(
                        tab["pos"][:, :], bass.IndirectOffsetOnAxis(ap=ends[u][:, j:j + 1], axis=0),
                        ids[u][:, 2 * J + j:2 * J + j + 1], None,
                        bounds_check=N - 1, oob_is_err=False).then_inc(placed[u], 16)

            blocks(eng, NB, body)
            for u in range(2):
                eng.wait_ge(placed[u], 32 * NB)

        @block.vector
        def _(eng):
            ln, lc = Link(eng, step_n, 4), Link(eng, step_c, 3)
            lf, ls, lm = Link(eng, step_f, LOGIT_LINKS), Link(eng, step_s, SUM_LINKS), Link(eng, step_m, MEAN_LINKS)
            eng.sem_inc(lead_ready, 2)
            eng.sem_inc(sums_ready, 2)
            eng.sem_inc(x1_ready, 1)
            start_attention(eng, t, start)

            def step(b, u, on):
                v = 1 - u
                if on(0):
                    ln.begin(b)
                    eng.wait_ge(gathered[u], nth(128, b, u))
                    for g in range(2 * J):
                        last = eng.bn_stats(norm.raw[u][:, g, :], x[u][:, g, :])
                    ln(last)
                    moments(eng, ln, norm, u).then_inc(var_ready, 1)
                    ln.end()
                if on(3):
                    lm.begin(b - 3)
                    eng.wait_ge(near_ready, b - 2)
                    eng.wait_ge(f_stored[v], nth(16, b - 3, v))
                    attention_mean(eng, lm, t, v, x1f[v][:, :]).then_inc(x1_ready, 1)
                    lm.end()
                if on(0):
                    lc.begin(b)
                    eng.wait_ge(guess_ready, b + 1)
                    scales(eng, lc, norm, u).then_inc(scale_ready, 1)
                    lc.end()
                if on(2):
                    ls.begin(b - 2)
                    eng.wait_ge(exp_ready, b - 1)
                    eng.wait_ge(ft_ready, b - 1)
                    attention_sums(eng, ls, t, p_ft[u], u).then_inc(sums_ready, 1)
                    ls.end()
                if on(1):
                    lf.begin(b - 1)
                    eng.wait_ge(slope_ready, b)
                    eng.wait_ge(cut_ready, b + 1)
                    attention_logits(eng, lf, p_z[v], slope[v], p_w, p_cut, t, v).then_inc(lead_ready, 1)
                    lf.end()

            steps(eng, NB, 3, step)

        @block.scalar
        def _(eng):
            eng.preload_act_table_set(TABLE)
            eng.sem_inc(h_ready, 2)

            def step(b, u, on):
                v = 1 - u
                if on(2):
                    eng.wait_ge(lead_ready, b + 1)
                    attention_exps(eng, t, u, relu_ready, b - 1).then_inc(exp_ready, 1)
                if on(0):
                    eng.wait_ge(var_ready, b + 1)
                    eng.activation(norm.log[u][:, :], norm.var[u][:, :], ACT.Ln).then_inc(log_ready, 1)
                    eng.wait_ge(log_ready, b + 1)
                    eng.activation(norm.guess[u][:, :], norm.log[u][:, :], ACT.Exp, scale=-0.5).then_inc(guess_ready, 1)
                if on(1):
                    eng.wait_ge(z_ready, b)
                    eng.activation(slope[v][:, :], p_z[v][:, :], ACT.Copy, scale=SLOPE).then_inc(slope_ready, 1)
                if on(0):
                    eng.wait_ge(scale_ready, b + 1)
                    for g in range(2 * J):
                        last = eng.activation(h[:, g, :], x[u][:, g, :], ACT.Relu,
                                              bias=norm.shift[u][:, g:g + 1], scale=norm.scale[u][:, g:g + 1])
                    last.then_inc(h_ready, 1)
                if on(3):
                    eng.wait_ge(x1_turned, b - 2)
                    eng.wait_ge(stored[v], nth(32, b - 3, v))
                    eng.activation(x1e[v][:, :, :].rearrange("p j f -> p (j f)"), p_t[0][:, :], ACT.Copy)
                    eng.activation(er2[v][:, :], p_t[1][0:H, :], ACT.Copy).then_inc(x1_copied, 1)
                if on(2):
                    eng.wait_ge(sums_ready, b + 1)
                    eng.wait_ge(x1_ready, b - 1)
                    attention_inverse(eng, t, u, ln_ready, b - 1).then_inc(near_ready, 1)
                if on(0):
                    eng.wait_ge(hT_ready, b + 1)
                    eng.activation(hT[:, 0, :], p_t[0][:, :], ACT.Copy)
                    eng.activation(hT[:, 1, :], p_t[1][:, :], ACT.Copy).then_inc(hT_copied, 1)

            steps(eng, NB, 3, step)

        @block.tensor
        def _(eng):
            eng.sem_inc(cut_ready, 1)

            def step(b, u, on):
                v = 1 - u
                if on(3):
                    eng.wait_ge(x1_ready, b - 1)
                    for j in range(J):
                        at = slice(j * 128, j * 128 + 128)
                        eng.transpose(p_t[0][:, at], x1f[v][:, at], keep["ident"][:, :])
                    eng.matmul(p_t[1][0:H, :], keep["wer2"][:, :], x1f[v][:, :], start=True, stop=True).then_inc(x1_turned, 1)
                if on(3):
                    eng.wait_ge(x1_copied, b - 2)
                if on(0):
                    eng.wait_ge(h_ready, b + 3)
                    for g in range(2 * J):
                        at = slice(g % J * 128, g % J * 128 + 128)
                        last = eng.transpose(p_t[g // J][:, at], h[:, g, :], keep["ident"][:, :])
                    last.then_inc(hT_ready, 1)
                    eng.wait_ge(lead_ready, b + 1)
                    eng.wait_ge(hT_copied, b + 1)
                    eng.matmul(p_z[u][:, :], keep["wel1"][:, :], hT[:, 0, :], start=True, stop=False)
                    eng.matmul(p_z[u][:, :], keep["wer1"][:, :], hT[:, 1, :], start=False, stop=True).then_inc(z_ready, 1)
                    eng.wait_ge(sums_ready, b + 1)
                    eng.matmul(p_ft[u][:, :], keep["w1"][:, :], hT[:, 0, :], start=True, stop=True).then_inc(ft_ready, 1)
                    eng.wait_ge(lead_ready, b + 2)
                    eng.wait_ge(rows_loaded[u], nth(16, b, u))
                    eng.matmul(p_w[:, :], keep["rowpick"][:, 0, :], rows[u][:, :], start=True, stop=True)
                    eng.matmul(p_cut[:, :], keep["rowpick"][:, 1, :], rows[u][:, :], start=True, stop=True).then_inc(cut_ready, 1)

            steps(eng, NB, 3, step)


def gat2_phase(nc, keep, inp, tab):
    from contextlib import ExitStack
    import concourse.bass as bass
    from concourse import mybir

    ACT, i32, bf16 = mybir.ActivationFunctionType, mybir.dt.int32, mybir.dt.bfloat16
    with ExitStack() as ctx:
        m = Memory(nc, ctx, "g2")
        two = lambda n, s, dt=None: [m.sb(f"{n}{u}", s, dt) for u in range(2)]
        ids, at_edge = two("ids", [128, 3 * J], i32), two("at_edge", [128, J], i32)
        x, x1f, x2f = two("x", [128, J, F]), two("x1f", [128, BE]), two("x2f", [128, BE])
        rows, er2 = two("rows", [4, BE], bf16), two("er2", [H, BE])
        hT, slope = m.sb("hT", [128, BE]), two("slope", [128, BE])
        delta = two("delta", [128, J, F])
        t = attention_tiles(m)
        p_hT, p_w, p_cut, p_delta = (m.ps(n, [128, BE]) for n in ("p_hT", "p_w", "p_cut", "p_delta"))
        p_z, p_ft = ([m.ps(f"{n}{u}", [128, BE]) for u in range(2)] for n in ("p_z", "p_ft"))
        names = ("ids_loaded", "rows_loaded", "x1f_loaded", "found", "found_stored", "gathered", "stored", "hT_ready",
                 "hT_copied", "z_ready", "cut_ready", "ft_ready", "slope_ready", "lead_ready", "relu_ready",
                 "exp_ready", "sums_ready", "log_ready", "near_ready", "x2_ready", "delta_ready", "delta_copied",
                 "start", "pool_go", "step_f", "step_s", "step_m")
        (ids_loaded, rows_loaded, x1f_loaded, found, found_stored, gathered, stored, hT_ready, hT_copied, z_ready,
         cut_ready, ft_ready, slope_ready, lead_ready, relu_ready, exp_ready, sums_ready, log_ready, near_ready,
         x2_ready, delta_ready, delta_copied, start, pool_go, step_f, step_s, step_m) = (
            m.slots(n) if n in DMA_SEMS else m.sem(n) for n in names)
        block = ctx.enter_context(nc.Block())

        @block.sync
        def _(eng):
            for u in range(2):
                eng.sem_inc(found_stored[u], 16)
                eng.sem_inc(stored[u], 16)

            def load_ids(b, u):
                eng.dma_start(ids[u][:, :], inp["ids"][b, :, :]).then_inc(ids_loaded[u], 16)

            def load_rows(b, u):
                at = bass.ds(b * BE, BE)
                eng.dma_start(rows[u][:, :], tab["rows"][:, at]).then_inc(rows_loaded[u], 16)
                eng.dma_start(er2[u][:, :], tab["er2"][:, at]).then_inc(rows_loaded[u], 16)

            def step(b, u, on):
                v = 1 - u
                if on(0):
                    eng.wait_ge(found[u], nth(64, b, u))
                    eng.dma_start(tab["at"][b, :, :], at_edge[u][:, :]).then_inc(found_stored[u], 16)
                    if on(-1):
                        load_ids(b + 2, u)
                        eng.wait_ge(cut_ready, b + 1)
                        load_rows(b + 1, v)
                if on(3):
                    eng.wait_ge(delta_ready, b - 2)
                    eng.dma_start(x1f[v][:, :], tab["x1f"][b - 3, :, :]).then_inc(x1f_loaded[v], 16)
                if on(4):
                    eng.wait_ge(delta_copied, b - 2)
                    eng.dma_start(edge_rows_of(tab["delta"], b - 4), delta[u][:, :, :]).then_inc(stored[u], 16)

            load_ids(0, 0)
            load_ids(1, 1)
            load_rows(0, 0)
            steps(eng, NB, 4, step, ahead=2)
            for u in range(2):
                eng.wait_ge(found_stored[u], 8 * NB + 16)
                eng.wait_ge(stored[u], 8 * NB + 16)
            eng.wait_ge(ids_loaded[0], 8 * NB + 16)

        @block.gpsimd
        def _(eng):
            def positions(b, u, first):
                eng.wait_ge(ids_loaded[u], nth(16, b, u))
                eng.wait_ge(found_stored[u], nth(16, b, u))
                if not first:
                    eng.wait_ge(gathered[u], nth(64, b, u) - 64)
                eng.sem_inc(pool_go, 1)
                for j in range(J):
                    eng.indirect_dma_start(
                        at_edge[u][:, j:j + 1], None, tab["pos"][:, :],
                        bass.IndirectOffsetOnAxis(ap=ids[u][:, j:j + 1], axis=0)).then_inc(found[u], 16)

            def rows_of_x1(b, u):
                eng.wait_ge(found[u], nth(64, b, u))
                eng.wait_ge(hT_ready, b + 1)
                eng.sem_inc(pool_go, 1)
                for j in range(J):
                    eng.indirect_dma_start(
                        x[u][:, j, :], None, tab["x1"][:, :],
                        bass.IndirectOffsetOnAxis(ap=at_edge[u][:, j:j + 1], axis=0)).then_inc(gathered[u], 16)

            def pair(b, first):
                for u in range(2):
                    positions(b + u, u, first)
                for u in range(2):
                    rows_of_x1(b + u, u)

            pair(0, True)
            with eng.Fori(1, NB // 2) as i:
                pair(i * 2, False)

        @block.vector
        def _(eng):
            lf, ls, lm = Link(eng, step_f, LOGIT_LINKS), Link(eng, step_s, SUM_LINKS), Link(eng, step_m, MEAN_LINKS)
            eng.sem_inc(lead_ready, 2)
            eng.sem_inc(sums_ready, 2)
            eng.sem_inc(x2_ready, 1)
            start_attention(eng, t, start)

            def step(b, u, on):
                v = 1 - u
                if on(3):
                    lm.begin(b - 3)
                    eng.wait_ge(near_ready, b - 2)
                    attention_mean(eng, lm, t, v, x2f[v][:, :]).then_inc(x2_ready, 1)
                    lm.end()
                if on(2):
                    ls.begin(b - 2)
                    eng.wait_ge(exp_ready, b - 1)
                    eng.wait_ge(ft_ready, b - 1)
                    attention_sums(eng, ls, t, p_ft[u], u).then_inc(sums_ready, 1)
                    ls.end()
                if on(1):
                    lf.begin(b - 1)
                    eng.wait_ge(slope_ready, b)
                    eng.wait_ge(cut_ready, b + 1)
                    attention_logits(eng, lf, p_z[v], slope[v], p_w, p_cut, t, v).then_inc(lead_ready, 1)
                    lf.end()

            steps(eng, NB, 3, step)

        @block.scalar
        def _(eng):
            eng.preload_act_table_set(TABLE)
            eng.sem_inc(delta_copied, 1)

            def step(b, u, on):
                v = 1 - u
                if on(2):
                    eng.wait_ge(lead_ready, b + 1)
                    attention_exps(eng, t, u, relu_ready, b - 1).then_inc(exp_ready, 1)
                if on(1):
                    eng.wait_ge(z_ready, b)
                    eng.activation(slope[v][:, :], p_z[v][:, :], ACT.Copy, scale=SLOPE).then_inc(slope_ready, 1)
                if on(0):
                    eng.wait_ge(hT_ready, b + 3)
                    eng.activation(hT[:, :], p_hT[:, :], ACT.Copy).then_inc(hT_copied, 1)
                if on(4):
                    eng.wait_ge(delta_ready, b - 1)
                    eng.wait_ge(stored[u], nth(16, b - 4, u))
                    eng.activation(delta[u][:, :, :].rearrange("p j f -> p (j f)"), p_delta[:, :],
                                   ACT.Copy).then_inc(delta_copied, 1)
                if on(2):
                    eng.wait_ge(sums_ready, b + 1)
                    eng.wait_ge(x2_ready, b - 1)
                    attention_inverse(eng, t, u, log_ready, b - 1).then_inc(near_ready, 1)

            steps(eng, NB, 4, step)

        @block.tensor
        def _(eng):
            eng.sem_inc(hT_ready, 2)
            eng.sem_inc(delta_ready, 2)
            eng.sem_inc(cut_ready, 1)

            def step(b, u, on):
                v = 1 - u
                if on(0):
                    eng.wait_ge(gathered[u], nth(64, b, u))
                    for j in range(J):
                        last = eng.transpose(p_hT[:, j * 128:(j + 1) * 128], x[u][:, j, :], keep["ident"][:, :])
                    last.then_inc(hT_ready, 1)
                if on(4):
                    eng.wait_ge(x1f_loaded[u], nth(16, b - 4, u))
                    eng.wait_ge(x2_ready, b - 2)
                    eng.wait_ge(delta_copied, b - 3)
                    eng.matmul(p_delta[:, :], keep["ones3"][:, :], keep["bm3"][:, :, :], start=True, stop=False)
                    for j in range(J):
                        at = slice(j * 128, j * 128 + 128)
                        eng.matmul(p_delta[:, at], x1f[u][:, at], keep["wm"][:, 0, :], start=False, stop=False)
                        last = eng.matmul(p_delta[:, at], x2f[u][:, at], keep["wm"][:, 1, :], start=False, stop=j == J - 1)
                    last.then_inc(delta_ready, 1)
                if on(0):
                    eng.wait_ge(lead_ready, b + 1)
                    eng.wait_ge(rows_loaded[u], nth(32, b, u))
                    eng.matmul(p_z[u][:, :], keep["expand"][:, :], er2[u][:, :], start=True, stop=False)
                    eng.wait_ge(hT_copied, b + 1)
                    eng.matmul(p_z[u][:, :], keep["wel2"][:, :], hT[:, :], start=False, stop=True).then_inc(z_ready, 1)
                    eng.wait_ge(sums_ready, b + 1)
                    eng.matmul(p_ft[u][:, :], keep["w2"][:, :], hT[:, :], start=True, stop=True).then_inc(ft_ready, 1)
                    eng.wait_ge(lead_ready, b + 2)
                    eng.matmul(p_w[:, :], keep["rowpick"][:, 0, :], rows[u][:, :], start=True, stop=True)
                    eng.matmul(p_cut[:, :], keep["rowpick"][:, 1, :], rows[u][:, :], start=True, stop=True).then_inc(cut_ready, 1)

            steps(eng, NB, 4, step)


def rgcn_phase(nc, keep, inp, tab, out):
    from contextlib import ExitStack
    import concourse.bass as bass
    from concourse import mybir
    from concourse.alu_op_type import AluOpType as ALU

    ACT, i32, bf16 = mybir.ActivationFunctionType, mybir.dt.int32, mybir.dt.bfloat16
    with ExitStack() as ctx:
        m = Memory(nc, ctx, "rg")
        two = lambda n, s, dt=None: [m.sb(f"{n}{u}", s, dt) for u in range(2)]
        at_edge, ends = two("at_edge", [128, J], i32), two("ends", [128, J], i32)
        x, own, far = two("x", [128, 2 * J, F]), two("own", [128, J, F]), two("far", [128, J, F])
        y = two("y", [128, 2 * J, F])
        y_own = two("y_own", [128, J, F])
        hot = two("hot", [R + 1, BE], bf16)
        h, hT = m.sb("h", [128, 2 * J, F]), two("hT", [128, 2, BE])
        of_rel = m.sb("of_rel", [128, R, BE])
        message, agg = m.sb("message", [128, BE]), two("agg", [128, BE])
        low, res = m.sb("low", [128, J, F]), two("res", [128, J, F])
        norm = Norm(m, 128, 2 * J)
        p_hT = [m.ps("p_hs", [128, BE]), m.ps("p_hd", [128, BE])]
        p_mask = [m.ps(f"p_mask{k}", [128, BE]) for k in range(3)]
        p_msg, p_same, p_o = m.ps("p_msg", [128, BE]), m.ps("p_same", [128, BE]), m.ps("p_o", [128, J, F])
        names = ("at_loaded", "ends_loaded", "x_loaded", "rows_loaded", "gathered", "scattered", "y_ready",
                 "var_ready", "log_ready", "guess_ready", "scale_ready", "h_ready", "hT_ready", "hT_copied",
                 "mask_ready", "of_rel_ready", "msg_ready", "same_ready", "msg_copied", "agg_ready", "o_ready", "res_ready",
                 "rows_left", "y_kept", "sync_go", "pool_go", "start", "step_n", "step_s", "step_o")
        (at_loaded, ends_loaded, x_loaded, rows_loaded, gathered, scattered, y_ready, var_ready, log_ready,
         guess_ready, scale_ready, h_ready, hT_ready, hT_copied, mask_ready, of_rel_ready, msg_ready, same_ready,
         msg_copied, agg_ready, o_ready, res_ready, rows_left, y_kept, sync_go, pool_go, start, step_n, step_s, step_o) = (m.slots(n) if n in DMA_SEMS else m.sem(n) for n in names)
        block = ctx.enter_context(nc.Block())

        @block.sync
        def _(eng):
            def load_at(b, u):
                eng.dma_start(at_edge[u][:, :], tab["at"][b, :, :]).then_inc(at_loaded[u], 16)

            def load_x(b, u):
                eng.dma_start(x[u][:, 0:J, :].rearrange("p j f -> p (j f)"), tab["xs"][b, :, :]).then_inc(x_loaded[u], 16)
                eng.dma_start(x[u][:, J:, :].rearrange("p j f -> p (j f)"), tab["xd"][b, :, :]).then_inc(x_loaded[u], 16)
                eng.dma_start(own[u][:, :, :], edge_rows_of(tab["delta"], b)).then_inc(x_loaded[u], 16)

            def step(b, u, on):
                v = 1 - u
                if on(-1) and on(0):
                    eng.wait_ge(y_ready, b + 1)
                    load_x(b + 1, v)
                    eng.wait_ge(gathered[u], nth(64, b, u))
                    load_at(b + 2, u)
                if on(1):
                    eng.wait_ge(msg_ready, b)
                    eng.dma_start(hot[v][:, :], tab["hot"][:, bass.ds((b - 1) * BE, BE)]).then_inc(rows_loaded[v], 16)
                if on(2):
                    eng.wait_ge(rows_left, b - 1)
                    eng.sem_inc(sync_go, 1)
                    eng.dma_start(ends[u][:, :], tab["end"][b - 2, :, :]).then_inc(ends_loaded[u], 16)
                if on(1):
                    eng.wait_ge(y_ready, b + 1)
                    eng.wait_ge(res_ready, b)
                    eng.dma_start(y_own[v][:, :, :], y[v][:, J:, :]).then_inc(y_kept[v], 16)

            load_at(0, 0)
            load_at(1, 1)
            load_x(0, 0)
            steps(eng, NB, 2, step, ahead=2)
            eng.wait_ge(at_loaded[0], 8 * NB + 16)

        @block.gpsimd
        def _(eng):
            eng.sem_inc(rows_left, 2)

            def gather(b, u):
                eng.wait_ge(at_loaded[u], nth(16, b, u))
                if not (isinstance(b, int) and b == 0):
                    eng.wait_ge(y_ready, b)
                eng.sem_inc(pool_go, 1)
                for j in range(J):
                    eng.indirect_dma_start(
                        far[u][:, j, :], None, tab["delta"][:, :],
                        bass.IndirectOffsetOnAxis(ap=at_edge[u][:, j:j + 1], axis=0)).then_inc(gathered[u], 16)

            def step(b, u, on):
                v = 1 - u
                if on(-1) and on(0):
                    gather(b + 1, v)
                if on(3):
                    eng.wait_ge(ends_loaded[v], nth(16, b - 3, v))
                    eng.wait_ge(res_ready, b)
                    eng.sem_inc(pool_go, 1)
                    for j in range(J):
                        eng.indirect_dma_start(
                            out[:, :], bass.IndirectOffsetOnAxis(ap=ends[v][:, j:j + 1], axis=0),
                            res[v][:, j, :], None, bounds_check=N - 1, oob_is_err=False).then_inc(scattered[v], 16)
                    eng.wait_ge(scattered[v], nth(64, b - 3, v))
                    eng.sem_inc(rows_left, 1)

            eng.wait_ge(start, 1)
            gather(0, 0)
            steps(eng, NB, 3, step, ahead=2)

        @block.vector
        def _(eng):
            ln, ls, lo = Link(eng, step_n, 4), Link(eng, step_s, 4), Link(eng, step_o, 2)
            eng.sem_inc(y_ready, 1)
            eng.sem_inc(res_ready, 2)
            eng.memset(agg[1][:, BE - 1:BE], 0.0).then_inc(start, 1)
            eng.wait_ge(start, 1)

            def out_rows(k, v):
                if k == 0:
                    eng.wait_ge(o_ready, lo.block + 1)
                    lo(eng.scalar_tensor_tensor(low[:, :, :], p_o[:, :, :], 0.0, keep["alpha4"][:, :, :],
                                                ALU.min, ALU.mult))
                elif k == 1:
                    lo(eng.scalar_tensor_tensor(low[:, :, :], p_o[:, :, :], 0.0, low[:, :, :], ALU.max, ALU.add))
                else:
                    eng.wait_ge(rows_left, lo.block + 1)
                    eng.tensor_tensor(res[v][:, :, :], low[:, :, :], y_own[v][:, :, :], ALU.add).then_inc(res_ready, 1)
                    lo.end()

            def step(b, u, on):
                v = 1 - u
                if on(2):
                    eng.wait_ge(hT_copied, b - 1)
                    eng.wait_ge(y_kept[u], nth(16, b - 2, u))
                if on(0):
                    ln.begin(b)
                    eng.wait_ge(x_loaded[u], nth(48, b, u))
                    eng.wait_ge(gathered[u], nth(64, b, u))
                    eng.tensor_tensor(y[u][:, J:, :], x[u][:, J:, :], own[u][:, :, :], ALU.add)
                    eng.tensor_tensor(y[u][:, 0:J, :], x[u][:, 0:J, :], far[u][:, :, :], ALU.add).then_inc(y_ready, 1)
                    eng.wait_ge(y_ready, b + 2)
                if on(3):
                    lo.begin(b - 3)
                    eng.wait_ge(y_kept[v], nth(16, b - 3, v))
                for r in range(R):
                    if on(2):
                        eng.wait_ge(mask_ready, (b - 2) * R + (r + 1))
                        eng.tensor_tensor(of_rel[:, r, :], p_mask[r % 3][:, :], hT[u][:, 0, :], ALU.mult).then_inc(of_rel_ready, 1)
                    if on(0):
                        last = eng.bn_stats(norm.raw[u][:, r, :], y[u][:, r, :])
                    if on(3) and r in (2, 4, 6):
                        out_rows(r // 2 - 1, v)
                if on(0):
                    ln(last)
                    moments(eng, ln, norm, u).then_inc(var_ready, 1)
                    ln.end()
                if on(2):
                    eng.wait_ge(msg_copied, b - 1)
                    eng.wait_ge(same_ready, b - 1)
                    eng.tensor_tensor_scan(agg[u][:, :], p_same[:, :], message[:, :], agg[v][:, BE - 1:BE],
                                           ALU.mult, ALU.add).then_inc(agg_ready, 1)
                if on(0):
                    ls.begin(b)
                    eng.wait_ge(guess_ready, b + 1)
                    scales(eng, ls, norm, u, keep["norm"][:, bass.ds(b * J, J)]).then_inc(scale_ready, 1)
                    ls.end()

            steps(eng, NB, 3, step)

        @block.scalar
        def _(eng):
            eng.preload_act_table_set(TABLE)

            def step(b, u, on):
                v = 1 - u
                if on(1):
                    eng.wait_ge(scale_ready, b)
                    for g in range(2 * J):
                        last = eng.activation(h[:, g, :], y[v][:, g, :], ACT.Relu,
                                              bias=norm.shift[v][:, g:g + 1], scale=norm.scale[v][:, g:g + 1])
                    last.then_inc(h_ready, 1)
                    eng.wait_ge(hT_ready, b)
                    eng.activation(hT[v][:, 0, :], p_hT[0][:, :], ACT.Copy)
                    eng.activation(hT[v][:, 1, :], p_hT[1][:, :], ACT.Copy).then_inc(hT_copied, 1)
                if on(0):
                    eng.wait_ge(var_ready, b + 1)
                    eng.activation(norm.log[u][:, :], norm.var[u][:, :], ACT.Ln).then_inc(log_ready, 1)
                    eng.wait_ge(log_ready, b + 1)
                    eng.activation(norm.guess[u][:, :], norm.log[u][:, :], ACT.Exp, scale=-0.5).then_inc(guess_ready, 1)
                if on(2):
                    eng.wait_ge(msg_ready, b + 1)
                    eng.activation(message[:, :], p_msg[:, :], ACT.Copy).then_inc(msg_copied, 1)

            steps(eng, NB, 2, step)

        @block.tensor
        def _(eng):
            eng.sem_inc(msg_ready, 2)

            def step(b, u, on):
                v = 1 - u

                def mask(r):
                    eng.matmul(p_mask[r % 3][:, :], keep["pick"][:, r, :], hot[u][:, :],
                               start=True, stop=True).then_inc(mask_ready, 1)

                def turn():
                    eng.wait_ge(h_ready, b)
                    for g in range(2 * J):
                        at = slice(g % J * 128, g % J * 128 + 128)
                        last = eng.transpose(p_hT[g // J][:, at], h[:, g, :], keep["ident"][:, :])
                    last.then_inc(hT_ready, 1)

                if on(2):
                    eng.wait_ge(rows_loaded[u], nth(16, b - 2, u))
                    for r in range(3):
                        mask(r)
                if on(3):
                    eng.wait_ge(agg_ready, b - 2)
                    eng.matmul(p_o[:, :, :], keep["ones3"][:, :], keep["bias3"][:, :, :], start=True, stop=False)
                    for j in range(J):
                        at = slice(j * 128, j * 128 + 128)
                        eng.matmul(p_o[:, j, :], hT[v][:, 1, at], keep["root"][:, :], start=False, stop=False)
                        last = eng.matmul(p_o[:, j, :], agg[v][:, at], keep["ident"][:, :], start=False, stop=j == J - 1)
                    last.then_inc(o_ready, 1)
                if on(2):
                    eng.matmul(p_same[:, :], keep["pick"][:, R, :], hot[u][:, :], start=True, stop=True).then_inc(same_ready, 1)
                    for r in range(R):
                        eng.wait_ge(of_rel_ready, (b - 2) * R + (r + 1))
                        last = eng.matmul(p_msg[:, :], keep["wrel"][:, r, :], of_rel[:, r, :],
                                          start=(r == 0), stop=(r == R - 1))
                        if r < R - 3:
                            mask(r + 3)
                        if on(1) and r == 4:
                            turn()
                    last.then_inc(msg_ready, 1)
                elif on(1):
                    turn()

            steps(eng, NB, 3, step)


def program(nc, inp, out):
    from contextlib import ExitStack
    from concourse import mybir

    fp32, i32, bf16 = mybir.dt.float32, mybir.dt.int32, mybir.dt.bfloat16
    shapes = {"xs": ((NB, 128, BE), fp32), "xd": ((NB, 128, BE), fp32), "x1f": ((NB, 128, BE), fp32),
              "x1": ((EP + 1, F), fp32), "delta": ((EP + 1, F), fp32), "er2": ((H, EP), fp32),
              "rows": ((4, EP), bf16), "hot": ((R + 1, EP), bf16), "pos": ((N, 1), i32), "parts": ((2, 3, F), bf16),
              "end": ((NB + 1, 128, J), i32), "at": ((NB + 1, 128, J), i32)}
    tab = {k: nc.dram_tensor(f"tab_{k}", s, dt).ap() for k, (s, dt) in shapes.items()}
    Memory.used.clear()
    with ExitStack() as ctx:
        m = Memory(nc, ctx, "keep")
        keep = {"ident": m.sb("ident", [128, 128]), "expand": m.sb("expand", [H, 128]),
                "pick": m.sb("pick", [R + 1, R + 1, 128], bf16), "rowpick": m.sb("rowpick", [4, 2, 128], bf16), "ones": m.sb("ones", [1, 128]),
                "w1": m.sb("w1", [128, 128]), "w2": m.sb("w2", [128, 128]), "wm": m.sb("wm", [128, 2, 128]),
                "root": m.sb("root", [128, 128]), "wrel": m.sb("wrel", [128, R, 128]),
                "wel1": m.sb("wel1", [128, 128]), "wer1": m.sb("wer1", [128, 128]),
                "wel2": m.sb("wel2", [128, 128]), "wer2": m.sb("wer2", [128, H]),
                "bmrow": m.sb("bmrow", [1, F]), "biasrow": m.sb("biasrow", [1, F]),
                "alpha4": m.sb("alpha4", [128, J, F]),
                "norm": m.sb("norm", [128, TILES]), "ones3": m.sb("ones3", [3, 128], bf16),
                "bm3": m.sb("bm3", [3, J, F], bf16), "bias3": m.sb("bias3", [3, J, F], bf16)}
        weights_phase(nc, keep, inp, tab)
        edge_rows_phase(nc, keep, inp, tab)
        counts_phases(nc, keep, inp, tab)
        clear_semaphores(nc)
        nodes_phase(nc, keep, inp, out)
        gat1_phase(nc, keep, inp, tab)
        spread_phases(nc, keep, inp, tab)
        gat2_phase(nc, keep, inp, tab)
        rgcn_phase(nc, keep, inp, tab, out)


def kernel(**inputs):
    import concourse.bacc as _bacc
    from concourse import mybir as _mybir
    from concourse.bass_utils import run_bass_kernel_spmd as _run
    import ml_dtypes

    src, dst, kind, w = (np.asarray(inputs[k]) for k in ("src", "dst", "edge_type_8", "edge_weight"))

    def padded(a, value, extra=0):
        return np.concatenate([a, np.full(EP + extra - E, value, a.dtype)])

    def edge_rows(a):
        return np.ascontiguousarray(a.reshape(-1, 128).T)

    def by_block(a):
        return a.reshape(NB + 1, J, 128).transpose(0, 2, 1)

    numbers = padded(np.arange(E, dtype=np.int32), 0, BE)
    ids = np.concatenate([by_block(padded(src, 0, BE)), by_block(padded(dst, 0, BE)), by_block(numbers)], axis=2)
    segments = padded(dst, N)
    row = np.arange(128)
    heads = (row[:, None] // D == np.arange(H)[None, :])
    arrays = {
        "x": np.asarray(inputs["x"]), "ids": np.ascontiguousarray(ids), "w": padded(w, 0), "kind": padded(kind, 0),
        "dseg": np.concatenate([np.full(1, -1, dst.dtype), segments, np.full(1, -1, dst.dtype)]),
        "here": edge_rows(segments), "next": edge_rows(np.concatenate([segments[1:], np.full(1, -1, dst.dtype)])),
        "ident": np.eye(128, dtype=np.float32), "ones": np.ones((1, 128), np.float32),
        "blockmask": (row[:, None] // D == row[None, :] // D).astype(np.float32),
        "headsel": heads.astype(np.float32), "expand": np.ascontiguousarray(heads.T.astype(np.float32)),
        "pick": np.ascontiguousarray(np.broadcast_to(np.eye(R + 1)[:, :, None], (R + 1, R + 1, 128)).astype(ml_dtypes.bfloat16)),
        "rowpick": np.ascontiguousarray(np.broadcast_to(
            np.array([[1, 0], [1, 0], [1, 0], [0, 1]])[:, :, None], (4, 2, 128)).astype(ml_dtypes.bfloat16)),
        "ones3": np.ones((3, 128), ml_dtypes.bfloat16),
        "relcol": (np.arange(R * C) // C).astype(np.float32)[:, None],
        "chunksel": (np.arange(R * C)[:, None] % C == np.arange(C)[None, :]).astype(np.float32),
        "W1": np.asarray(inputs["L0_gnn_W1"]), "W2": np.asarray(inputs["L0_gnn_W2"]),
        "al1": np.asarray(inputs["L0_gnn_al1"]), "ar1": np.asarray(inputs["L0_gnn_ar1"]),
        "al2": np.asarray(inputs["L0_gnn_al2"]), "ar2": np.asarray(inputs["L0_gnn_ar2"]),
        "Wm": np.asarray(inputs["L0_gnn_Wm"]), "bm": np.asarray(inputs["L0_gnn_bm"]),
        "basis": np.asarray(inputs["L1_gnn_basis"]), "comp": np.asarray(inputs["L1_gnn_comp"]),
        "root": np.asarray(inputs["L1_gnn_root"]), "bias": np.asarray(inputs["L1_gnn_bias"]),
        "alpha": np.asarray(inputs["L1_gnn_alpha"]),
    }
    nc = _bacc.Bacc("TRN2", target_bir_lowering=False, num_devices=1)
    inp = {k: nc.dram_tensor(f"in_{k}", a.shape, _mybir.dt.from_np(a.dtype), kind="ExternalInput").ap()
           for k, a in arrays.items()}
    out = nc.dram_tensor("out_0", (N, F), _mybir.dt.float32, kind="ExternalOutput").ap()
    program(nc, inp, out)
    r = _run(nc, [{f"in_{k}": a for k, a in arrays.items()}], core_ids=[0])
    return r.results[0]["out_0"]
```

```python
import numpy as np

N = 100000
E = 50000
F = 128
H = 8
D = F // H
R = 8
BE = 512
J = BE // 128
NB = 2 * -(-E // (2 * BE))
EP = NB * BE
TILES = EP // 128
C = 14
CL = EP // C
CT = CL // 128
NP = 125
JN = 8
NQ = N // (NP * JN)
ZERO_ROW = EP
UNROLL = 4
FAR = 1 << 20
CUT = -1e30
EPS = 1e-5
SLOPE = 0.1
DMA_SEMS = {"x_loaded", "xs_loaded", "stored", "gathered", "placed", "spilled", "f_stored", "ids_loaded", "rows_loaded",
            "x1f_loaded", "found", "found_stored", "y_kept", "at_loaded", "ends_loaded", "scattered"}
TABLE = "natural_log_exp_and_others"


def steps(eng, count, depth, step, ahead=0, ways=2):
    def peeled(b):
        step(b, b % ways, lambda k: 0 <= b - k < count)

    head = -(-depth // ways) * ways
    turns = (count - head - ahead) // UNROLL
    for b in range(head):
        peeled(b)
    with eng.Fori(0, turns) as i:
        for k in range(UNROLL):
            step(i * UNROLL + (head + k), (head + k) % ways, lambda k: True)
    for b in range(head + turns * UNROLL, count + depth):
        peeled(b)


def blocks(eng, count, body):
    with eng.Fori(0, count // 2) as i:
        body(i * 2, 0)
        body(i * 2 + 1, 1)


def nth(k, b, slot, ways=2):
    return (b - slot) * (k // ways) + k


class Link:

    def __init__(self, eng, sem, per_block):
        self.eng, self.sem, self.per_block = eng, sem, per_block

    def begin(self, b):
        self.block, self.base, self.n = b, b * self.per_block, 0

    def mark(self, ins):
        self.n += 1
        ins.then_inc(self.sem, 1)

    def wait(self):
        self.eng.wait_ge(self.sem, self.base + self.n)

    def __call__(self, ins):
        self.mark(ins)
        self.wait()

    def end(self):
        assert self.n == self.per_block, self.n


class Memory:

    used = []

    def __init__(self, nc, ctx, name):
        from concourse import mybir

        self.nc, self.ctx, self.name, self.fp32 = nc, ctx, name, mybir.dt.float32

    def sb(self, name, shape, dt=None):
        return self.ctx.enter_context(self.nc.sbuf_tensor(f"{self.name}_{name}", shape, dt or self.fp32))

    def ps(self, name, shape):
        return self.ctx.enter_context(self.nc.psum_tensor(f"{self.name}_{name}", shape, self.fp32))

    def slots(self, name):
        return [self.sem(f"{name}{u}") for u in range(2)]

    def sem(self, name):
        sem = self.ctx.enter_context(self.nc.semaphore(f"{self.name}_{name}"))
        Memory.used.append(sem)
        return sem


def clear_semaphores(nc):
    with nc.Block() as block:
        @block.gpsimd
        def _(eng):
            for sem in Memory.used:
                eng.sem_clear(sem)
            Memory.used.clear()


def weights_phase(nc, keep, inp, tab):
    from contextlib import ExitStack
    from concourse import mybir
    from concourse.alu_op_type import AluOpType as ALU

    bf16 = mybir.dt.bfloat16
    with ExitStack() as ctx:
        m = Memory(nc, ctx, "wt")
        wT = m.sb("wT", [128, 2, 128])
        att = m.sb("att", [128, 4])
        attx = m.sb("attx", [128, 4, 128])
        blockmask = m.sb("blockmask", [128, 128])
        headsel = m.sb("headsel", [128, H])
        att8 = m.sb("att8", [128, H])
        basis = m.sb("basis", [128, R, 128])
        comp = m.sb("comp", [128, R * R])
        p_wT = m.ps("p_wT", [128, 2, 128])
        p_x = m.ps("p_x", [128, 3, 128])
        p_8 = m.ps("p_8", [128, H])
        rest = [m.sb(f"rest{k}", [1, F]) for k in range(3)]
        part = [[m.sb(f"part{n}{k}", [1, F], bf16) for k in range(3)] for n in range(2)]
        loaded, expanded, turned, turned_sb, folded, step, done, split, stored, spread = (m.sem(n) for n in (
            "loaded", "expanded", "turned", "turned_sb", "folded", "step", "done", "split", "stored", "spread"))
        block = ctx.enter_context(nc.Block())
        LOADS = 20 + J

        @block.sync
        def _(eng):
            def load(dst, src):
                eng.dma_start(dst, src).then_inc(loaded, 16)

            load(keep["ident"][:, :], inp["ident"])
            load(blockmask[:, :], inp["blockmask"])
            load(headsel[:, :], inp["headsel"])
            load(keep["expand"][:, :], inp["expand"])
            load(keep["pick"][:, :, :], inp["pick"])
            load(keep["ones3"][:, :], inp["ones3"])
            load(keep["rowpick"][:, :, :], inp["rowpick"])
            load(keep["w1"][:, :], inp["W1"])
            load(keep["w2"][:, :], inp["W2"])
            with nc.allow_non_contiguous_dma(reason="four columns of 128 numbers"):
                for n, name in enumerate(("al1", "ar1", "al2", "ar2")):
                    load(att[:, n:n + 1], inp[name].rearrange("h (d a) -> (h d) a", a=1))
            load(keep["wm"][:, :, :], inp["Wm"].rearrange("(l k) n -> k l n", l=2))
            load(keep["bmrow"][:, :], inp["bm"].rearrange("(a n) -> a n", a=1))
            load(keep["root"][:, :], inp["root"])
            load(keep["biasrow"][:, :], inp["bias"].rearrange("(a n) -> a n", a=1))
            load(basis[:, :, :], inp["basis"].rearrange("b k n -> k b n"))
            load(comp[:, :], inp["comp"].rearrange("r b -> (r b)").partition_broadcast(128))
            load(keep["ones"][:, :], inp["ones"])
            for j in range(J):
                load(keep["alpha4"][:, j, :], inp["alpha"].partition_broadcast(128))
            eng.wait_ge(split, 1)
            for n in range(2):
                for k in range(3):
                    eng.dma_start(tab["parts"][n, k:k + 1, :], part[n][k][:, :]).then_inc(stored, 16)
            eng.wait_ge(stored, 6 * 16)
            for n, name in enumerate(("bm3", "bias3")):
                for j in range(J):
                    eng.dma_start(keep[name][:, j, :], tab["parts"][n]).then_inc(spread, 16)
            eng.wait_ge(spread, 2 * J * 16)

        @block.tensor
        def _(eng):
            eng.wait_ge(loaded, 16 * LOADS)
            eng.transpose(p_wT[:, 0, :], keep["w1"][:, :], keep["ident"][:, :])
            eng.transpose(p_wT[:, 1, :], keep["w2"][:, :], keep["ident"][:, :]).then_inc(turned, 1)
            eng.wait_ge(turned_sb, 1)
            eng.wait_ge(expanded, 1)
            for n, layer in ((0, 0), (1, 0), (2, 1)):
                eng.matmul(p_x[:, n, :], wT[:, layer, :], attx[:, n, :], start=True, stop=True)
            eng.matmul(p_8[:, :], wT[:, 1, :], att8[:, :], start=True, stop=True).then_inc(folded, 1)

        @block.vector
        def _(eng):
            link = Link(eng, step, R * R + 11)
            link.begin(0)
            eng.wait_ge(loaded, 16 * LOADS)
            for n, row in enumerate((keep["bmrow"], keep["biasrow"])):
                link(eng.tensor_copy(rest[0][:, :], row[:, :]))
                for k in range(3):
                    if n == 1 and k == 2:
                        eng.tensor_copy(part[n][k][:, :], rest[k][:, :]).then_inc(split, 1)
                    else:
                        link(eng.tensor_copy(part[n][k][:, :], rest[k][:, :]))
                    if k < 2:
                        link(eng.tensor_tensor(rest[k + 1][:, :], rest[k][:, :], part[n][k][:, :], ALU.subtract))
            for n in range(3):
                eng.tensor_scalar(attx[:, n, :], blockmask[:, :], att[:, n:n + 1], None, ALU.mult)
            eng.tensor_scalar(att8[:, :], headsel[:, :], att[:, 3:4], None, ALU.mult).then_inc(expanded, 1)
            eng.wait_ge(turned, 1)
            eng.tensor_copy(wT[:, :, :], p_wT[:, :, :]).then_inc(turned_sb, 1)
            for b in range(R):
                for r in range(R):
                    w, c = keep["wrel"][:, r, :], comp[:, r * R + b:r * R + b + 1]
                    if b == 0:
                        link(eng.tensor_scalar(w, basis[:, b, :], c, None, ALU.mult))
                    else:
                        link(eng.scalar_tensor_tensor(w, basis[:, b, :], c, w, ALU.mult, ALU.add))
            link.end()
            eng.wait_ge(folded, 1)
            eng.tensor_copy(keep["wel1"][:, :], p_x[:, 0, :])
            eng.tensor_copy(keep["wer1"][:, :], p_x[:, 1, :])
            eng.tensor_copy(keep["wel2"][:, :], p_x[:, 2, :])
            eng.tensor_copy(keep["wer2"][:, :], p_8[:, :]).then_inc(done, 1)


def edge_rows_phase(nc, keep, inp, tab):
    from contextlib import ExitStack
    from concourse import mybir
    from concourse.alu_op_type import AluOpType as ALU

    i32, bf16 = mybir.dt.int32, mybir.dt.bfloat16
    FILL = N // NP
    with ExitStack() as ctx:
        m = Memory(nc, ctx, "er")
        cur, prev = m.sb("cur", [NB, BE], i32), m.sb("prev", [NB, BE], i32)
        same, cut = m.sb("same", [NB, BE]), m.sb("cut", [NB, BE], bf16)
        same16 = m.sb("same16", [NB, BE], bf16)
        w, part = [m.sb(f"w{k}", [NB, BE]) for k in range(3)], [m.sb(f"part{k}", [NB, BE], bf16) for k in range(3)]
        here, nxt = m.sb("here", [128, TILES], i32), m.sb("nxt", [128, TILES], i32)
        goes_on, end = m.sb("goes_on", [128, TILES]), m.sb("end", [128, TILES], i32)
        zero, no_edge = m.sb("zero", [1, F]), m.sb("no_edge", [128, FILL], i32)
        loaded, step, ready, stored = (m.sem(n) for n in ("loaded", "step", "ready", "stored"))
        block = ctx.enter_context(nc.Block())

        @block.sync
        def _(eng):
            row = lambda k: inp["dseg"][k:k + EP].rearrange("(b e) -> b e", e=BE)
            eng.dma_start(cur[:, :], row(1)).then_inc(loaded, 16)
            eng.dma_start(prev[:, :], row(0)).then_inc(loaded, 16)
            eng.dma_start(here[:, :], inp["here"]).then_inc(loaded, 16)
            eng.dma_start(nxt[:, :], inp["next"]).then_inc(loaded, 16)
            eng.dma_start(w[0][:, :], inp["w"].rearrange("(b e) -> b e", e=BE)).then_inc(loaded, 16)
            eng.wait_ge(ready, 4)
            rows = lambda t: t.rearrange("(b e) -> b e", e=BE)
            for k, t in enumerate((*part, cut)):
                eng.dma_start(rows(tab["rows"][k, :]), t[:, :]).then_inc(stored, 16)
            eng.dma_start(rows(tab["hot"][R, :]), same16[:, :]).then_inc(stored, 16)
            eng.dma_start(tab["end"][0:NB].rearrange("b p j -> p b j"),
                          end[:, :].rearrange("p (b j) -> p b j", j=J)).then_inc(stored, 16)
            eng.dma_start(tab["x1"][ZERO_ROW:ZERO_ROW + 1, :], zero[:, :]).then_inc(stored, 16)
            eng.dma_start(tab["delta"][ZERO_ROW:ZERO_ROW + 1, :], keep["bmrow"][:, :]).then_inc(stored, 16)
            eng.dma_start(tab["pos"].rearrange("(p n) a -> p (n a)", p=NP), no_edge[0:NP, :]).then_inc(stored, 16)
            eng.dma_start(tab["end"][NB, :, :], no_edge[:, 0:J]).then_inc(stored, 16)
            eng.dma_start(tab["at"][NB, :, :], no_edge[:, 0:J]).then_inc(stored, 16)
            eng.wait_ge(stored, 11 * 16)

        @block.vector
        def _(eng):
            link = Link(eng, step, 6)
            link.begin(0)
            eng.memset(zero[:, :], 0.0)
            eng.memset(no_edge[:, :], ZERO_ROW).then_inc(ready, 1)
            eng.wait_ge(loaded, 80)
            for k in range(3):
                if k == 2:
                    eng.tensor_copy(part[k][:, :], w[k][:, :]).then_inc(ready, 1)
                else:
                    link(eng.tensor_copy(part[k][:, :], w[k][:, :]))
                    link(eng.tensor_tensor(w[k + 1][:, :], w[k][:, :], part[k][:, :], ALU.subtract))
            link(eng.tensor_tensor(same[:, :], cur[:, :], prev[:, :], ALU.is_equal))
            eng.tensor_copy(same16[:, :], same[:, :])
            eng.tensor_scalar(cut[:, :], same[:, :], -CUT, CUT, ALU.mult, ALU.add).then_inc(ready, 1)
            link(eng.tensor_tensor(goes_on[:, :], here[:, :], nxt[:, :], ALU.is_equal))
            eng.scalar_tensor_tensor(end[:, :], goes_on[:, :], float(FAR), here[:, :],
                                     ALU.mult, ALU.add).then_inc(ready, 1)
            link.end()


def chunk_scan_phase(nc, keep, name, on, add, out, backward):
    from contextlib import ExitStack
    from concourse import mybir
    from concourse.alu_op_type import AluOpType as ALU

    P = H * C
    way = slice(None, None, -1) if backward else slice(None)
    last = 0 if backward else CL - 1
    with ExitStack() as ctx:
        m = Memory(nc, ctx, name)
        whole, col = m.sb("whole", [P, 1]), m.sb("col", [P, 1])
        whole_row, sum_row, carry_row = m.sb("whole_row", [1, P]), m.sb("sum_row", [1, P]), m.sb("carry_row", [1, P])
        p_rows, p_col = m.ps("p_rows", [1, 2, P]), m.ps("p_col", [P, 1])
        summed, rowed, carried, columned, step = (m.sem(n) for n in ("summed", "rowed", "carried", "columned", "step"))
        block = ctx.enter_context(nc.Block())

        @block.vector
        def _(eng):
            link = Link(eng, step, 5)
            link.begin(0)
            eng.tensor_tensor_scan(out[:, way], on[:, way], add[:, way], 0.0, ALU.mult, ALU.add)
            eng.tensor_reduce(whole[:, :], on, mybir.AxisListType.X, ALU.min).then_inc(summed, 1)
            eng.wait_ge(rowed, 1)
            link(eng.tensor_copy(whole_row[:, :], p_rows[:, 1, :]))
            link(eng.tensor_tensor_scan(sum_row[:, way], whole_row[:, way], p_rows[:, 0, way], 0.0,
                                        ALU.mult, ALU.add))
            link(eng.memset(carry_row[:, :], 0.0))
            rows = lambda t: t[:, :].rearrange("a (h c) -> a h c", c=C)
            if backward:
                to, frm = rows(carry_row)[:, :, 0:C - 1], rows(sum_row)[:, :, 1:C]
            else:
                to, frm = rows(carry_row)[:, :, 1:C], rows(sum_row)[:, :, 0:C - 1]
            eng.tensor_copy(to, frm).then_inc(carried, 1)
            eng.wait_ge(columned, 1)
            link(eng.tensor_copy(col[:, :], p_col[:, :]))
            link(eng.tensor_tensor_scan(out[:, way], on[:, way], add[:, way], col[:, 0:1], ALU.mult, ALU.add))
            link.end()

        @block.tensor
        def _(eng):
            eng.wait_ge(summed, 1)
            eng.matmul(p_rows[:, 0, :], out[:, last:last + 1], keep["ident"][0:P, 0:P], start=True, stop=True)
            eng.matmul(p_rows[:, 1, :], whole[:, :], keep["ident"][0:P, 0:P], start=True, stop=True).then_inc(rowed, 1)
            eng.wait_ge(carried, 1)
            eng.matmul(p_col[:, :], carry_row[:, :], keep["ones"][0:1, 0:1], start=True, stop=True).then_inc(columned, 1)


def chunked(t):
    return t.rearrange("(c e) -> c e", e=CL)


def counts_phases(nc, keep, inp, tab):
    from contextlib import ExitStack
    from concourse import mybir
    from concourse.alu_op_type import AluOpType as ALU

    i32, bf16 = mybir.dt.int32, mybir.dt.bfloat16
    P = R * C
    with ExitStack() as ctx:
        m = Memory(nc, ctx, "ct")
        kind, cur = m.sb("kind", [P, CL], i32), m.sb("cur", [P, CL], i32)
        before, after = m.sb("before", [P, CL]), m.sb("after", [P, CL])
        hot, hot16 = m.sb("hot", [P, CL]), m.sb("hot16", [P, CL], bf16)
        relcol, chunksel = m.sb("relcol", [P, 1]), m.sb("chunksel", [P, C])
        fwd, bwd = kind[:, :].bitcast(m.fp32), cur[:, :].bitcast(m.fp32)
        loaded, ready, made, stored = (m.sem(n) for n in ("loaded", "ready", "made", "stored"))
        with nc.Block() as block:
            @block.sync
            def _(eng):
                eng.dma_start(relcol[:, :], inp["relcol"]).then_inc(loaded, 16)
                eng.dma_start(chunksel[:, :], inp["chunksel"]).then_inc(loaded, 16)
                for r in range(R):
                    at = slice(r * C, r * C + C)
                    eng.dma_start(kind[at, :], chunked(inp["kind"])).then_inc(loaded, 16)
                    eng.dma_start(cur[at, :], chunked(inp["dseg"][1:EP + 1])).then_inc(loaded, 16)
                    eng.dma_start(before[at, :].bitcast(i32), chunked(inp["dseg"][0:EP])).then_inc(loaded, 16)
                    eng.dma_start(after[at, :].bitcast(i32), chunked(inp["dseg"][2:EP + 2])).then_inc(loaded, 16)
                eng.wait_ge(ready, 1)
                eng.dma_start(tab["hot"][0:R, :].rearrange("r (c e) -> (r c) e", e=CL), hot16[:, :]).then_inc(stored, 16)
                eng.wait_ge(stored, 16)

            @block.vector
            def _(eng):
                eng.wait_ge(loaded, 16 * (2 + 4 * R))
                eng.tensor_scalar(hot[:, :], kind[:, :], relcol[:, 0:1], None, ALU.is_equal).then_inc(made, 1)
                eng.wait_ge(made, 1)
                eng.tensor_copy(hot16[:, :], hot[:, :]).then_inc(ready, 1)
                eng.tensor_tensor(before[:, :], cur[:, :], before[:, :].bitcast(i32), ALU.is_equal)
                eng.tensor_tensor(after[:, :], cur[:, :], after[:, :].bitcast(i32), ALU.is_equal).then_inc(made, 1)
                eng.wait_ge(made, 2)
        chunk_scan_phase(nc, keep, "cf", before[:, :], hot[:, :], fwd, False)
        chunk_scan_phase(nc, keep, "cb", after[:, :], hot[:, :], bwd, True)
        p_cnt = m.ps("p_cnt", [128, CT, C])
        cnt = m.sb("cnt", [128, CT, C])
        link_sem, own, counted, done = (m.sem(n) for n in ("step", "own", "counted", "done"))
        with nc.Block() as block:
            @block.vector
            def _(eng):
                link = Link(eng, link_sem, 3)
                link.begin(0)
                link(eng.tensor_tensor(fwd, fwd, bwd, ALU.add))
                link(eng.tensor_tensor(fwd, fwd, hot[:, :], ALU.subtract))
                eng.tensor_tensor(fwd, fwd, hot[:, :], ALU.mult).then_inc(own, 1)
                eng.wait_ge(counted, 1)
                link(eng.tensor_scalar(cnt[:, :, :], p_cnt[:, :, :], 1.0, None, ALU.max))
                eng.reciprocal(keep["norm"][:, :].rearrange("p (c t) -> p t c", t=CT), cnt[:, :, :]).then_inc(done, 1)
                link.end()

            @block.tensor
            def _(eng):
                eng.wait_ge(own, 1)
                for t in range(CT):
                    last = eng.matmul(p_cnt[:, t, :], fwd[:, t * 128:(t + 1) * 128], chunksel[:, :],
                                      start=True, stop=True)
                last.then_inc(counted, 1)


def spread_phases(nc, keep, inp, tab):
    from contextlib import ExitStack
    from concourse import mybir
    from concourse.alu_op_type import AluOpType as ALU

    i32 = mybir.dt.int32
    P = H * C
    with ExitStack() as ctx:
        m = Memory(nc, ctx, "sp")
        cur, after = m.sb("cur", [P, CL], i32), m.sb("after", [P, CL])
        term, spread = m.sb("term", [P, CL]), m.sb("spread", [P, CL])
        loaded, step, stored = (m.sem(n) for n in ("loaded", "step", "stored"))
        rows = tab["er2"].rearrange("h (c e) -> (h c) e", e=CL)
        with nc.Block() as block:
            @block.sync
            def _(eng):
                eng.dma_start(term[:, :], rows).then_inc(loaded, 16)
                for h in range(H):
                    at = slice(h * C, h * C + C)
                    eng.dma_start(cur[at, :], chunked(inp["dseg"][1:EP + 1])).then_inc(loaded, 16)
                    eng.dma_start(after[at, :].bitcast(i32), chunked(inp["dseg"][2:EP + 2])).then_inc(loaded, 16)

            @block.vector
            def _(eng):
                link = Link(eng, step, 3)
                link.begin(0)
                eng.wait_ge(loaded, 16 * (1 + 2 * H))
                link(eng.tensor_tensor(after[:, :], cur[:, :], after[:, :].bitcast(i32), ALU.is_equal))
                link(eng.tensor_tensor(spread[:, :], term[:, :], after[:, :], ALU.mult))
                link(eng.tensor_tensor(term[:, :], term[:, :], spread[:, :], ALU.subtract))
                link.end()
        chunk_scan_phase(nc, keep, "sb", after[:, :], term[:, :], spread[:, :], True)
        with nc.Block() as block:
            @block.sync
            def _(eng):
                eng.dma_start(rows, spread[:, :]).then_inc(stored, 16)
                eng.wait_ge(stored, 16)


class Norm:

    def __init__(self, m, parts, groups):
        def two(name):
            return [m.sb(f"{name}{u}", [parts, groups]) for u in range(2)]

        self.raw = [m.sb(f"raw{u}", [parts, groups, 6]) for u in range(2)]
        self.total, self.apart, self.spread, self.var = two("total"), two("apart"), two("spread"), two("var")
        self.log, self.guess, self.square, self.part = two("log"), two("guess"), two("square"), two("part")
        self.scale, self.shift = two("scale"), two("shift")


def moments_part(eng, link, n, u, k):
    from concourse.alu_op_type import AluOpType as ALU

    raw, total, apart, square = n.raw[u], n.total[u][:, :], n.apart[u][:, :], n.square[u][:, :]
    link.wait()
    if k == 0:
        eng.tensor_tensor(total, raw[:, :, 1], raw[:, :, 4], ALU.add)
        eng.tensor_tensor(n.spread[u][:, :], raw[:, :, 2], raw[:, :, 5], ALU.add)
        link.mark(eng.tensor_tensor(apart, raw[:, :, 1], raw[:, :, 4], ALU.subtract))
    elif k == 1:
        link.mark(eng.tensor_tensor(square, apart, apart, ALU.mult))
    elif k == 2:
        link.mark(eng.scalar_tensor_tensor(apart, square, F / 4.0, n.spread[u][:, :], ALU.mult, ALU.add))
    else:
        return eng.tensor_scalar(n.var[u][:, :], apart, 1.0 / F, EPS, ALU.mult, ALU.add)


def scales_part(eng, link, n, u, k, factor=None):
    from concourse.alu_op_type import AluOpType as ALU

    g, s, v, t, scale = n.guess[u][:, :], n.square[u][:, :], n.var[u][:, :], n.part[u][:, :], n.scale[u]
    if k > 0:
        link.wait()
    if k == 0:
        link.mark(eng.tensor_tensor(s, g, g, ALU.mult))
    elif k == 1:
        link.mark(eng.scalar_tensor_tensor(t, v, -0.5, s, ALU.mult, ALU.mult))
    elif k == 2:
        link.mark(eng.scalar_tensor_tensor(scale[:, :], t, 1.5, g, ALU.add, ALU.mult))
    elif k == 3 and factor is not None:
        link.mark(eng.tensor_tensor(scale[:, 0:J], scale[:, 0:J], factor, ALU.mult))
    else:
        return eng.scalar_tensor_tensor(n.shift[u][:, :], n.total[u][:, :], -0.5, scale[:, :], ALU.mult, ALU.mult)


def nodes_phase(nc, keep, inp, tab, out):
    from contextlib import ExitStack
    import concourse.bass as bass
    from concourse import mybir
    from concourse.alu_op_type import AluOpType as ALU

    ACT, i32 = mybir.ActivationFunctionType, mybir.dt.int32
    x_b = inp["x"].rearrange("(p b j) f -> p b j f", p=NP, j=JN)
    out_b = out.rearrange("(p b j) f -> p b j f", p=NP, j=JN)
    WAYS = 4
    with ExitStack() as ctx:
        m = Memory(nc, ctx, "nd")
        x, y = ([m.sb(f"{n}{s}", [NP, JN, F]) for s in range(WAYS)] for n in ("x", "y"))
        low, res = m.sb("low", [NP, JN, F]), [m.sb(f"res{u}", [NP, JN, F]) for u in range(2)]
        ids, ends = ([m.sb(f"{n}{s}", [128, w * J], i32) for s in range(WAYS)] for n, w in (("ids", 3), ("ends", 1)))
        xs = [m.sb(f"xs{s}", [128, J, F]) for s in range(WAYS)]
        hn, hT = m.sb("hn", [NP, JN, F]), m.sb("hT", [128, JN, NP])
        bm8, alpha8 = m.sb("bm8", [NP, JN, F]), m.sb("alpha8", [NP, JN, F])
        norm = Norm(m, NP, JN)
        p_hT = m.ps("p_hT", [128, JN, 128])
        p_o = [m.ps(f"p_o{u}", [NP, JN, F]) for u in range(2)]
        x_loaded, ids_loaded, gathered, placed, spilled = (
            [m.sem(f"{n}{s}") for s in range(WAYS)] for n in ("x_loaded", "ids_loaded", "gathered", "placed", "spilled"))
        stored = m.slots("stored")
        (rows_loaded, y_ready, var_ready, log_ready, guess_ready, scale_ready, hn_ready, hT_ready, hT_copied,
         o_ready, low_ready, res_ready, pool_go, step_n, step_c, step_o) = (m.sem(n) for n in (
            "rows_loaded", "y_ready", "var_ready", "log_ready", "guess_ready", "scale_ready", "hn_ready", "hT_ready",
            "hT_copied", "o_ready", "low_ready", "res_ready", "pool_go", "step_n", "step_c", "step_o"))
        block = ctx.enter_context(nc.Block())

        @block.sync
        def _(eng):
            for u in range(2):
                eng.sem_inc(stored[u], 16)
            for s in range(WAYS):
                eng.sem_inc(spilled[s], 16)

            def load_x(b, s):
                eng.dma_start(x[s][:, :, :], x_b[:, b, :, :]).then_inc(x_loaded[s], 16)

            def load_ids(b, s):
                eng.dma_start(ids[s][:, :], inp["ids"][b, :, :]).then_inc(ids_loaded[s], 16)
                eng.dma_start(ends[s][:, :], tab["end"][b, :, :]).then_inc(ids_loaded[s], 16)

            def step(b, s, on):
                edges = lambda k: on(k) and not (isinstance(b, int) and b - k >= NB)
                v = (s - 1) % WAYS
                if on(-WAYS):
                    eng.wait_ge(y_ready, b + 1)
                    load_x(b + WAYS, s)
                if edges(1):
                    eng.wait_ge(gathered[v], nth(64, b - 1, v, WAYS))
                    eng.dma_start(tab["xs"][b - 1, :, :], xs[v][:, :, :].rearrange("p j f -> p (j f)")).then_inc(spilled[v], 16)
                    if edges(-3):
                        eng.wait_ge(placed[v], nth(64, b - 1, v, WAYS))
                        load_ids(b + 3, v)
                if on(2):
                    eng.wait_ge(res_ready, b)
                    eng.dma_start(out_b[:, b - 2, :, :], res[s % 2][:, :, :]).then_inc(stored[s % 2], 16)

            load_ids(0, 0)
            load_x(0, 0)
            for j in range(JN):
                eng.dma_start(bm8[:, j, :], inp["bm"].partition_broadcast(NP)).then_inc(rows_loaded, 16)
                eng.dma_start(alpha8[:, j, :], inp["alpha"].partition_broadcast(NP)).then_inc(rows_loaded, 16)
            for b in range(1, WAYS):
                load_x(b, b)
                load_ids(b, b)
            steps(eng, NQ, 2, step, ahead=WAYS, ways=WAYS)
            for s in range(WAYS):
                eng.wait_ge(spilled[s], (NB - s + WAYS - 1) // WAYS * 16 + 16)
            for u in range(2):
                eng.wait_ge(stored[u], 8 * NQ + 16)

        @block.gpsimd
        def _(eng):
            def step(b, s, on):
                eng.wait_ge(ids_loaded[s], nth(32, b, s, WAYS))
                eng.wait_ge(spilled[s], nth(16, b, s, WAYS))
                eng.sem_inc(pool_go, 1)
                for j in range(J):
                    eng.indirect_dma_start(
                        xs[s][:, j, :], None, inp["x"][:, :],
                        bass.IndirectOffsetOnAxis(ap=ids[s][:, j:j + 1], axis=0)).then_inc(gathered[s], 16)
                for j in range(J):
                    eng.indirect_dma_start(
                        tab["pos"][:, :], bass.IndirectOffsetOnAxis(ap=ends[s][:, j:j + 1], axis=0),
                        ids[s][:, 2 * J + j:2 * J + j + 1], None,
                        bounds_check=N - 1, oob_is_err=False).then_inc(placed[s], 16)

            steps(eng, NB, 0, step, ways=WAYS)
            for s in range(WAYS):
                eng.wait_ge(placed[s], (NB - s + WAYS - 1) // WAYS * 64)

        @block.vector
        def _(eng):
            eng.sem_inc(low_ready, 2)
            eng.sem_inc(res_ready, 1)
            ln, lc = Link(eng, step_n, 4), Link(eng, step_c, 3)

            def step(b, s, on):
                u = s % 2
                if on(0):
                    ln.begin(b)
                    eng.wait_ge(x_loaded[s], nth(16, b, s, WAYS))
                    eng.tensor_tensor(y[s][:, :, :], x[s][:, :, :], bm8[:, :, :], ALU.add).then_inc(y_ready, 1)
                    eng.wait_ge(y_ready, b + 1)
                    for j in range(JN - 1):
                        eng.bn_stats(norm.raw[u][:, j, :], y[s][:, j, :])
                if on(2):
                    eng.wait_ge(o_ready, b)
                    eng.wait_ge(res_ready, b - 1)
                    eng.scalar_tensor_tensor(low[:, :, :], p_o[u][:, :, :], 0.0, alpha8[:, :, :],
                                             ALU.min, ALU.mult).then_inc(step_o, 1)
                if on(0):
                    ln.mark(eng.bn_stats(norm.raw[u][:, JN - 1, :], y[s][:, JN - 1, :]))
                    for k in range(3):
                        moments_part(eng, ln, norm, u, k)
                    moments_part(eng, ln, norm, u, 3).then_inc(var_ready, 1)
                    ln.end()
                if on(2):
                    eng.wait_ge(step_o, b - 1)
                    eng.scalar_tensor_tensor(low[:, :, :], p_o[u][:, :, :], 0.0, low[:, :, :],
                                             ALU.max, ALU.add).then_inc(low_ready, 1)
                if on(0):
                    lc.begin(b)
                    eng.wait_ge(guess_ready, b + 1)
                    for k in range(3):
                        scales_part(eng, lc, norm, u, k)
                    scales_part(eng, lc, norm, u, 3).then_inc(scale_ready, 1)
                    lc.end()
                if on(2):
                    eng.wait_ge(low_ready, b + 1)
                    eng.wait_ge(stored[u], nth(16, b - 2, u))
                    eng.tensor_tensor(res[u][:, :, :], low[:, :, :], y[(s + 2) % WAYS][:, :, :],
                                      ALU.add).then_inc(res_ready, 1)

            eng.wait_ge(rows_loaded, 2 * JN * 16)
            steps(eng, NQ, 2, step, ways=WAYS)

        @block.scalar
        def _(eng):
            eng.preload_act_table_set(TABLE)

            def step(b, s, on):
                u = s % 2
                if on(0):
                    eng.wait_ge(var_ready, b + 1)
                    eng.activation(norm.log[u][:, :], norm.var[u][:, :], ACT.Ln).then_inc(log_ready, 1)
                    eng.wait_ge(log_ready, b + 1)
                    eng.activation(norm.guess[u][:, :], norm.log[u][:, :], ACT.Exp, scale=-0.5).then_inc(guess_ready, 1)
                if on(1):
                    eng.wait_ge(hT_ready, b)
                    eng.wait_ge(o_ready, b)
                    eng.activation(hT[:, :, :], p_hT[:, :, 0:NP], ACT.Copy).then_inc(hT_copied, 1)
                if on(0):
                    eng.wait_ge(scale_ready, b + 1)
                    for j in range(JN):
                        last = eng.activation(hn[:, j, :], y[s][:, j, :], ACT.Relu,
                                              bias=norm.shift[u][:, j:j + 1], scale=norm.scale[u][:, j:j + 1])
                    last.then_inc(hn_ready, 1)

            steps(eng, NQ, 1, step, ways=WAYS)

        @block.tensor
        def _(eng):
            eng.sem_inc(o_ready, 1)

            def step(b, u, on):
                v = 1 - u
                if on(1):
                    eng.wait_ge(hT_copied, b)
                    eng.wait_ge(low_ready, b)
                    for j in range(JN):
                        if j % 4 == 0:
                            eng.matmul(p_o[v][:, j:j + 4, :], keep["ones3"][:, 0:NP], keep["bias3"][:, :, :],
                                       start=True, stop=False)
                        last = eng.matmul(p_o[v][:, j, :], hT[:, j, :], keep["root"][:, :], start=False, stop=j % 4 == 3)
                    last.then_inc(o_ready, 1)
                if on(0):
                    eng.wait_ge(hn_ready, b + 1)
                    for j in range(JN):
                        last = eng.transpose(p_hT[:, j, 0:NP], hn[:, j, :], keep["ident"][0:NP, 0:NP])
                    last.then_inc(hT_ready, 1)

            steps(eng, NQ, 1, step)


def attention_logits(eng, link, z, slope, w, cut, t, u):
    from concourse.alu_op_type import AluOpType as ALU

    logit, before = t["logit"], t["before"]
    link.mark(eng.tensor_tensor(slope[:, :], z[:, :], slope[:, :], ALU.max))
    eng.tensor_copy(logit[u][:, 0:1], logit[1 - u][:, BE:BE + 1])
    link.wait()
    link(eng.tensor_tensor(logit[u][:, 1:BE + 1], w[:, :], slope[:, :], ALU.mult))
    link(eng.tensor_tensor_scan(before[u][:, :], logit[u][:, 0:BE], cut[:, :], before[1 - u][:, BE - 1:BE],
                                ALU.max, ALU.add))
    return eng.tensor_tensor(t["lead"][u][:, :], logit[u][:, 1:BE + 1], before[u][:, :], ALU.subtract)


def attention_exps(eng, t, u, sem, count):
    from concourse import mybir

    ACT = mybir.ActivationFunctionType
    eng.activation(t["under"][:, :], t["lead"][u][:, :], ACT.Relu, scale=-1.0)
    eng.activation(t["over"][:, :], t["lead"][u][:, :], ACT.Relu).then_inc(sem, 1)
    eng.wait_ge(sem, count)
    eng.activation(t["weight"][u][:, :], t["under"][:, :], ACT.Exp, scale=-1.0)
    return eng.activation(t["fade"][u][:, :], t["over"][:, :], ACT.Exp, scale=-1.0)


def attention_sums_part(eng, link, t, ft, u, k):
    from concourse.alu_op_type import AluOpType as ALU

    num, den = t["num"], t["den"]
    if k == 0:
        link.mark(eng.tensor_tensor(t["message"][:, :], ft[:, :], t["weight"][u][:, :], ALU.mult))
    elif k == 1:
        eng.tensor_tensor_scan(den[u][:, :], t["fade"][u][:, :], t["weight"][u][:, :], den[1 - u][:, BE - 1:BE],
                               ALU.mult, ALU.add)
    else:
        link.wait()
        return eng.tensor_tensor_scan(num[u][:, :], t["fade"][u][:, :], t["message"][:, :], num[1 - u][:, BE - 1:BE],
                                      ALU.mult, ALU.add)


def attention_inverse(eng, t, u, sem, count):
    from concourse import mybir

    ACT = mybir.ActivationFunctionType
    eng.activation(t["log"][:, :], t["den"][u][:, :], ACT.Ln).then_inc(sem, 1)
    eng.wait_ge(sem, count)
    return eng.activation(t["near"][:, :], t["log"][:, :], ACT.Exp, scale=-1.0)


def attention_mean_part(eng, link, t, u, result, k):
    from concourse.alu_op_type import AluOpType as ALU

    inverse, near = t["inverse"][:, :], t["near"][:, :]
    if k > 0:
        link.wait()
    if k == 0:
        link.mark(eng.tensor_tensor(inverse, t["den"][u][:, :], near, ALU.mult))
    elif k == 1:
        link.mark(eng.scalar_tensor_tensor(inverse, inverse, 2.0, near, ALU.subtract, ALU.mult, reverse0=True))
    else:
        return eng.scalar_tensor_tensor(result, t["num"][u][:, :], 0.0, inverse, ALU.max, ALU.mult)


LOGIT_LINKS, SUM_LINKS, MEAN_LINKS = 3, 1, 2


def attention_tiles(m):
    def two(name, width=BE):
        return [m.sb(f"{name}{u}", [128, width]) for u in range(2)]

    t = {"logit": two("logit", BE + 1)}
    t.update({name: two(name) for name in ("before", "lead", "weight", "fade", "num", "den")})
    t.update({name: m.sb(name, [128, BE]) for name in ("under", "over", "message", "inverse", "log", "near")})
    return t


def start_attention(eng, t, sem):
    eng.memset(t["logit"][1][:, BE:BE + 1], CUT)
    eng.memset(t["before"][1][:, BE - 1:BE], CUT)
    eng.memset(t["num"][1][:, BE - 1:BE], 0.0)
    eng.memset(t["den"][1][:, BE - 1:BE], 0.0).then_inc(sem, 1)
    eng.wait_ge(sem, 1)


def edge_rows_of(table, b):
    import concourse.bass as bass

    return table[bass.ds(b * BE, BE), :].rearrange("(j p) f -> p j f", p=128)


def gat1_phase(nc, keep, inp, tab):
    from contextlib import ExitStack
    import concourse.bass as bass
    from concourse import mybir

    ACT, i32, bf16 = mybir.ActivationFunctionType, mybir.dt.int32, mybir.dt.bfloat16
    with ExitStack() as ctx:
        m = Memory(nc, ctx, "g1")
        two = lambda n, s, dt=None: [m.sb(f"{n}{u}", s, dt) for u in range(2)]
        ids = two("ids", [128, 3 * J], i32)
        at_edge = two("at_edge", [128, J], i32)
        x = two("x", [128, 2 * J, F])
        rows = two("rows", [4, BE], bf16)
        h, hT = m.sb("h", [128, 2 * J, F]), m.sb("hT", [128, 2, BE])
        slope = two("slope", [128, BE])
        x1f, x1e, er2 = two("x1f", [128, BE]), two("x1e", [128, J, F]), two("er2", [H, BE])
        t, norm = attention_tiles(m), Norm(m, 128, 2 * J)
        p_t = [m.ps("p_t0", [128, BE]), m.ps("p_t1", [128, BE])]
        p_w, p_cut = m.ps("p_w", [128, BE]), m.ps("p_cut", [128, BE])
        p_z, p_ft = ([m.ps(f"{n}{u}", [128, BE]) for u in range(2)] for n in ("p_z", "p_ft"))
        names = ("ids_loaded", "rows_loaded", "xs_loaded", "gathered", "found", "found_stored", "spilled", "stored",
                 "f_stored", "var_ready", "log_ready",
                 "guess_ready", "scale_ready", "h_ready", "hT_ready", "hT_copied", "z_ready", "ft_ready", "cut_ready",
                 "slope_ready", "lead_ready", "relu_ready", "exp_ready", "sums_ready", "ln_ready", "near_ready", "x1_ready",
                 "x1_turned", "x1_copied", "start", "pool_go", "sync_go", "step_n", "step_c", "step_f", "step_s", "step_m")
        (ids_loaded, rows_loaded, xs_loaded, gathered, found, found_stored, spilled, stored, f_stored,
         var_ready, log_ready, guess_ready, scale_ready, h_ready, hT_ready, hT_copied, z_ready, ft_ready, cut_ready,
         slope_ready, lead_ready, relu_ready,
         exp_ready, sums_ready, ln_ready, near_ready, x1_ready, x1_turned, x1_copied, start, pool_go, sync_go, step_n, step_c,
         step_f, step_s, step_m) = (m.slots(n) if n in DMA_SEMS else m.sem(n) for n in names)
        block = ctx.enter_context(nc.Block())

        @block.sync
        def _(eng):
            for u in range(2):
                eng.sem_inc(spilled[u], 16)
                eng.sem_inc(found_stored[u], 16)
                eng.sem_inc(stored[u], 32)
                eng.sem_inc(f_stored[u], 16)

            def load_ids(b, u):
                eng.dma_start(ids[u][:, :], inp["ids"][b, :, :]).then_inc(ids_loaded[u], 16)

            def load_rows(b, u):
                at = bass.ds(b * BE, BE)
                eng.dma_start(rows[u][:, :], tab["rows"][:, at]).then_inc(rows_loaded[u], 16)

            def load_xs(b, u):
                eng.dma_start(x[u][:, 0:J, :].rearrange("p j f -> p (j f)"), tab["xs"][b, :, :]).then_inc(xs_loaded[u], 16)

            def step(b, u, on):
                v = 1 - u
                if on(0):
                    if on(-1):
                        eng.wait_ge(h_ready, b + 2)
                        load_xs(b + 1, v)
                    eng.wait_ge(gathered[u], nth(64, b, u))
                    eng.dma_start(tab["xd"][b, :, :], x[u][:, J:, :].rearrange("p j f -> p (j f)")).then_inc(spilled[u], 16)
                    if on(-1):
                        eng.wait_ge(cut_ready, b + 1)
                        eng.sem_inc(sync_go, 1)
                        load_rows(b + 1, v)
                    eng.wait_ge(found[u], nth(64, b, u))
                    eng.sem_inc(sync_go, 1)
                    eng.dma_start(tab["at"][b, :, :], at_edge[u][:, :]).then_inc(found_stored[u], 16)
                    if on(-1):
                        load_ids(b + 2, u)
                if on(3):
                    eng.wait_ge(x1_ready, b - 1)
                    eng.dma_start(tab["x1f"][b - 3, :, :], x1f[v][:, :]).then_inc(f_stored[v], 16)
                    eng.wait_ge(x1_copied, b - 2)
                    eng.dma_start(edge_rows_of(tab["x1"], b - 3), x1e[v][:, :, :]).then_inc(stored[v], 16)
                    eng.dma_start(tab["er2"][:, bass.ds((b - 3) * BE, BE)], er2[v][:, :]).then_inc(stored[v], 16)

            load_ids(0, 0)
            load_ids(1, 1)
            load_xs(0, 0)
            load_rows(0, 0)
            steps(eng, NB, 3, step, ahead=2)
            for u in range(2):
                eng.wait_ge(spilled[u], 8 * NB + 16)
                eng.wait_ge(found_stored[u], 8 * NB + 16)
                eng.wait_ge(stored[u], 16 * NB + 32)
                eng.wait_ge(f_stored[u], 8 * NB + 16)
            eng.wait_ge(ids_loaded[0], 8 * NB + 16)

        @block.gpsimd
        def _(eng):
            def body(b, u):
                eng.wait_ge(ids_loaded[u], nth(16, b, u))
                eng.wait_ge(h_ready, b + 1)
                eng.wait_ge(spilled[u], nth(16, b, u))
                eng.sem_inc(pool_go, 1)
                for j in range(J):
                    eng.indirect_dma_start(
                        x[u][:, J + j, :], None, inp["x"][:, :],
                        bass.IndirectOffsetOnAxis(ap=ids[u][:, J + j:J + j + 1], axis=0)).then_inc(gathered[u], 16)
                eng.wait_ge(found_stored[u], nth(16, b, u))
                eng.sem_inc(pool_go, 1)
                for j in range(J):
                    eng.indirect_dma_start(
                        at_edge[u][:, j:j + 1], None, tab["pos"][:, :],
                        bass.IndirectOffsetOnAxis(ap=ids[u][:, j:j + 1], axis=0)).then_inc(found[u], 16)

            blocks(eng, NB, body)

        @block.vector
        def _(eng):
            ln, lc = Link(eng, step_n, 4), Link(eng, step_c, 3)
            lf, ls, lm = Link(eng, step_f, LOGIT_LINKS), Link(eng, step_s, SUM_LINKS), Link(eng, step_m, MEAN_LINKS)
            eng.sem_inc(lead_ready, 2)
            eng.sem_inc(sums_ready, 2)
            eng.sem_inc(x1_ready, 1)
            start_attention(eng, t, start)

            def step(b, u, on):
                v = 1 - u

                def moments(k):
                    if on(0):
                        last = moments_part(eng, ln, norm, u, k)
                        if k == 3:
                            last.then_inc(var_ready, 1)
                            ln.end()

                def mean(k):
                    if on(3):
                        last = attention_mean_part(eng, lm, t, v, x1f[v][:, :], k)
                        if k == 2:
                            last.then_inc(x1_ready, 1)
                            lm.end()

                def scales(k):
                    if on(0):
                        last = scales_part(eng, lc, norm, u, k)
                        if k == 3:
                            last.then_inc(scale_ready, 1)
                            lc.end()

                def sums(k):
                    if on(2):
                        last = attention_sums_part(eng, ls, t, p_ft[u], u, k)
                        if k == 2:
                            last.then_inc(sums_ready, 1)
                            ls.end()

                if on(0):
                    ln.begin(b)
                    eng.wait_ge(xs_loaded[u], nth(16, b, u))
                    eng.wait_ge(gathered[u], nth(64, b, u))
                    for g in range(2 * J):
                        last = eng.bn_stats(norm.raw[u][:, g, :], x[u][:, g, :])
                    ln.mark(last)
                if on(3):
                    lm.begin(b - 3)
                    eng.wait_ge(near_ready, b - 2)
                    eng.wait_ge(f_stored[v], nth(16, b - 3, v))
                mean(0)
                moments(0)
                mean(1)
                moments(1)
                moments(2)
                moments(3)
                mean(2)
                if on(0):
                    lc.begin(b)
                    eng.wait_ge(guess_ready, b + 1)
                for k in range(4):
                    scales(k)
                if on(2):
                    ls.begin(b - 2)
                    eng.wait_ge(exp_ready, b - 1)
                    eng.wait_ge(ft_ready, b - 1)
                for k in range(3):
                    sums(k)
                if on(1):
                    lf.begin(b - 1)
                    eng.wait_ge(slope_ready, b)
                    eng.wait_ge(cut_ready, b + 1)
                    attention_logits(eng, lf, p_z[v], slope[v], p_w, p_cut, t, v).then_inc(lead_ready, 1)
                    lf.end()

            steps(eng, NB, 3, step)

        @block.scalar
        def _(eng):
            eng.preload_act_table_set(TABLE)
            eng.sem_inc(h_ready, 2)

            def step(b, u, on):
                v = 1 - u
                if on(2):
                    eng.wait_ge(lead_ready, b + 1)
                    attention_exps(eng, t, u, relu_ready, b - 1).then_inc(exp_ready, 1)
                if on(0):
                    eng.wait_ge(var_ready, b + 1)
                    eng.activation(norm.log[u][:, :], norm.var[u][:, :], ACT.Ln).then_inc(log_ready, 1)
                    eng.wait_ge(log_ready, b + 1)
                    eng.activation(norm.guess[u][:, :], norm.log[u][:, :], ACT.Exp, scale=-0.5).then_inc(guess_ready, 1)
                if on(1):
                    eng.wait_ge(z_ready, b)
                    eng.activation(slope[v][:, :], p_z[v][:, :], ACT.Copy, scale=SLOPE).then_inc(slope_ready, 1)
                if on(0):
                    eng.wait_ge(scale_ready, b + 1)
                    for g in range(2 * J):
                        last = eng.activation(h[:, g, :], x[u][:, g, :], ACT.Relu,
                                              bias=norm.shift[u][:, g:g + 1], scale=norm.scale[u][:, g:g + 1])
                    last.then_inc(h_ready, 1)
                if on(3):
                    eng.wait_ge(x1_turned, b - 2)
                    eng.wait_ge(stored[v], nth(32, b - 3, v))
                    eng.activation(x1e[v][:, :, :].rearrange("p j f -> p (j f)"), p_t[0][:, :], ACT.Copy)
                    eng.activation(er2[v][:, :], p_t[1][0:H, :], ACT.Copy).then_inc(x1_copied, 1)
                if on(2):
                    eng.wait_ge(sums_ready, b + 1)
                    eng.wait_ge(x1_ready, b - 1)
                    attention_inverse(eng, t, u, ln_ready, b - 1).then_inc(near_ready, 1)
                if on(0):
                    eng.wait_ge(hT_ready, b + 1)
                    eng.activation(hT[:, 0, :], p_t[0][:, :], ACT.Copy)
                    eng.activation(hT[:, 1, :], p_t[1][:, :], ACT.Copy).then_inc(hT_copied, 1)

            steps(eng, NB, 3, step)

        @block.tensor
        def _(eng):
            eng.sem_inc(cut_ready, 1)

            def step(b, u, on):
                v = 1 - u
                if on(3):
                    eng.wait_ge(x1_ready, b - 1)
                    for j in range(J):
                        at = slice(j * 128, j * 128 + 128)
                        eng.transpose(p_t[0][:, at], x1f[v][:, at], keep["ident"][:, :])
                    eng.matmul(p_t[1][0:H, :], keep["wer2"][:, :], x1f[v][:, :], start=True, stop=True).then_inc(x1_turned, 1)
                if on(3):
                    eng.wait_ge(x1_copied, b - 2)
                if on(0):
                    eng.wait_ge(h_ready, b + 3)
                    for g in range(2 * J):
                        at = slice(g % J * 128, g % J * 128 + 128)
                        last = eng.transpose(p_t[g // J][:, at], h[:, g, :], keep["ident"][:, :])
                    last.then_inc(hT_ready, 1)
                    eng.wait_ge(lead_ready, b + 1)
                    eng.wait_ge(hT_copied, b + 1)
                    eng.matmul(p_z[u][:, :], keep["wel1"][:, :], hT[:, 0, :], start=True, stop=False)
                    eng.matmul(p_z[u][:, :], keep["wer1"][:, :], hT[:, 1, :], start=False, stop=True).then_inc(z_ready, 1)
                    eng.wait_ge(sums_ready, b + 1)
                    eng.matmul(p_ft[u][:, :], keep["w1"][:, :], hT[:, 0, :], start=True, stop=True).then_inc(ft_ready, 1)
                    eng.wait_ge(lead_ready, b + 2)
                    eng.wait_ge(rows_loaded[u], nth(16, b, u))
                    eng.matmul(p_w[:, :], keep["rowpick"][:, 0, :], rows[u][:, :], start=True, stop=True)
                    eng.matmul(p_cut[:, :], keep["rowpick"][:, 1, :], rows[u][:, :], start=True, stop=True).then_inc(cut_ready, 1)

            steps(eng, NB, 3, step)


def gat2_phase(nc, keep, inp, tab):
    from contextlib import ExitStack
    import concourse.bass as bass
    from concourse import mybir

    ACT, i32, bf16 = mybir.ActivationFunctionType, mybir.dt.int32, mybir.dt.bfloat16
    with ExitStack() as ctx:
        m = Memory(nc, ctx, "g2")
        two = lambda n, s, dt=None: [m.sb(f"{n}{u}", s, dt) for u in range(2)]
        at_edge = two("at_edge", [128, J], i32)
        x, x1f, x2f = two("x", [128, J, F]), two("x1f", [128, BE]), two("x2f", [128, BE])
        rows, er2 = two("rows", [4, BE], bf16), two("er2", [H, BE])
        hT, slope = m.sb("hT", [128, BE]), two("slope", [128, BE])
        delta = two("delta", [128, J, F])
        t = attention_tiles(m)
        p_hT, p_w, p_cut, p_delta = (m.ps(n, [128, BE]) for n in ("p_hT", "p_w", "p_cut", "p_delta"))
        p_z, p_ft = ([m.ps(f"{n}{u}", [128, BE]) for u in range(2)] for n in ("p_z", "p_ft"))
        names = ("at_loaded", "rows_loaded", "x1f_loaded", "gathered", "stored", "hT_ready",
                 "hT_copied", "z_ready", "cut_ready", "ft_ready", "slope_ready", "lead_ready", "relu_ready",
                 "exp_ready", "sums_ready", "log_ready", "near_ready", "x2_ready", "delta_ready", "delta_copied",
                 "start", "pool_go", "sync_go", "step_f", "step_s", "step_m")
        (at_loaded, rows_loaded, x1f_loaded, gathered, stored, hT_ready, hT_copied, z_ready,
         cut_ready, ft_ready, slope_ready, lead_ready, relu_ready, exp_ready, sums_ready, log_ready, near_ready,
         x2_ready, delta_ready, delta_copied, start, pool_go, sync_go, step_f, step_s, step_m) = (
            m.slots(n) if n in DMA_SEMS else m.sem(n) for n in names)
        block = ctx.enter_context(nc.Block())

        @block.sync
        def _(eng):
            for u in range(2):
                eng.sem_inc(stored[u], 16)

            def load_at(b, u):
                eng.dma_start(at_edge[u][:, :], tab["at"][b, :, :]).then_inc(at_loaded[u], 16)

            def load_rows(b, u):
                at = bass.ds(b * BE, BE)
                eng.dma_start(rows[u][:, :], tab["rows"][:, at]).then_inc(rows_loaded[u], 16)
                eng.dma_start(er2[u][:, :], tab["er2"][:, at]).then_inc(rows_loaded[u], 16)

            def step(b, u, on):
                v = 1 - u
                if on(0) and on(-1):
                    eng.wait_ge(gathered[u], nth(64, b, u))
                    load_at(b + 2, u)
                    eng.wait_ge(cut_ready, b + 1)
                    eng.sem_inc(sync_go, 1)
                    load_rows(b + 1, v)
                if on(3):
                    eng.wait_ge(delta_ready, b - 2)
                    eng.dma_start(x1f[v][:, :], tab["x1f"][b - 3, :, :]).then_inc(x1f_loaded[v], 16)
                if on(4):
                    eng.wait_ge(delta_copied, b - 2)
                    eng.dma_start(edge_rows_of(tab["delta"], b - 4), delta[u][:, :, :]).then_inc(stored[u], 16)

            load_at(0, 0)
            load_at(1, 1)
            load_rows(0, 0)
            steps(eng, NB, 4, step, ahead=2)
            for u in range(2):
                eng.wait_ge(stored[u], 8 * NB + 16)
            eng.wait_ge(at_loaded[0], 8 * NB + 16)

        @block.gpsimd
        def _(eng):
            def body(b, u):
                eng.wait_ge(at_loaded[u], nth(16, b, u))
                eng.wait_ge(hT_ready, b + 1)
                eng.sem_inc(pool_go, 1)
                for j in range(J):
                    eng.indirect_dma_start(
                        x[u][:, j, :], None, tab["x1"][:, :],
                        bass.IndirectOffsetOnAxis(ap=at_edge[u][:, j:j + 1], axis=0)).then_inc(gathered[u], 16)

            blocks(eng, NB, body)

        @block.vector
        def _(eng):
            lf, ls, lm = Link(eng, step_f, LOGIT_LINKS), Link(eng, step_s, SUM_LINKS), Link(eng, step_m, MEAN_LINKS)
            eng.sem_inc(lead_ready, 2)
            eng.sem_inc(sums_ready, 2)
            eng.sem_inc(x2_ready, 1)
            start_attention(eng, t, start)

            def step(b, u, on):
                v = 1 - u
                if on(3):
                    lm.begin(b - 3)
                    eng.wait_ge(near_ready, b - 2)
                    for k in range(2):
                        attention_mean_part(eng, lm, t, v, x2f[v][:, :], k)
                    attention_mean_part(eng, lm, t, v, x2f[v][:, :], 2).then_inc(x2_ready, 1)
                    lm.end()
                if on(2):
                    ls.begin(b - 2)
                    eng.wait_ge(exp_ready, b - 1)
                    eng.wait_ge(ft_ready, b - 1)
                    for k in range(2):
                        attention_sums_part(eng, ls, t, p_ft[u], u, k)
                    attention_sums_part(eng, ls, t, p_ft[u], u, 2).then_inc(sums_ready, 1)
                    ls.end()
                if on(1):
                    lf.begin(b - 1)
                    eng.wait_ge(slope_ready, b)
                    eng.wait_ge(cut_ready, b + 1)
                    attention_logits(eng, lf, p_z[v], slope[v], p_w, p_cut, t, v).then_inc(lead_ready, 1)
                    lf.end()

            steps(eng, NB, 3, step)

        @block.scalar
        def _(eng):
            eng.preload_act_table_set(TABLE)
            eng.sem_inc(delta_copied, 1)

            def step(b, u, on):
                v = 1 - u
                if on(2):
                    eng.wait_ge(lead_ready, b + 1)
                    attention_exps(eng, t, u, relu_ready, b - 1).then_inc(exp_ready, 1)
                if on(1):
                    eng.wait_ge(z_ready, b)
                    eng.activation(slope[v][:, :], p_z[v][:, :], ACT.Copy, scale=SLOPE).then_inc(slope_ready, 1)
                if on(0):
                    eng.wait_ge(hT_ready, b + 3)
                    eng.activation(hT[:, :], p_hT[:, :], ACT.Copy).then_inc(hT_copied, 1)
                if on(4):
                    eng.wait_ge(delta_ready, b - 1)
                    eng.wait_ge(stored[u], nth(16, b - 4, u))
                    eng.activation(delta[u][:, :, :].rearrange("p j f -> p (j f)"), p_delta[:, :],
                                   ACT.Copy).then_inc(delta_copied, 1)
                if on(2):
                    eng.wait_ge(sums_ready, b + 1)
                    eng.wait_ge(x2_ready, b - 1)
                    attention_inverse(eng, t, u, log_ready, b - 1).then_inc(near_ready, 1)

            steps(eng, NB, 4, step)

        @block.tensor
        def _(eng):
            eng.sem_inc(hT_ready, 2)
            eng.sem_inc(delta_ready, 2)
            eng.sem_inc(cut_ready, 1)

            def step(b, u, on):
                v = 1 - u
                if on(0):
                    eng.wait_ge(gathered[u], nth(64, b, u))
                    for j in range(J):
                        last = eng.transpose(p_hT[:, j * 128:(j + 1) * 128], x[u][:, j, :], keep["ident"][:, :])
                    last.then_inc(hT_ready, 1)
                if on(4):
                    eng.wait_ge(x1f_loaded[u], nth(16, b - 4, u))
                    eng.wait_ge(x2_ready, b - 2)
                    eng.wait_ge(delta_copied, b - 3)
                    eng.matmul(p_delta[:, :], keep["ones3"][:, :], keep["bm3"][:, :, :], start=True, stop=False)
                    for j in range(J):
                        at = slice(j * 128, j * 128 + 128)
                        eng.matmul(p_delta[:, at], x1f[u][:, at], keep["wm"][:, 0, :], start=False, stop=False)
                        last = eng.matmul(p_delta[:, at], x2f[u][:, at], keep["wm"][:, 1, :], start=False, stop=j == J - 1)
                    last.then_inc(delta_ready, 1)
                if on(0):
                    eng.wait_ge(lead_ready, b + 1)
                    eng.wait_ge(rows_loaded[u], nth(32, b, u))
                    eng.matmul(p_z[u][:, :], keep["expand"][:, :], er2[u][:, :], start=True, stop=False)
                    eng.wait_ge(hT_copied, b + 1)
                    eng.matmul(p_z[u][:, :], keep["wel2"][:, :], hT[:, :], start=False, stop=True).then_inc(z_ready, 1)
                    eng.wait_ge(sums_ready, b + 1)
                    eng.matmul(p_ft[u][:, :], keep["w2"][:, :], hT[:, :], start=True, stop=True).then_inc(ft_ready, 1)
                    eng.wait_ge(lead_ready, b + 2)
                    eng.matmul(p_w[:, :], keep["rowpick"][:, 0, :], rows[u][:, :], start=True, stop=True)
                    eng.matmul(p_cut[:, :], keep["rowpick"][:, 1, :], rows[u][:, :], start=True, stop=True).then_inc(cut_ready, 1)

            steps(eng, NB, 4, step)


def rgcn_phase(nc, keep, inp, tab, out):
    from contextlib import ExitStack
    import concourse.bass as bass
    from concourse import mybir
    from concourse.alu_op_type import AluOpType as ALU

    ACT, i32, bf16 = mybir.ActivationFunctionType, mybir.dt.int32, mybir.dt.bfloat16
    with ExitStack() as ctx:
        m = Memory(nc, ctx, "rg")
        two = lambda n, s, dt=None: [m.sb(f"{n}{u}", s, dt) for u in range(2)]
        at_edge, ends = two("at_edge", [128, J], i32), two("ends", [128, J], i32)
        x, own, far = two("x", [128, 2 * J, F]), two("own", [128, J, F]), two("far", [128, J, F])
        y = two("y", [128, 2 * J, F])
        y_own = two("y_own", [128, J, F])
        hot = two("hot", [R + 1, BE], bf16)
        h, hT = m.sb("h", [128, 2 * J, F]), two("hT", [128, 2, BE])
        of_rel = m.sb("of_rel", [128, R, BE])
        message, agg = m.sb("message", [128, BE]), two("agg", [128, BE])
        low, res = m.sb("low", [128, J, F]), two("res", [128, J, F])
        norm = Norm(m, 128, 2 * J)
        p_hT = m.ps("p_hT", [128, BE])
        p_mask = [m.ps(f"p_mask{k}", [128, BE]) for k in range(3)]
        p_msg = [m.ps(f"p_msg{u}", [128, BE]) for u in range(2)]
        p_same, p_o = m.ps("p_same", [128, BE]), m.ps("p_o", [128, J, F])
        names = ("at_loaded", "ends_loaded", "x_loaded", "rows_loaded", "gathered", "scattered", "y_ready",
                 "var_ready", "log_ready", "guess_ready", "scale_ready", "h_ready", "hT_ready", "hT_copied",
                 "hd_ready", "hd_copied",
                 "mask_ready", "of_rel_ready", "msg_ready", "same_ready", "msg_copied", "agg_ready", "o_ready", "res_ready",
                 "rows_left", "y_kept", "sync_go", "pool_go", "start", "step_n", "step_s", "step_o")
        (at_loaded, ends_loaded, x_loaded, rows_loaded, gathered, scattered, y_ready, var_ready, log_ready,
         guess_ready, scale_ready, h_ready, hT_ready, hT_copied, hd_ready, hd_copied,
         mask_ready, of_rel_ready, msg_ready, same_ready,
         msg_copied, agg_ready, o_ready, res_ready, rows_left, y_kept, sync_go, pool_go, start,
         step_n, step_s, step_o) = (m.slots(n) if n in DMA_SEMS else m.sem(n) for n in names)
        MASK_SLOT = (0, 1, 2, 0, 1, 0, 1, 2)
        MASKS_AFTER = ((3,), (4,), (), (5,), (6, 7), (0,), (1,), (2,))
        block = ctx.enter_context(nc.Block())

        @block.sync
        def _(eng):
            def load_at(b, u):
                eng.dma_start(at_edge[u][:, :], tab["at"][b, :, :]).then_inc(at_loaded[u], 16)

            def load_x(b, u):
                eng.dma_start(x[u][:, 0:J, :].rearrange("p j f -> p (j f)"), tab["xs"][b, :, :]).then_inc(x_loaded[u], 16)
                eng.dma_start(x[u][:, J:, :].rearrange("p j f -> p (j f)"), tab["xd"][b, :, :]).then_inc(x_loaded[u], 16)
                eng.dma_start(own[u][:, :, :], edge_rows_of(tab["delta"], b)).then_inc(x_loaded[u], 16)

            def step(b, u, on):
                v = 1 - u
                if on(-1) and on(0):
                    eng.wait_ge(y_ready, b + 1)
                    load_x(b + 1, v)
                    eng.wait_ge(gathered[u], nth(64, b, u))
                    load_at(b + 2, u)
                if on(1):
                    eng.wait_ge(msg_ready, b)
                    eng.sem_inc(sync_go, 1)
                    eng.dma_start(hot[v][:, :], tab["hot"][:, bass.ds((b - 1) * BE, BE)]).then_inc(rows_loaded[v], 16)
                if on(2):
                    eng.wait_ge(rows_left, b - 1)
                    eng.sem_inc(sync_go, 1)
                    eng.dma_start(ends[u][:, :], tab["end"][b - 2, :, :]).then_inc(ends_loaded[u], 16)
                if on(1):
                    eng.wait_ge(y_ready, b + 1)
                    eng.wait_ge(res_ready, b)
                    eng.dma_start(y_own[v][:, :, :], y[v][:, J:, :]).then_inc(y_kept[v], 16)

            load_at(0, 0)
            load_at(1, 1)
            load_x(0, 0)
            steps(eng, NB, 2, step, ahead=2)
            eng.wait_ge(at_loaded[0], 8 * NB + 16)

        @block.gpsimd
        def _(eng):
            eng.sem_inc(rows_left, 2)

            def gather(b, u):
                eng.wait_ge(at_loaded[u], nth(16, b, u))
                if not (isinstance(b, int) and b == 0):
                    eng.wait_ge(y_ready, b)
                eng.sem_inc(pool_go, 1)
                for j in range(J):
                    eng.indirect_dma_start(
                        far[u][:, j, :], None, tab["delta"][:, :],
                        bass.IndirectOffsetOnAxis(ap=at_edge[u][:, j:j + 1], axis=0)).then_inc(gathered[u], 16)

            def step(b, u, on):
                v = 1 - u
                if on(-1) and on(0):
                    gather(b + 1, v)
                if on(3):
                    eng.wait_ge(ends_loaded[v], nth(16, b - 3, v))
                    eng.wait_ge(res_ready, b)
                    eng.sem_inc(pool_go, 1)
                    for j in range(J):
                        eng.indirect_dma_start(
                            out[:, :], bass.IndirectOffsetOnAxis(ap=ends[v][:, j:j + 1], axis=0),
                            res[v][:, j, :], None, bounds_check=N - 1, oob_is_err=False).then_inc(scattered[v], 16)
                    eng.wait_ge(scattered[v], nth(64, b - 3, v))
                    eng.sem_inc(rows_left, 1)

            eng.wait_ge(start, 1)
            gather(0, 0)
            steps(eng, NB, 3, step, ahead=2)

        @block.vector
        def _(eng):
            ln, ls, lo = Link(eng, step_n, 4), Link(eng, step_s, 4), Link(eng, step_o, 2)
            eng.sem_inc(y_ready, 1)
            eng.sem_inc(res_ready, 2)
            eng.memset(agg[1][:, BE - 1:BE], 0.0).then_inc(start, 1)
            eng.wait_ge(start, 1)

            def step(b, u, on):
                v = 1 - u

                def relation(r):
                    if on(2):
                        if r == 0:
                            eng.wait_ge(hT_copied, b - 1)
                        eng.wait_ge(mask_ready, (b - 2) * R + (r + 1))
                        eng.tensor_tensor(of_rel[:, r, :], p_mask[MASK_SLOT[r]][:, :], hT[u][:, 0, :],
                                          ALU.mult).then_inc(of_rel_ready, 1)

                def sums():
                    if on(3):
                        eng.wait_ge(msg_copied, b - 2)
                        eng.wait_ge(same_ready, b - 2)
                        eng.tensor_tensor_scan(agg[v][:, :], p_same[:, :], message[:, :], agg[u][:, BE - 1:BE],
                                               ALU.mult, ALU.add).then_inc(agg_ready, 1)

                def scales(k):
                    if on(1):
                        if k == 0:
                            ls.begin(b - 1)
                            eng.wait_ge(guess_ready, b)
                        last = scales_part(eng, ls, norm, v, k, keep["norm"][:, bass.ds((b - 1) * J, J)])
                        if k == 4:
                            last.then_inc(scale_ready, 1)
                            ls.end()

                def y_rows(k):
                    if on(0) and k == 0:
                        if on(2):
                            eng.wait_ge(y_kept[u], nth(16, b - 2, u))
                        eng.wait_ge(x_loaded[u], nth(48, b, u))
                        eng.wait_ge(gathered[u], nth(64, b, u))
                        eng.tensor_tensor(y[u][:, J:, :], x[u][:, J:, :], own[u][:, :, :], ALU.add)
                    if on(0) and k == 1:
                        eng.tensor_tensor(y[u][:, 0:J, :], x[u][:, 0:J, :], far[u][:, :, :], ALU.add).then_inc(y_ready, 1)

                def stats(groups):
                    if on(0):
                        if groups[0] == 0:
                            ln.begin(b)
                            eng.wait_ge(y_ready, b + 2)
                        for g in groups:
                            last = eng.bn_stats(norm.raw[u][:, g, :], y[u][:, g, :])
                        if g == 2 * J - 1:
                            ln.mark(last)

                def moments(k):
                    if on(0):
                        last = moments_part(eng, ln, norm, u, k)
                        if k == 3:
                            last.then_inc(var_ready, 1)
                            ln.end()

                def out_rows(k):
                    if on(3) and k == 0:
                        lo.begin(b - 3)
                        eng.wait_ge(o_ready, b - 2)
                        lo.mark(eng.scalar_tensor_tensor(low[:, :, :], p_o[:, :, :], 0.0, keep["alpha4"][:, :, :],
                                                           ALU.min, ALU.mult))
                    if on(3) and k == 1:
                        lo.wait()
                        lo.mark(eng.scalar_tensor_tensor(low[:, :, :], p_o[:, :, :], 0.0, low[:, :, :],
                                                           ALU.max, ALU.add))
                    if on(3) and k == 2:
                        eng.wait_ge(y_kept[v], nth(16, b - 3, v))
                        eng.wait_ge(rows_left, b - 2)
                        lo.wait()
                        eng.tensor_tensor(res[v][:, :, :], low[:, :, :], y_own[v][:, :, :], ALU.add).then_inc(res_ready, 1)
                        lo.end()

                relation(0)
                scales(0)
                relation(1)
                scales(1)
                sums()
                scales(2)
                y_rows(0)
                scales(3)
                relation(2)
                scales(4)
                y_rows(1)
                relation(3)
                stats(range(0, 2))
                relation(4)
                stats(range(2, 5))
                relation(5)
                stats(range(5, 2 * J))
                out_rows(0)
                moments(0)
                relation(6)
                moments(1)
                out_rows(1)
                moments(2)
                relation(7)
                moments(3)
                out_rows(2)

            steps(eng, NB, 3, step)

        @block.scalar
        def _(eng):
            eng.preload_act_table_set(TABLE)

            def step(b, u, on):
                v = 1 - u
                if on(1):
                    eng.wait_ge(scale_ready, b)
                    for g in range(2 * J):
                        last = eng.activation(h[:, g, :], y[v][:, g, :], ACT.Relu,
                                              bias=norm.shift[v][:, g:g + 1], scale=norm.scale[v][:, g:g + 1])
                    last.then_inc(h_ready, 1)
                    eng.wait_ge(hT_ready, b)
                    eng.activation(hT[v][:, 0, :], p_hT[:, :], ACT.Copy).then_inc(hT_copied, 1)
                    eng.wait_ge(hd_ready, b)
                    eng.activation(hT[v][:, 1, :], p_hT[:, :], ACT.Copy).then_inc(hd_copied, 1)
                if on(0):
                    eng.wait_ge(var_ready, b + 1)
                    eng.activation(norm.log[u][:, :], norm.var[u][:, :], ACT.Ln).then_inc(log_ready, 1)
                    eng.wait_ge(log_ready, b + 1)
                    eng.activation(norm.guess[u][:, :], norm.log[u][:, :], ACT.Exp, scale=-0.5).then_inc(guess_ready, 1)
                if on(2):
                    eng.wait_ge(msg_ready, b + 1)
                    eng.activation(message[:, :], p_msg[u][:, :], ACT.Copy).then_inc(msg_copied, 1)

            steps(eng, NB, 2, step)

        @block.tensor
        def _(eng):
            eng.sem_inc(msg_ready, 2)

            def step(b, u, on):
                v = 1 - u

                def mask(r, slot):
                    eng.matmul(p_mask[MASK_SLOT[r]][:, :], keep["pick"][:, r, :], hot[slot][:, :],
                               start=True, stop=True).then_inc(mask_ready, 1)

                def turn(first):
                    for j in range(J):
                        last = eng.transpose(p_hT[:, j * 128:j * 128 + 128], h[:, first + j, :], keep["ident"][:, :])
                    return last

                def between(r):
                    if on(3) and 1 <= r < 1 + J:
                        if r == 1:
                            eng.wait_ge(agg_ready, b - 2)
                            eng.matmul(p_o[:, :, :], keep["ones3"][:, :], keep["bias3"][:, :, :], start=True, stop=False)
                        j = r - 1
                        at = slice(j * 128, j * 128 + 128)
                        eng.matmul(p_o[:, j, :], hT[v][:, 1, at], keep["root"][:, :], start=False, stop=False)
                        last = eng.matmul(p_o[:, j, :], agg[v][:, at], keep["ident"][:, :], start=False, stop=j == J - 1)
                        if j == J - 1:
                            last.then_inc(o_ready, 1)
                    if on(1) and r == 5:
                        eng.wait_ge(h_ready, b)
                        if on(2):
                            eng.wait_ge(hd_copied, b - 1)
                        turn(0).then_inc(hT_ready, 1)
                    if on(2) and r == 5:
                        eng.matmul(p_same[:, :], keep["pick"][:, R, :], hot[u][:, :], start=True, stop=True).then_inc(same_ready, 1)
                    if on(1) and r == 6:
                        eng.wait_ge(hT_copied, b)
                        turn(J).then_inc(hd_ready, 1)

                if on(1) and not on(2):
                    eng.wait_ge(rows_loaded[v], nth(16, b - 1, v))
                    for r in range(3):
                        mask(r, v)
                for r in range(R):
                    if on(2):
                        eng.wait_ge(of_rel_ready, (b - 2) * R + (r + 1))
                        for k in MASKS_AFTER[r]:
                            if k > r:
                                mask(k, u)
                            elif on(1):
                                if k == 0:
                                    eng.wait_ge(rows_loaded[v], nth(16, b - 1, v))
                                mask(k, v)
                    between(r)
                    if on(2):
                        last = eng.matmul(p_msg[u][:, :], keep["wrel"][:, r, :], of_rel[:, r, :],
                                          start=(r == 0), stop=(r == R - 1))
                if on(2):
                    last.then_inc(msg_ready, 1)
            steps(eng, NB, 3, step)


def program(nc, inp, out):
    from contextlib import ExitStack
    from concourse import mybir

    fp32, i32, bf16 = mybir.dt.float32, mybir.dt.int32, mybir.dt.bfloat16
    shapes = {"xs": ((NB, 128, BE), fp32), "xd": ((NB, 128, BE), fp32), "x1f": ((NB, 128, BE), fp32),
              "x1": ((EP + 1, F), fp32), "delta": ((EP + 1, F), fp32), "er2": ((H, EP), fp32),
              "rows": ((4, EP), bf16), "hot": ((R + 1, EP), bf16), "pos": ((N, 1), i32), "parts": ((2, 3, F), bf16),
              "end": ((NB + 1, 128, J), i32), "at": ((NB + 1, 128, J), i32)}
    tab = {k: nc.dram_tensor(f"tab_{k}", s, dt).ap() for k, (s, dt) in shapes.items()}
    Memory.used.clear()
    with ExitStack() as ctx:
        m = Memory(nc, ctx, "keep")
        keep = {"ident": m.sb("ident", [128, 128]), "expand": m.sb("expand", [H, 128]),
                "pick": m.sb("pick", [R + 1, R + 1, 128], bf16), "rowpick": m.sb("rowpick", [4, 2, 128], bf16),
                "ones": m.sb("ones", [1, 128]),
                "w1": m.sb("w1", [128, 128]), "w2": m.sb("w2", [128, 128]), "wm": m.sb("wm", [128, 2, 128]),
                "root": m.sb("root", [128, 128]), "wrel": m.sb("wrel", [128, R, 128]),
                "wel1": m.sb("wel1", [128, 128]), "wer1": m.sb("wer1", [128, 128]),
                "wel2": m.sb("wel2", [128, 128]), "wer2": m.sb("wer2", [128, H]),
                "bmrow": m.sb("bmrow", [1, F]), "biasrow": m.sb("biasrow", [1, F]),
                "alpha4": m.sb("alpha4", [128, J, F]),
                "norm": m.sb("norm", [128, TILES]), "ones3": m.sb("ones3", [3, 128], bf16),
                "bm3": m.sb("bm3", [3, J, F], bf16), "bias3": m.sb("bias3", [3, J, F], bf16)}
        weights_phase(nc, keep, inp, tab)
        edge_rows_phase(nc, keep, inp, tab)
        counts_phases(nc, keep, inp, tab)
        clear_semaphores(nc)
        nodes_phase(nc, keep, inp, tab, out)
        clear_semaphores(nc)
        gat1_phase(nc, keep, inp, tab)
        spread_phases(nc, keep, inp, tab)
        gat2_phase(nc, keep, inp, tab)
        rgcn_phase(nc, keep, inp, tab, out)


def kernel(**inputs):
    import concourse.bacc as _bacc
    from concourse import mybir as _mybir
    from concourse.bass_utils import run_bass_kernel_spmd as _run
    import ml_dtypes

    src, dst, kind, w = (np.asarray(inputs[k]) for k in ("src", "dst", "edge_type_8", "edge_weight"))

    def padded(a, value, extra=0):
        return np.concatenate([a, np.full(EP + extra - E, value, a.dtype)])

    def edge_rows(a):
        return np.ascontiguousarray(a.reshape(-1, 128).T)

    def by_block(a):
        return a.reshape(NB + 1, J, 128).transpose(0, 2, 1)

    numbers = padded(np.arange(E, dtype=np.int32), 0, BE)
    ids = np.concatenate([by_block(padded(src, 0, BE)), by_block(padded(dst, 0, BE)), by_block(numbers)], axis=2)
    segments = padded(dst, N)
    row = np.arange(128)
    heads = (row[:, None] // D == np.arange(H)[None, :])
    arrays = {
        "x": np.asarray(inputs["x"]), "ids": np.ascontiguousarray(ids), "w": padded(w, 0), "kind": padded(kind, 0),
        "dseg": np.concatenate([np.full(1, -1, dst.dtype), segments, np.full(1, -1, dst.dtype)]),
        "here": edge_rows(segments), "next": edge_rows(np.concatenate([segments[1:], np.full(1, -1, dst.dtype)])),
        "ident": np.eye(128, dtype=np.float32), "ones": np.ones((1, 128), np.float32),
        "blockmask": (row[:, None] // D == row[None, :] // D).astype(np.float32),
        "headsel": heads.astype(np.float32), "expand": np.ascontiguousarray(heads.T.astype(np.float32)),
        "pick": np.ascontiguousarray(np.broadcast_to(
            np.eye(R + 1)[:, :, None], (R + 1, R + 1, 128)).astype(ml_dtypes.bfloat16)),
        "rowpick": np.ascontiguousarray(np.broadcast_to(
            np.array([[1, 0], [1, 0], [1, 0], [0, 1]])[:, :, None], (4, 2, 128)).astype(ml_dtypes.bfloat16)),
        "ones3": np.ones((3, 128), ml_dtypes.bfloat16),
        "relcol": (np.arange(R * C) // C).astype(np.float32)[:, None],
        "chunksel": (np.arange(R * C)[:, None] % C == np.arange(C)[None, :]).astype(np.float32),
        "W1": np.asarray(inputs["L0_gnn_W1"]), "W2": np.asarray(inputs["L0_gnn_W2"]),
        "al1": np.asarray(inputs["L0_gnn_al1"]), "ar1": np.asarray(inputs["L0_gnn_ar1"]),
        "al2": np.asarray(inputs["L0_gnn_al2"]), "ar2": np.asarray(inputs["L0_gnn_ar2"]),
        "Wm": np.asarray(inputs["L0_gnn_Wm"]), "bm": np.asarray(inputs["L0_gnn_bm"]),
        "basis": np.asarray(inputs["L1_gnn_basis"]), "comp": np.asarray(inputs["L1_gnn_comp"]),
        "root": np.asarray(inputs["L1_gnn_root"]), "bias": np.asarray(inputs["L1_gnn_bias"]),
        "alpha": np.asarray(inputs["L1_gnn_alpha"]),
    }
    nc = _bacc.Bacc("TRN2", target_bir_lowering=False, num_devices=1)
    inp = {k: nc.dram_tensor(f"in_{k}", a.shape, _mybir.dt.from_np(a.dtype), kind="ExternalInput").ap()
           for k, a in arrays.items()}
    out = nc.dram_tensor("out_0", (N, F), _mybir.dt.float32, kind="ExternalOutput").ap()
    program(nc, inp, out)
    r = _run(nc, [{f"in_{k}": a for k, a in arrays.items()}], core_ids=[0])
    return r.results[0]["out_0"]
```
